# Optimizing a Trainium2 kernel written in Bass

```python
import numpy as np
import jax
import jax.numpy as jnp

def _softmax(x, axis=-1):
    return jax.nn.softmax(x, axis=axis)

def _gelu(x):
    return jax.nn.gelu(x, approximate=True)

def _silu(x):
    return jax.nn.silu(x)

def _sigmoid(x):
    return jax.nn.sigmoid(x)

def _layernorm(x, axis=-1, eps=1e-05):
    m = jnp.mean(x, axis=axis, keepdims=True)
    v = jnp.var(x, axis=axis, keepdims=True)
    return (x - m) / jnp.sqrt(v + eps)

def _scatter_add(tgt, idx, src, axis=0):
    return tgt.at[idx].add(src)

def _segment_sum(src, seg, n):
    return jax.ops.segment_sum(src, seg, n)
kernel_name = 'mk_gnn_preln_d4_gnn_r8_19ce9c'

def setup_inputs(seed: int=0):
    np.random.seed(seed)
    _w = jnp.asarray

    def _rec_inputs():
        import jax
        import jax.numpy as jnp
        _gk = jax.random.key(seed)
        x = -0.0005121 + 1.001 * jax.random.normal(jax.random.fold_in(_gk, 1), (12500, 64), jnp.float32)
        src = jax.random.randint(jax.random.fold_in(_gk, 2), (200000,), 0, 12500, jnp.int32)
        dst = jax.random.randint(jax.random.fold_in(_gk, 3), (200000,), 0, 12500, jnp.int32)
        _o = jnp.argsort(dst, stable=True)
        src = src[_o]
        dst = dst[_o]
        edge_attr_32 = 0.000196303 + 1.00016 * jax.random.normal(jax.random.fold_in(_gk, 12), (200000, 32), jnp.float32)
        edge_attr_64 = -9.77346e-05 + 0.999888 * jax.random.normal(jax.random.fold_in(_gk, 13), (200000, 64), jnp.float32)
        edge_attr_8 = 0.000254156 + 0.999948 * jax.random.normal(jax.random.fold_in(_gk, 14), (200000, 8), jnp.float32)
        return (x, src, dst, edge_attr_32, edge_attr_64, edge_attr_8)
    x, src, dst, edge_attr_32, edge_attr_64, edge_attr_8 = _rec_inputs()

    def _L0_gnn_setup():
        import jax, jax.numpy as jnp
        import numpy as np
        N = 6250
        E = 100000
        D = 64
        H = 64
        DE = 32

        def _transformer_conv(x, src, dst, edge_attr, wq, bq, wk, bk, wv, bv, we, ws, bs, n_nodes):
            q = x @ wq + bq
            k = x @ wk + bk
            v = x @ wv + bv
            e = edge_attr @ we
            ke = k[src] + e
            score = jnp.sum(q[dst] * ke, axis=-1) / jnp.sqrt(jnp.asarray(ke.shape[-1], x.dtype))
            smax = jax.ops.segment_max(score, dst, num_segments=n_nodes)
            a = jnp.exp(score - smax[dst])
            denom = jax.ops.segment_sum(a, dst, num_segments=n_nodes)
            alpha = a / denom[dst]
            msg = alpha[:, None] * (v[src] + e)
            out = jax.ops.segment_sum(msg, dst, num_segments=n_nodes)
            out = out + x @ ws + bs
            return out
        key = jax.random.key(seed)
        ks = jax.random.split(key, 24)

        def g(i, shape, scale):
            return jax.random.normal(ks[i], shape, dtype=jnp.float32) * scale
        inp = {'x': g(0, (N, D), 1.0), 'edge_index': jax.random.randint(ks[1], (2, E), 0, N, dtype=jnp.int64), 'edge_attr': g(2, (E, DE), 1.0), 'q1_w': g(3, (D, H), D ** (-0.5)), 'q1_b': jnp.zeros((H,), jnp.float32), 'k1_w': g(4, (D, H), D ** (-0.5)), 'k1_b': jnp.zeros((H,), jnp.float32), 'v1_w': g(5, (D, H), D ** (-0.5)), 'v1_b': jnp.zeros((H,), jnp.float32), 'e1_w': g(6, (DE, H), DE ** (-0.5)), 's1_w': g(7, (D, H), D ** (-0.5)), 's1_b': jnp.zeros((H,), jnp.float32), 'q2_w': g(8, (H, H), H ** (-0.5)), 'q2_b': jnp.zeros((H,), jnp.float32), 'k2_w': g(9, (H, H), H ** (-0.5)), 'k2_b': jnp.zeros((H,), jnp.float32), 'v2_w': g(10, (H, H), H ** (-0.5)), 'v2_b': jnp.zeros((H,), jnp.float32), 'e2_w': g(11, (DE, H), DE ** (-0.5)), 's2_w': g(12, (H, H), H ** (-0.5)), 's2_b': jnp.zeros((H,), jnp.float32), 'skip_w': g(13, (2 * H, D), (2 * H) ** (-0.5)), 'skip_b': jnp.zeros((D,), jnp.float32)}
        return inp
    _L0_gnn_all = _L0_gnn_setup()
    _L0_gnn_in = {k: v for k, v in _L0_gnn_all.items() if k in ('q1_w', 'q1_b', 'k1_w', 'k1_b', 'v1_w', 'v1_b', 'e1_w', 's1_w', 's1_b', 'q2_w', 'q2_b', 'k2_w', 'k2_b', 'v2_w', 'v2_b', 'e2_w', 's2_w', 's2_b', 'skip_w', 'skip_b')}
    del _L0_gnn_all

    def _L1_gnn_setup():
        import jax, jax.numpy as jnp
        import numpy as np
        N_NODES = 12500
        N_EDGES = 200000
        IN_CH, OUT_CH, HEADS, EDGE_DIM = (64, 16, 4, 8)
        NEG_SLOPE = 0.2
        key = jax.random.key(seed)
        ks = jax.random.split(key, 9)
        x = jax.random.normal(ks[0], (N_NODES, IN_CH), dtype=jnp.float32)
        edge_index = jax.random.randint(ks[1], (2, N_EDGES), 0, N_NODES, dtype=jnp.int64)
        edge_attr = jax.random.normal(ks[2], (N_EDGES, EDGE_DIM), dtype=jnp.float32)
        W = jax.random.normal(ks[3], (HEADS, IN_CH, OUT_CH), dtype=jnp.float32)
        W_e = jax.random.normal(ks[4], (HEADS, EDGE_DIM, OUT_CH), dtype=jnp.float32)
        a_s = jax.random.normal(ks[5], (HEADS, OUT_CH), dtype=jnp.float32)
        a_t = jax.random.normal(ks[6], (HEADS, OUT_CH), dtype=jnp.float32)
        a_e = jax.random.normal(ks[7], (HEADS, OUT_CH), dtype=jnp.float32)
        b_GAT = jax.random.normal(ks[8], (HEADS, OUT_CH), dtype=jnp.float32)
        return {'x': x, 'edge_index': edge_index, 'edge_attr': edge_attr, 'W': W, 'W_e': W_e, 'a_s': a_s, 'a_t': a_t, 'a_e': a_e, 'b_GAT': b_GAT}
    _L1_gnn_all = _L1_gnn_setup()
    _L1_gnn_in = {k: v for k, v in _L1_gnn_all.items() if k in ('W', 'W_e', 'a_s', 'a_t', 'a_e', 'b_GAT')}
    del _L1_gnn_all

    def _L2_gnn_setup():
        import jax, jax.numpy as jnp
        import numpy as np
        NUM_NODES = 12500
        EMBED_DIM = 64
        HIDDEN_DIM = 64
        HEADS = 4
        NEG_SLOPE = 0.2

        def _gat_conv(x, src, dst, num_nodes, W, a_s, a_d, heads, out_ch):
            h = (x @ W).reshape(-1, heads, out_ch)
            alpha_s = (h * a_s[None]).sum(-1)
            alpha_d = (h * a_d[None]).sum(-1)
            e = alpha_s[src] + alpha_d[dst]
            e = jnp.where(e > 0, e, NEG_SLOPE * e)
            m = jax.ops.segment_max(e, dst, num_segments=num_nodes)
            w = jnp.exp(e - m[dst])
            denom = jax.ops.segment_sum(w, dst, num_segments=num_nodes)
            alpha = w / (denom[dst] + 1e-16)
            out = jax.ops.segment_sum(alpha[:, :, None] * h[src], dst, num_segments=num_nodes)
            return out

        def _forward(edge_index, emb, W1, a_src1, a_dst1, b1, W2, a_src2, a_dst2, b2):
            N = emb.shape[0]
            loops = jnp.arange(N, dtype=edge_index.dtype)
            src = jnp.concatenate([edge_index[0], loops])
            dst = jnp.concatenate([edge_index[1], loops])
            x = _gat_conv(emb, src, dst, N, W1, a_src1, a_dst1, HEADS, HIDDEN_DIM // HEADS)
            x = x.reshape(N, -1) + b1
            x = jax.nn.elu(x)
            x = _gat_conv(x, src, dst, N, W2, a_src2, a_dst2, 1, HIDDEN_DIM)
            x = x[:, 0, :] + b2
            norm = jnp.maximum(jnp.linalg.norm(x, axis=1, keepdims=True), 1e-12)
            return x / norm
        key = jax.random.key(seed)
        ks = jax.random.split(key, 10)
        E = 125000
        edge_index = jax.random.randint(ks[0], (2, E), 0, NUM_NODES, dtype=jnp.int64)
        out1 = HIDDEN_DIM // HEADS
        s = 1.0 / np.sqrt(EMBED_DIM)
        emb = jax.random.normal(ks[1], (NUM_NODES, EMBED_DIM), jnp.float32) * s
        W1 = jax.random.normal(ks[2], (EMBED_DIM, HEADS * out1), jnp.float32) * s
        a_src1 = jax.random.normal(ks[3], (HEADS, out1), jnp.float32) * 0.1
        a_dst1 = jax.random.normal(ks[4], (HEADS, out1), jnp.float32) * 0.1
        b1 = jnp.zeros((HEADS * out1,), jnp.float32)
        W2 = jax.random.normal(ks[5], (HIDDEN_DIM, HIDDEN_DIM), jnp.float32) * s
        a_src2 = jax.random.normal(ks[6], (1, HIDDEN_DIM), jnp.float32) * 0.1
        a_dst2 = jax.random.normal(ks[7], (1, HIDDEN_DIM), jnp.float32) * 0.1
        b2 = jnp.zeros((HIDDEN_DIM,), jnp.float32)
        return {'edge_index': edge_index, 'emb': emb, 'W1': W1, 'a_src1': a_src1, 'a_dst1': a_dst1, 'b1': b1, 'W2': W2, 'a_src2': a_src2, 'a_dst2': a_dst2, 'b2': b2}
    _L2_gnn_all = _L2_gnn_setup()
    _L2_gnn_in = {k: v for k, v in _L2_gnn_all.items() if k in ('W1', 'a_src1', 'a_dst1', 'b1', 'W2', 'a_src2', 'a_dst2', 'b2')}
    del _L2_gnn_all

    def _L3_gnn_setup():
        import jax, jax.numpy as jnp
        import numpy as np
        N_NODES = 6250
        N_EDGES = 100000
        D_FEAT = 64
        AVG_D = float(np.log(17.0))
        EPS_STD = 1e-05
        EPS_BN = 1e-05
        key = jax.random.key(seed)
        k1, k2, k3, k4, k5, k6 = jax.random.split(key, 6)
        h = jax.random.normal(k1, (N_NODES, D_FEAT), jnp.float32)
        ef = jax.random.normal(k2, (N_EDGES, D_FEAT), jnp.float32)
        src = jax.random.randint(k3, (N_EDGES,), 0, N_NODES, jnp.int32)
        dst = jax.random.randint(k4, (N_EDGES,), 0, N_NODES, jnp.int32)
        gamma = jax.random.uniform(k5, (D_FEAT,), jnp.float32, 0.5, 1.5)
        beta = 0.1 * jax.random.normal(k6, (D_FEAT,), jnp.float32)
        return {'h': h, 'ef': ef, 'gamma': gamma, 'beta': beta, 'src': src, 'dst': dst}
    _L3_gnn_all = _L3_gnn_setup()
    _L3_gnn_in = {k: v for k, v in _L3_gnn_all.items() if k in ('gamma', 'beta')}
    del _L3_gnn_all
    return {'x': x, 'src': src, 'dst': dst, 'edge_attr_32': edge_attr_32, 'edge_attr_64': edge_attr_64, 'edge_attr_8': edge_attr_8, 'L0_gnn_q1_w': _L0_gnn_in['q1_w'], 'L0_gnn_q1_b': _L0_gnn_in['q1_b'], 'L0_gnn_k1_w': _L0_gnn_in['k1_w'], 'L0_gnn_k1_b': _L0_gnn_in['k1_b'], 'L0_gnn_v1_w': _L0_gnn_in['v1_w'], 'L0_gnn_v1_b': _L0_gnn_in['v1_b'], 'L0_gnn_e1_w': _L0_gnn_in['e1_w'], 'L0_gnn_s1_w': _L0_gnn_in['s1_w'], 'L0_gnn_s1_b': _L0_gnn_in['s1_b'], 'L0_gnn_q2_w': _L0_gnn_in['q2_w'], 'L0_gnn_q2_b': _L0_gnn_in['q2_b'], 'L0_gnn_k2_w': _L0_gnn_in['k2_w'], 'L0_gnn_k2_b': _L0_gnn_in['k2_b'], 'L0_gnn_v2_w': _L0_gnn_in['v2_w'], 'L0_gnn_v2_b': _L0_gnn_in['v2_b'], 'L0_gnn_e2_w': _L0_gnn_in['e2_w'], 'L0_gnn_s2_w': _L0_gnn_in['s2_w'], 'L0_gnn_s2_b': _L0_gnn_in['s2_b'], 'L0_gnn_skip_w': _L0_gnn_in['skip_w'], 'L0_gnn_skip_b': _L0_gnn_in['skip_b'], 'L1_gnn_W': _L1_gnn_in['W'], 'L1_gnn_W_e': _L1_gnn_in['W_e'], 'L1_gnn_a_s': _L1_gnn_in['a_s'], 'L1_gnn_a_t': _L1_gnn_in['a_t'], 'L1_gnn_a_e': _L1_gnn_in['a_e'], 'L1_gnn_b_GAT': _L1_gnn_in['b_GAT'], 'L2_gnn_W1': _L2_gnn_in['W1'], 'L2_gnn_a_src1': _L2_gnn_in['a_src1'], 'L2_gnn_a_dst1': _L2_gnn_in['a_dst1'], 'L2_gnn_b1': _L2_gnn_in['b1'], 'L2_gnn_W2': _L2_gnn_in['W2'], 'L2_gnn_a_src2': _L2_gnn_in['a_src2'], 'L2_gnn_a_dst2': _L2_gnn_in['a_dst2'], 'L2_gnn_b2': _L2_gnn_in['b2'], 'L3_gnn_gamma': _L3_gnn_in['gamma'], 'L3_gnn_beta': _L3_gnn_in['beta']}

def reference(x, src, dst, edge_attr_32, edge_attr_64, edge_attr_8, L0_gnn_q1_w, L0_gnn_q1_b, L0_gnn_k1_w, L0_gnn_k1_b, L0_gnn_v1_w, L0_gnn_v1_b, L0_gnn_e1_w, L0_gnn_s1_w, L0_gnn_s1_b, L0_gnn_q2_w, L0_gnn_q2_b, L0_gnn_k2_w, L0_gnn_k2_b, L0_gnn_v2_w, L0_gnn_v2_b, L0_gnn_e2_w, L0_gnn_s2_w, L0_gnn_s2_b, L0_gnn_skip_w, L0_gnn_skip_b, L1_gnn_W, L1_gnn_W_e, L1_gnn_a_s, L1_gnn_a_t, L1_gnn_a_e, L1_gnn_b_GAT, L2_gnn_W1, L2_gnn_a_src1, L2_gnn_a_dst1, L2_gnn_b1, L2_gnn_W2, L2_gnn_a_src2, L2_gnn_a_dst2, L2_gnn_b2, L3_gnn_gamma, L3_gnn_beta):
    import jax
    import jax.numpy as jnp

    def _L0_gnn_ref(x, edge_index, edge_attr, q1_w, q1_b, k1_w, k1_b, v1_w, v1_b, e1_w, s1_w, s1_b, q2_w, q2_b, k2_w, k2_b, v2_w, v2_b, e2_w, s2_w, s2_b, skip_w, skip_b):
        import jax, jax.numpy as jnp
        import numpy as np
        N = 6250
        E = 100000
        D = 64
        H = 64
        DE = 32

        def _transformer_conv(x, src, dst, edge_attr, wq, bq, wk, bk, wv, bv, we, ws, bs, n_nodes):
            q = x @ wq + bq
            k = x @ wk + bk
            v = x @ wv + bv
            e = edge_attr @ we
            ke = k[src] + e
            score = jnp.sum(q[dst] * ke, axis=-1) / jnp.sqrt(jnp.asarray(ke.shape[-1], x.dtype))
            smax = jax.ops.segment_max(score, dst, num_segments=n_nodes)
            a = jnp.exp(score - smax[dst])
            denom = jax.ops.segment_sum(a, dst, num_segments=n_nodes)
            alpha = a / denom[dst]
            msg = alpha[:, None] * (v[src] + e)
            out = jax.ops.segment_sum(msg, dst, num_segments=n_nodes)
            out = out + x @ ws + bs
            return out
        src, dst = (edge_index[0], edge_index[1])
        n = x.shape[0]
        h1 = jax.nn.relu(_transformer_conv(x, src, dst, edge_attr, q1_w, q1_b, k1_w, k1_b, v1_w, v1_b, e1_w, s1_w, s1_b, n))
        h2 = jax.nn.relu(_transformer_conv(h1, src, dst, edge_attr, q2_w, q2_b, k2_w, k2_b, v2_w, v2_b, e2_w, s2_w, s2_b, n))
        skip_xs = jnp.concatenate([h1, h2], axis=-1)
        return jax.nn.relu(skip_xs @ skip_w + skip_b)

    def _L1_gnn_ref(x, edge_index, edge_attr, W, W_e, a_s, a_t, a_e, b_GAT):
        import jax, jax.numpy as jnp
        import numpy as np
        N_NODES = 12500
        N_EDGES = 200000
        IN_CH, OUT_CH, HEADS, EDGE_DIM = (64, 16, 4, 8)
        NEG_SLOPE = 0.2
        N = x.shape[0]
        row, col = (edge_index[0], edge_index[1])
        x_proj = jnp.einsum('hio,ni->hno', W, x)
        e_proj = jnp.einsum('hdo,ed->heo', W_e, edge_attr)
        ax_s = jnp.einsum('ho,hno->hn', a_s, x_proj)
        ax_t = jnp.einsum('ho,hno->hn', a_t, x_proj)
        ae = jnp.einsum('ho,heo->he', a_e, e_proj)
        logits = jax.nn.leaky_relu(ax_s[:, row] + ax_t[:, col] + ae, NEG_SLOPE)
        seg_max = jax.ops.segment_max(logits.T, col, num_segments=N)
        w = jnp.exp(logits - seg_max[col].T)
        denom = jax.ops.segment_sum(w.T, col, num_segments=N)
        alpha = w / denom[col].T
        msgs = alpha[..., None] * x_proj[:, row]
        out = jax.ops.segment_sum(msgs.transpose(1, 0, 2), col, num_segments=N)
        out = out + b_GAT[None]
        return out.reshape(N, -1)

    def _L2_gnn_ref(edge_index, emb, W1, a_src1, a_dst1, b1, W2, a_src2, a_dst2, b2):
        import jax, jax.numpy as jnp
        import numpy as np
        NUM_NODES = 12500
        EMBED_DIM = 64
        HIDDEN_DIM = 64
        HEADS = 4
        NEG_SLOPE = 0.2

        def _gat_conv(x, src, dst, num_nodes, W, a_s, a_d, heads, out_ch):
            h = (x @ W).reshape(-1, heads, out_ch)
            alpha_s = (h * a_s[None]).sum(-1)
            alpha_d = (h * a_d[None]).sum(-1)
            e = alpha_s[src] + alpha_d[dst]
            e = jnp.where(e > 0, e, NEG_SLOPE * e)
            m = jax.ops.segment_max(e, dst, num_segments=num_nodes)
            w = jnp.exp(e - m[dst])
            denom = jax.ops.segment_sum(w, dst, num_segments=num_nodes)
            alpha = w / (denom[dst] + 1e-16)
            out = jax.ops.segment_sum(alpha[:, :, None] * h[src], dst, num_segments=num_nodes)
            return out

        def _forward(edge_index, emb, W1, a_src1, a_dst1, b1, W2, a_src2, a_dst2, b2):
            N = emb.shape[0]
            loops = jnp.arange(N, dtype=edge_index.dtype)
            src = jnp.concatenate([edge_index[0], loops])
            dst = jnp.concatenate([edge_index[1], loops])
            x = _gat_conv(emb, src, dst, N, W1, a_src1, a_dst1, HEADS, HIDDEN_DIM // HEADS)
            x = x.reshape(N, -1) + b1
            x = jax.nn.elu(x)
            x = _gat_conv(x, src, dst, N, W2, a_src2, a_dst2, 1, HIDDEN_DIM)
            x = x[:, 0, :] + b2
            norm = jnp.maximum(jnp.linalg.norm(x, axis=1, keepdims=True), 1e-12)
            return x / norm
        return _forward(edge_index, emb, W1, a_src1, a_dst1, b1, W2, a_src2, a_dst2, b2)

    def _L3_gnn_ref(h, ef, gamma, beta, src, dst):
        import jax, jax.numpy as jnp
        import numpy as np
        N_NODES = 6250
        N_EDGES = 100000
        D_FEAT = 64
        AVG_D = float(np.log(17.0))
        EPS_STD = 1e-05
        EPS_BN = 1e-05
        N, d = h.shape
        z = h[src] + h[dst] + ef
        deg = jax.ops.segment_sum(jnp.ones((z.shape[0],), z.dtype), dst, num_segments=N)
        deg_safe = jnp.maximum(deg, 1.0)[:, None]
        has_edge = (deg > 0)[:, None]
        mean = jax.ops.segment_sum(z, dst, num_segments=N) / deg_safe
        mean_sq = jax.ops.segment_sum(z * z, dst, num_segments=N) / deg_safe
        std = jnp.sqrt(jax.nn.relu(mean_sq - mean * mean) + EPS_STD)
        mx = jnp.where(has_edge, jax.ops.segment_max(z, dst, num_segments=N), 0.0)
        mn = jnp.where(has_edge, jax.ops.segment_min(z, dst, num_segments=N), 0.0)
        agg = jnp.concatenate([mean, mx, mn, std], axis=1)
        log_deg = jnp.log(deg + 1.0)
        amp = agg * (log_deg / AVG_D)[:, None]
        att = agg * (AVG_D / jnp.where(deg > 0, log_deg, 1.0))[:, None]
        h_agg = jnp.concatenate([agg, amp, att], axis=1)
        h_agg = jnp.where(has_edge, h_agg, 0.0)
        hc = jnp.concatenate([h, h_agg], axis=1).reshape(N, 13, d).mean(axis=1)
        mu = hc.mean(axis=0)
        var = hc.var(axis=0)
        out = (hc - mu) / jnp.sqrt(var + EPS_BN) * gamma + beta
        return out
    edge_index = jnp.stack([src, dst])
    h = jnp.maximum(_layernorm(x, axis=-1), 0.0)
    x = x + _L0_gnn_ref(h, edge_index, edge_attr_32, L0_gnn_q1_w, L0_gnn_q1_b, L0_gnn_k1_w, L0_gnn_k1_b, L0_gnn_v1_w, L0_gnn_v1_b, L0_gnn_e1_w, L0_gnn_s1_w, L0_gnn_s1_b, L0_gnn_q2_w, L0_gnn_q2_b, L0_gnn_k2_w, L0_gnn_k2_b, L0_gnn_v2_w, L0_gnn_v2_b, L0_gnn_e2_w, L0_gnn_s2_w, L0_gnn_s2_b, L0_gnn_skip_w, L0_gnn_skip_b)
    h = jnp.maximum(_layernorm(x, axis=-1), 0.0)
    x = x + _L1_gnn_ref(h, edge_index, edge_attr_8, L1_gnn_W, L1_gnn_W_e, L1_gnn_a_s, L1_gnn_a_t, L1_gnn_a_e, L1_gnn_b_GAT)
    h = jnp.maximum(_layernorm(x, axis=-1), 0.0)
    x = x + _L2_gnn_ref(edge_index, h, L2_gnn_W1, L2_gnn_a_src1, L2_gnn_a_dst1, L2_gnn_b1, L2_gnn_W2, L2_gnn_a_src2, L2_gnn_a_dst2, L2_gnn_b2)
    h = jnp.maximum(_layernorm(x, axis=-1), 0.0)
    x = x + _L3_gnn_ref(h, edge_attr_64, L3_gnn_gamma, L3_gnn_beta, src, dst)
    return x

_drawn_inputs = setup_inputs


def setup_inputs(seed=0):
    import zlib

    import numpy as np

    out = dict(_drawn_inputs(seed))
    spreads = {'L0_gnn_q1_b': (0.0, 0.1),
     'L0_gnn_k1_b': (0.0, 0.8),
     'L0_gnn_v1_b': (0.0, 0.1),
     'L0_gnn_s1_b': (0.0, 0.1),
     'L0_gnn_q2_b': (0.0, 0.1),
     'L0_gnn_k2_b': (0.0, 0.8),
     'L0_gnn_v2_b': (0.0, 0.1),
     'L0_gnn_s2_b': (0.0, 0.1),
     'L0_gnn_skip_b': (0.0, 0.1),
     'L2_gnn_b1': (0.0, 0.8),
     'L2_gnn_b2': (0.0, 0.8)}
    factors = {'L2_gnn_W1': 2.923,
     'L2_gnn_a_src1': 8.0,
     'L2_gnn_a_dst1': 8.0,
     'L2_gnn_W2': 3.386,
     'L2_gnn_a_src2': 8.0,
     'L2_gnn_a_dst2': 8.0,
     'L3_gnn_beta': 3.424}
    for name, (base, spread) in spreads.items():
        noise = np.random.default_rng([zlib.crc32(name.encode()), seed]).standard_normal(out[name].shape)
        drawn = base * np.exp(spread * noise) if base else spread * noise
        out[name] = jnp.asarray(drawn.astype(out[name].dtype))
    for name, factor in factors.items():
        out[name] = (out[name] * factor).astype(out[name].dtype)
    return out
```

```python
from contextlib import ExitStack

import numpy as np

import concourse.bass as bass
from concourse import mybir

F32 = mybir.dt.float32
I32 = mybir.dt.int32
BF16 = mybir.dt.bfloat16
ALU = mybir.AluOpType
ACT = mybir.ActivationFunctionType
AX = mybir.AxisListType

P = 128
D = 64
N_NODES, N_EDGES = 12500, 200000
NC = 98
NP_ = P * NC
G = 16
NG = 98
ET = G * NG
EP = P * ET
NB = 7
NBLK = NC // NB
DE = 32
YT = D + DE + 1
BIG = 1.0e30
TINY = 1.0e-30
SLOPE = 0.2
AVG_D = float(np.log(17.0))
HG, JG = 4, 16
TG = D + 2 * HG
OH = 14
assert NP_ >= N_NODES and EP >= N_EDGES and NBLK % 2 == 0 and NG % 2 == 0


class Signal:

    def __init__(self, h):
        self.h, self.base = h, 0

    def __call__(self, n):
        return self.h, n + self.base


class Chain:

    def __init__(self, signal, names):
        self.upto, self.names = signal, names.split()
        self.h = signal.h

    def before(self, name):
        return self.upto(self.names.index(name))

    def __len__(self):
        return len(self.names)


class Stage:

    def __init__(self, nc, tag, signals):
        self.nc, self.tag, self.signals, self.used = nc, tag, signals, {}
        self.ctx = ExitStack()

    def sb(self, name, shape, dt=F32):
        return self.ctx.enter_context(self.nc.sbuf_tensor(f"{self.tag}_{name}", shape, dt))

    def ps(self, name, shape, dt=F32):
        return self.ctx.enter_context(self.nc.psum_tensor(f"{self.tag}_{name}", shape, dt))

    def sem(self, name, total):
        if name not in self.signals:
            self.signals[name] = Signal(self.nc.alloc_semaphore(name))
        self.used[name] = total
        return self.signals[name]

    def slots(self, name, total):
        return [self.sem(f"{name}{b}", total) for b in range(2)]

    def chain(self, name, names):
        c = Chain(self.sem(name, len(names.split())), names)
        return c

    def close(self):
        for name, total in self.used.items():
            self.signals[name].base += total
        self.ctx.close()


def build(nc, a, out):
    root = ExitStack()
    signals = {}

    def keep(name, shape, dt=F32):
        return root.enter_context(nc.sbuf_tensor(name, shape, dt))

    def dram(name, shape, dt=F32):
        return nc.dram_tensor(name, shape, dt, kind="Internal").ap()

    x = keep("x", [P, NC, D])
    h = keep("h", [P, NC, D])
    same = keep("same", [P, ET])
    pen = keep("pen", [P, ET])
    deg = keep("deg", [P, NC])
    has = keep("has", [P, NC])
    hneg = keep("hneg", [P, NC])
    valid = keep("valid", [P, NC])
    dst0 = keep("dst0", [P, 1], I32)
    fix_at = keep("fix_at", [P, 1], I32)
    cont = keep("cont", [P, 1])
    contpen = keep("contpen", [P, 1])
    ident = keep("ident", [P, P])
    ones = keep("ones", [P, P])
    whole_t = keep("whole_t", [P, P])
    whole_pen = keep("whole_pen", [P, P])
    eps = keep("eps", [P, 1])
    carry_v = keep("carry_v", [P, 4 * D])
    carry_m = keep("carry_m", [P, HG])

    h_tab = dram("h_tab", (NP_, D))
    q_tab = dram("q_tab", (NP_, YT))
    g_tab = dram("g_tab", (NP_, TG))
    q_start = dram("q_start", (EP + NP_, YT))
    ad_start = dram("ad_start", (EP + NP_, HG))
    start_d = dram("start_d", (P, NC), I32)
    last_d = dram("last_d", (P, NC), I32)
    rows_d = [dram(f"rows{n}_d", (EP, w)) for n, w in enumerate([YT + 1, YT + 1, TG, TG, TG, 4 * D])]

    def by_edge(t):
        return t[0:EP, :].rearrange("(p t) f -> p t f", p=P)

    def by_node(t):
        return t.rearrange("(p c) f -> p c f", p=P)

    def row_of(v, n, parts=P):
        return v.rearrange("(a n) -> a n", a=1).to_broadcast([parts, n])

    def indexed(ap):
        return bass.IndirectOffsetOnAxis(ap=ap, axis=0)

    def setup():
        st = Stage(nc, "setup", signals)
        sb = st.sb
        cur_i, prev_i = sb("cur_i", [P, ET], I32), sb("prev_i", [P, ET], I32)
        cur, prev = sb("cur", [P, ET]), sb("prev", [P, ET])
        hi, lo = sb("hi", [P, ET]), sb("lo", [P, ET])
        iota_i, iota = sb("iota_i", [P, P], I32), sb("iota", [P, P])
        row_i, row = sb("row_i", [P, 1], I32), sb("row", [P, 1])
        node_i, node = sb("node_i", [P, NC], I32), sb("node", [P, NC])
        oh_hi, oh_lo = sb("oh_hi", [P, 2, OH, P], BF16), sb("oh_lo", [P, 2, OH, NC], BF16)
        zero16, zero = sb("zero16", [P, P], BF16), sb("zero", [P, ET // 2 * HG])
        upper = sb("upper", [P, P])
        cnt, whole, fixf, incl, excl = (sb(n, [P, 1]) for n in ("cnt", "whole", "fixf", "incl1", "excl"))
        run = sb("run", [P, NC])
        startf, lastf, none_at = sb("startf", [P, NC]), sb("lastf", [P, NC]), sb("none_at", [P, NC])
        start_i, last_i = sb("start_i", [P, NC], I32), sb("last_i", [P, NC], I32)
        wide = sb("wide", [P, P])
        counts, before, turned = st.ps("counts", [P, 512]), st.ps("before", [P, 512]), st.ps("turned", [P, 512])

        loaded = st.sem("loaded", 3 * 16)
        zeroed = st.sem("zeroed", 2)
        filled = st.sem("filled", 16 * (NG // 2 + 1))
        patterns = st.sem("patterns", 9)
        hot = st.slots("hot", ET // OH // 2)
        counted = st.slots("counted", ET // OH // 2)
        all_counted = st.sem("all_counted", 1)
        vs = st.chain("setup_steps", """cur prev same pen eq cnt cont contpen whole1 whole dst0 row fixf fix_at iota node
            valid none_at hi1 hi2 lo wide turned whole_t whole_pen deg has hneg run tot excl startf lastf lastc lasti none1
            none2 start2 starti""")
        stored = st.sem("stored", 48)

        with nc.Block() as block:
            @block.sync
            def _(sp):
                sp.dma_start(x[:], by_node(a["x"])).then_inc(loaded.h, 16)
                sp.dma_start(cur_i[:], a["dst"][1:EP + 1].rearrange("(p t) -> p t", p=P)).then_inc(loaded.h, 16)
                sp.dma_start(prev_i[:], a["dst"][0:EP].rearrange("(p t) -> p t", p=P)).then_inc(loaded.h, 16)
                sp.wait_ge(*zeroed(2))
                with sp.Fori(0, NG // 2) as i:
                    sp.dma_start(by_edge(q_start)[:, bass.ds(i * (2 * G), 2 * G), :].rearrange("p t f -> p (t f)"),
                                 zero[:, 0:2 * G * YT]).then_inc(filled.h, 16)
                sp.dma_start(ad_start[0:EP // 2, :].rearrange("(p t) f -> p (t f)", p=P),
                             zero[:]).then_inc(filled.h, 16)
                sp.wait_ge(*filled(16 * (NG // 2 + 1)))

            @block.gpsimd
            def _(pool):
                nc.gpsimd.iota(iota_i[:], pattern=[[1, P]], base=0, channel_multiplier=0).then_inc(patterns.h, 1)
                nc.gpsimd.iota(row_i[:], pattern=[[0, 1]], base=0, channel_multiplier=ET).then_inc(patterns.h, 1)
                nc.gpsimd.iota(node_i[:], pattern=[[1, NC]], base=0, channel_multiplier=NC).then_inc(patterns.h, 1)
                nc.gpsimd.memset(ident[:], 0.0).then_inc(patterns.h, 1)
                nc.gpsimd.memset(upper[:], 1.0).then_inc(patterns.h, 1)
                nc.gpsimd.memset(ones[:], 1.0).then_inc(patterns.h, 1)
                nc.gpsimd.memset(eps[:], 1e-5).then_inc(patterns.h, 1)
                pool.wait_ge(*patterns(7))
                nc.gpsimd.affine_select(out=ident[:], in_=ident[:], compare_op=ALU.not_equal, fill=1.0, base=0,
                                        pattern=[[-1, P]], channel_multiplier=1).then_inc(patterns.h, 1)
                nc.gpsimd.affine_select(out=upper[:], in_=upper[:], compare_op=ALU.is_gt, fill=0.0, base=0,
                                        pattern=[[1, P]], channel_multiplier=-1).then_inc(patterns.h, 1)

            @block.vector
            def _(v):

                v.memset(zero16[:], 0.0).then_inc(zeroed.h, 1)
                v.memset(zero[:], 0.0).then_inc(zeroed.h, 1)
                v.wait_ge(*loaded(48))
                v.wait_ge(*vs.before("cur"))
                v.tensor_copy(cur[:], cur_i[:]).then_inc(vs.h, 1)
                v.wait_ge(*vs.before("prev"))
                v.tensor_copy(prev[:], prev_i[:]).then_inc(vs.h, 1)
                v.wait_ge(*vs.before("same"))
                v.tensor_tensor(same[:], cur[:], prev[:], ALU.is_equal).then_inc(vs.h, 1)
                v.wait_ge(*vs.before("pen"))
                v.tensor_scalar(pen[:], same[:], -1.0, BIG, ALU.add, ALU.mult).then_inc(vs.h, 1)
                v.wait_ge(*vs.before("eq"))
                v.tensor_scalar(prev[:], cur[:], cur[:, 0:1], None, ALU.is_equal).then_inc(vs.h, 1)
                v.wait_ge(*vs.before("cnt"))
                v.reduce_sum(cnt[:], prev[:], axis=AX.X).then_inc(vs.h, 1)
                v.wait_ge(*vs.before("cont"))
                v.tensor_copy(cont[:], same[:, 0:1]).then_inc(vs.h, 1)
                v.wait_ge(*vs.before("contpen"))
                v.tensor_copy(contpen[:], pen[:, 0:1]).then_inc(vs.h, 1)
                v.wait_ge(*vs.before("whole1"))
                v.tensor_scalar(whole[:], cnt[:], float(ET), None, ALU.is_equal).then_inc(vs.h, 1)
                v.wait_ge(*vs.before("whole"))
                v.tensor_tensor(whole[:], whole[:], cont[:], ALU.mult).then_inc(vs.h, 1)
                v.wait_ge(*patterns(9))
                v.wait_ge(*vs.before("dst0"))
                v.tensor_copy(dst0[:], cur_i[:, 0:1]).then_inc(vs.h, 1)
                v.wait_ge(*vs.before("row"))
                v.tensor_copy(row[:], row_i[:]).then_inc(vs.h, 1)
                v.wait_ge(*vs.before("fixf"))
                v.scalar_tensor_tensor(out=fixf[:], in0=cnt[:], scalar=-1.0, in1=row[:],
                                       op0=ALU.add, op1=ALU.add).then_inc(vs.h, 1)
                v.wait_ge(*vs.before("fix_at"))
                v.tensor_copy(fix_at[:], fixf[:]).then_inc(vs.h, 1)
                v.wait_ge(*vs.before("iota"))
                v.tensor_copy(iota[:], iota_i[:]).then_inc(vs.h, 1)
                v.wait_ge(*vs.before("node"))
                v.tensor_copy(node[:], node_i[:]).then_inc(vs.h, 1)
                v.wait_ge(*vs.before("valid"))
                v.tensor_scalar(valid[:], node[:], float(N_NODES), None, ALU.is_lt).then_inc(vs.h, 1)
                v.wait_ge(*vs.before("none_at"))
                v.tensor_scalar(none_at[:], node[:], float(EP), None, ALU.add).then_inc(vs.h, 1)
                v.wait_ge(*vs.before("hi1"))
                v.tensor_scalar(hi[:], cur[:], -(NC - 1) / 2.0, 1.0 / NC, ALU.add, ALU.mult).then_inc(vs.h, 1)
                v.wait_ge(*vs.before("hi2"))
                v.tensor_scalar(hi[:], hi[:], 1.5 * 2.0 ** 23, -1.5 * 2.0 ** 23, ALU.add, ALU.add).then_inc(vs.h, 1)
                v.wait_ge(*vs.before("lo"))
                v.scalar_tensor_tensor(out=lo[:], in0=hi[:], scalar=-float(NC), in1=cur[:],
                                       op0=ALU.mult, op1=ALU.add).then_inc(vs.h, 1)
                v.wait_ge(*vs.before("wide"))
                v.tensor_copy(wide[:], whole[:].to_broadcast([P, P])).then_inc(vs.h, 1)
                v.wait_ge(*vs.before("turned"))
                with v.Fori(0, ET // OH // 2) as i:
                    for b in range(2):
                        t0 = (i * 2 + b) * OH
                        v.wait_ge(*counted[b](i))
                        v.tensor_tensor(oh_hi[:, b], hi[:, bass.ds(t0, OH)].unsqueeze(2).to_broadcast([P, OH, P]),
                                        iota[:].unsqueeze(1).to_broadcast([P, OH, P]), ALU.is_equal)
                        v.tensor_tensor(oh_lo[:, b], lo[:, bass.ds(t0, OH)].unsqueeze(2).to_broadcast([P, OH, NC]),
                                        iota[:, 0:NC].unsqueeze(1).to_broadcast([P, OH, NC]),
                                        ALU.is_equal).then_inc(hot[b].h, 1)
                v.wait_ge(*vs.before("whole_t"))
                v.tensor_copy(whole_t[:], turned[:, 0:P]).then_inc(vs.h, 1)
                v.wait_ge(*vs.before("whole_pen"))
                v.tensor_scalar(whole_pen[:], whole_t[:], -1.0, BIG, ALU.add, ALU.mult).then_inc(vs.h, 1)
                v.wait_ge(*all_counted(1))
                v.wait_ge(*vs.before("deg"))
                v.tensor_copy(deg[:], counts[:, 0:NC]).then_inc(vs.h, 1)
                v.wait_ge(*vs.before("has"))
                v.tensor_scalar(has[:], deg[:], 1.0, None, ALU.min).then_inc(vs.h, 1)
                v.wait_ge(*vs.before("hneg"))
                v.tensor_scalar(hneg[:], has[:], -1.0, BIG, ALU.add, ALU.mult).then_inc(vs.h, 1)
                v.wait_ge(*vs.before("run"))
                v.tensor_tensor_scan(run[:], ones[:, 0:NC], deg[:], 0.0, ALU.mult, ALU.add).then_inc(vs.h, 1)
                v.wait_ge(*vs.before("excl"))
                v.tensor_copy(excl[:], before[:, 0:1]).then_inc(vs.h, 1)
                v.wait_ge(*vs.before("startf"))
                v.tensor_scalar(lastf[:], run[:], excl[:, 0:1], None, ALU.add).then_inc(vs.h, 1)
                v.wait_ge(*vs.before("lastf"))
                v.tensor_tensor(startf[:], lastf[:], deg[:], ALU.subtract).then_inc(vs.h, 1)
                v.wait_ge(*vs.before("lastc"))
                v.tensor_scalar(lastf[:], lastf[:], -1.0, 0.0, ALU.add, ALU.max).then_inc(vs.h, 1)
                v.wait_ge(*vs.before("lasti"))
                v.tensor_copy(last_i[:], lastf[:]).then_inc(vs.h, 1)
                v.wait_ge(*vs.before("none1"))
                v.tensor_tensor(startf[:], startf[:], none_at[:], ALU.subtract).then_inc(vs.h, 1)
                v.wait_ge(*vs.before("none2"))
                v.tensor_tensor(startf[:], startf[:], has[:], ALU.mult).then_inc(vs.h, 1)
                v.wait_ge(*vs.before("start2"))
                v.tensor_tensor(startf[:], startf[:], none_at[:], ALU.add).then_inc(vs.h, 1)
                v.wait_ge(*vs.before("starti"))
                v.tensor_copy(start_i[:], startf[:]).then_inc(vs.h, 1)

            @block.tensor
            def _(pe):
                pe.wait_ge(*patterns(9))
                pe.wait_ge(*vs.before("turned"))
                nc.tensor.transpose(turned[:, 0:P], wide[:], ident[:]).then_inc(vs.h, 1)
                pe.wait_ge(*zeroed(1))
                nc.tensor.matmul(counts[:, 0:NC], zero16[:], zero16[:, 0:NC], start=True, stop=False)
                with pe.Fori(0, ET // OH // 2) as i:
                    for b in range(2):
                        pe.wait_ge(*hot[b](i + 1))
                        pe.nop(nofuse=True)
                        for k in range(OH):
                            last = nc.tensor.matmul(counts[:, 0:NC], oh_hi[:, b, k, :], oh_lo[:, b, k, :],
                                                    start=False, stop=False)
                        last.then_inc(counted[b].h, 1)
                nc.tensor.matmul(counts[:, 0:NC], zero16[:], zero16[:, 0:NC], start=False,
                                 stop=True).then_inc(all_counted.h, 1)
                pe.wait_ge(*vs.before("tot"))
                nc.tensor.matmul(before[:, 0:1], upper[:], run[:, NC - 1:NC], start=True, stop=True).then_inc(vs.h, 1)

            @block.scalar
            def _(act):
                act.wait_ge(*zeroed(2))
                act.dma_start(ad_start[EP // 2:EP, :].rearrange("(p t) f -> p (t f)", p=P),
                              zero[:]).then_inc(stored.h, 16)
                act.wait_ge(*vs.before("none1"))
                act.dma_start(last_d, last_i[:]).then_inc(stored.h, 16)
                act.wait_ge(*vs.upto(len(vs)))
                act.dma_start(start_d, start_i[:]).then_inc(stored.h, 16)
                act.wait_ge(*stored(48))
        st.close()

    def layer_norm(tag):
        st = Stage(nc, tag, signals)
        sq = st.sb("sq", [P, NC, D])
        mean, var, sd, rs = (st.sb(n, [P, NC]) for n in ("mean", "var", "sd", "rs"))
        summed, scaled, centred = (st.sem(n, 2) for n in ("ln_summed", "ln_scaled", "ln_centred"))
        squared, var_ready, rooted = (st.sem(n, 2) for n in ("ln_squared", "ln_var", "ln_rooted"))
        inverted, done = (st.sem(n, 2) for n in ("ln_inverted", "ln_done"))
        half = [slice(0, NC // 2), slice(NC // 2, NC)]

        def wide(t, s):
            return t[:, s].unsqueeze(2).to_broadcast([P, NC // 2, D])

        with nc.Block() as block:
            @block.vector
            def _(v):
                for n, s in enumerate(half):
                    v.reduce_sum(mean[:, s], x[:, s, :], axis=AX.X).then_inc(summed.h, 1)
                    v.wait_ge(*summed(n + 1))
                    v.tensor_scalar(mean[:, s], mean[:, s], 1.0 / D, None, ALU.mult).then_inc(scaled.h, 1)
                    v.wait_ge(*scaled(n + 1))
                    v.tensor_tensor(h[:, s, :], x[:, s, :], wide(mean, s), ALU.subtract).then_inc(centred.h, 1)
                for n, s in enumerate(half):
                    v.wait_ge(*squared(n + 1))
                    v.reduce_sum(var[:, s], sq[:, s, :], axis=AX.X).then_inc(var_ready.h, 1)
                for n, s in enumerate(half):
                    v.wait_ge(*rooted(n + 1))
                    v.reciprocal(rs[:, s], sd[:, s]).then_inc(inverted.h, 1)
                    v.wait_ge(*inverted(n + 1))
                    v.scalar_tensor_tensor(out=h[:, s, :], in0=h[:, s, :], scalar=0.0, in1=wide(rs, s),
                                           op0=ALU.max, op1=ALU.mult).then_inc(done.h, 1)
                v.wait_ge(*done(2))

            @block.scalar
            def _(act):
                for n, s in enumerate(half):
                    act.wait_ge(*centred(n + 1))
                    act.activation(sq[:, s, :], h[:, s, :], ACT.Square).then_inc(squared.h, 1)
                for n, s in enumerate(half):
                    act.wait_ge(*var_ready(n + 1))
                    act.activation(sd[:, s], var[:, s], ACT.Sqrt, bias=eps[:], scale=1.0 / D).then_inc(rooted.h, 1)
        st.close()

    def prepare_conv(tag, wq_t, bq, wk_t, bk, we_t):
        st = Stage(nc, tag, signals)
        wq1 = st.sb("wq1", [D, D + 1])
        wk1 = st.sb("wk1", [D, YT])
        wqq = st.sb("wqq", [D + 1, YT])
        hs, ht = st.sb("hs", [P, NB, D]), st.sb("ht", [D + 1, NB, P])
        qs = st.sb("qs", [P, 2, NB, YT])
        at = st.sb("at", [P, 2, NB], I32)
        ps_h, ps_q, ps_w = st.ps("ps_h", [P, 8, P]), st.ps("ps_q", [P, 8, P]), st.ps("ps_w", [P, 512])
        loaded = st.sem("w_loaded", 5 * 16)
        made = st.sem("w_made", 2)
        ones_set = st.sem("ones_set", 1)
        tab = st.sem("tab_stored", 16)
        at_loaded = st.slots("at_loaded", 16 * NBLK // 2)
        scattered = st.slots("scattered", 16 * NB * NBLK // 2)
        q_stored = st.slots("q_stored", 16 * NBLK // 2)
        hs_ready, turned, ht_ready = (st.sem(n, NBLK) for n in ("hs_ready", "h_turned", "ht_ready"))
        mixed = st.sem("mixed", NBLK)
        q_ready = st.slots("q_ready", NBLK // 2)

        with nc.Block() as block:
            @block.sync
            def _(sp):
                for dst_, src_ in ((wq1[:, 0:D], wq_t), (wq1[:, D:D + 1], bq.rearrange("(n a) -> n a", a=1)),
                                   (wk1[:, 0:D], wk_t), (wk1[:, D:D + DE], we_t),
                                   (wk1[:, D + DE:YT], bk.rearrange("(n a) -> n a", a=1))):
                    sp.dma_start(dst_, src_).then_inc(loaded.h, 16)
                sp.dma_start(by_node(h_tab), h[:]).then_inc(tab.h, 16)
                with sp.Fori(0, NBLK // 2) as i:
                    for b in range(2):
                        c0 = (i * 2 + b) * NB
                        sp.wait_ge(*scattered[b](i * (16 * NB)))
                        sp.dma_start(at[:, b, :], start_d[:, bass.ds(c0, NB)]).then_inc(at_loaded[b].h, 16)
                        sp.wait_ge(*q_ready[b](i + 1))
                        sp.dma_start(by_node(q_tab)[:, bass.ds(c0, NB), :], qs[:, b]).then_inc(q_stored[b].h, 16)
                sp.wait_ge(*tab(16))
                for b in range(2):
                    sp.wait_ge(*q_stored[b](16 * NBLK // 2))
                    sp.wait_ge(*scattered[b](16 * NB * NBLK // 2))

            @block.gpsimd
            def _(pool):
                with pool.Fori(0, NBLK // 2) as i:
                    for b in range(2):
                        pool.wait_ge(*at_loaded[b](i * 16 + 16))
                        pool.nop(nofuse=True)
                        pool.wait_ge(*q_ready[b](i + 1))
                        pool.nop(nofuse=True)
                        for k in range(NB):
                            nc.gpsimd.indirect_dma_start(q_start, indexed(at[:, b, k:k + 1]), qs[:, b, k, :],
                                                         None).then_inc(scattered[b].h, 16)

            @block.scalar
            def _(act):
                act.wait_ge(*made(1))
                act.activation(wqq[:], ps_w[0:D + 1, 0:YT], ACT.Copy, scale=1.0 / 8.0).then_inc(made.h, 1)
                with act.Fori(0, NBLK // 2) as i:
                    for b in range(2):
                        g = i * 2 + b
                        act.wait_ge(*turned(g))
                        act.activation(hs[:], h[:, bass.ds(g * NB, NB), :], ACT.Copy).then_inc(hs_ready.h, 1)
                        act.wait_ge(*mixed(g + 1))
                        act.wait_ge(*scattered[b](i * (16 * NB)))
                        act.wait_ge(*q_stored[b](i * 16))
                        act.activation(qs[:, b], ps_q[:, 0:NB, 0:YT], ACT.Copy).then_inc(q_ready[b].h, 1)

            @block.vector
            def _(v):
                v.memset(ht[D:D + 1], 1.0).then_inc(ones_set.h, 1)
                with v.Fori(0, NBLK // 2) as i:
                    for b in range(2):
                        g = i * 2 + b
                        v.wait_ge(*turned(g + 1))
                        v.wait_ge(*mixed(g))
                        v.tensor_copy(ht[0:D], ps_h[0:D, 0:NB, :]).then_inc(ht_ready.h, 1)

            @block.tensor
            def _(pe):
                pe.wait_ge(*loaded(80))
                nc.tensor.matmul(ps_w[0:D + 1, 0:YT], wq1[:], wk1[:], start=True, stop=True).then_inc(made.h, 1)
                pe.wait_ge(*made(2))
                pe.wait_ge(*ones_set(1))
                with pe.Fori(0, NBLK // 2) as i:
                    for b in range(2):
                        g = i * 2 + b
                        pe.wait_ge(*hs_ready(g + 1))
                        pe.nop(nofuse=True)
                        pe.wait_ge(*ht_ready(g))
                        pe.nop(nofuse=True)
                        for k in range(NB):
                            last = nc.tensor.transpose(ps_h[0:D, k, :], hs[:, k, :], ident[:])
                        last.then_inc(turned.h, 1)
                        pe.wait_ge(*ht_ready(g + 1))
                        pe.nop(nofuse=True)
                        if b == 0:
                            pe.wait_ge(*q_ready[1](i))
                        else:
                            pe.wait_ge(*q_ready[0](i + 1))
                        pe.nop(nofuse=True)
                        for k in range(NB):
                            last = nc.tensor.matmul(ps_q[:, k, 0:YT], ht[:, k, :], wqq[:], start=True, stop=True)
                        last.then_inc(mixed.h, 1)
        st.close()

    def conv_edges(tag, rows):
        H, F = 1, YT
        st = Stage(nc, tag, signals)
        at = st.sb("at", [P, 2, G], I32)
        q_raw, y = st.sb("q_raw", [P, 2, G, F]), st.sb("y", [P, 2, G, F])
        q_in, mask = st.sb("q_in", [P, 2, F, G + 1]), st.sb("mask", [P, 2, F, G + 1])
        q_all, prod = st.sb("q_all", [P, F, G + 1]), st.sb("prod", [P, G, F])
        s, fm = st.sb("s", [P, G]), st.sb("fm", [P, 2, G + 1])
        de, ex = st.sb("de", [P, 2, G]), st.sb("ex", [P, 2, G])
        r, w_in = st.sb("r", [P, F, G + 1]), st.sb("w_in", [P, F, G + 1])
        acc = st.sb("acc", [P, 2, F, G + 1])
        row = st.sb("row", [P, 2, G, F + 1])
        q0 = st.sb("q0", [P, F])
        half = NG // 2
        ready = st.sem("edges_ready", 8)
        q0_got = st.sem("q0_got", 16)
        at_loaded, q_loaded, e_loaded = (st.slots(n, 16 * half) for n in ("at_loaded", "q_loaded", "e_loaded"))
        gathered = st.slots(f"gathered_{tag}_", 16 * G * half)
        q_turned, weighted, row_ready = (st.slots(n, half) for n in ("q_turned", "weighted", "row_ready"))
        row_stored = st.slots("row_stored", 16 * half)
        filled, q_carried, multiplied, scored = (st.sem(n, NG) for n in
                                                 ("q_filled", "q_carried", "multiplied", "scored"))
        maxed, m_carried, shifted, exps, r_ready = (st.sem(n, NG) for n in
                                                    ("maxed", "m_carried", "shifted", "exps", "r_ready"))
        summed, carried = (st.sem(n, NG) for n in ("summed", "carried"))
        differed = st.sem("differed", NG)

        with nc.Block() as block:
            @block.sync
            def _(sp):
                with sp.Fori(0, half) as i:
                    for b in range(2):
                        t0 = (i * 2 + b) * G
                        sp.wait_ge(*gathered[b](i * (16 * G)))
                        sp.dma_start(at[:, b], a["src"].rearrange("(p t) -> p t", p=P)[:, bass.ds(t0, G)])\
                            .then_inc(at_loaded[b].h, 16)
                        sp.wait_ge(*q_turned[b](i))
                        sp.dma_start(q_raw[:, b], by_edge(q_start)[:, bass.ds(t0, G), :]).then_inc(q_loaded[b].h, 16)
                        sp.wait_ge(*weighted[b](i))
                        sp.dma_start(y[:, b, :, D:D + DE],
                                     a["edge_attr_32"].rearrange("(p t) f -> p t f", p=P)[:, bass.ds(t0, G), :])\
                            .then_inc(e_loaded[b].h, 16)

            @block.gpsimd
            def _(pool):
                nc.gpsimd.indirect_dma_start(q0[:], None, q_tab, indexed(dst0[:])).then_inc(q0_got.h, 16)
                with pool.Fori(0, half) as i:
                    for b in range(2):
                        pool.wait_ge(*at_loaded[b](i * 16 + 16))
                        pool.nop(nofuse=True)
                        pool.wait_ge(*weighted[b](i))
                        pool.nop(nofuse=True)
                        for k in range(G):
                            nc.gpsimd.indirect_dma_start(y[:, b, k, 0:D], None, h_tab, indexed(at[:, b, k:k + 1]))\
                                .then_inc(gathered[b].h, 16)

            @block.vector
            def _(v):
                v.memset(mask[:, 0, :, 0:1], 0.0).then_inc(ready.h, 1)
                v.memset(mask[:, 1, :, 0:1], 0.0).then_inc(ready.h, 1)
                v.memset(r[:, :, 0:1], 0.0).then_inc(ready.h, 1)
                v.memset(w_in[:, :, 0:1], 0.0).then_inc(ready.h, 1)
                v.memset(fm[:, 0, 0:1], -BIG).then_inc(ready.h, 1)
                v.memset(y[:, 0, :, F - 1:F], 1.0).then_inc(ready.h, 1)
                v.memset(y[:, 1, :, F - 1:F], 1.0).then_inc(ready.h, 1)
                v.wait_ge(*q0_got(16))
                v.tensor_copy(q_in[:, 0, :, 0:1], q0[:].unsqueeze(2)).then_inc(ready.h, 1)
                v.wait_ge(*ready(8))
                with v.Fori(0, half) as i:
                    for b in range(2):
                        g = i * 2 + b
                        v.wait_ge(*q_turned[b](i + 1))
                        v.wait_ge(*q_carried(g))
                        v.tensor_tensor_scan(q_all[:].rearrange("p f t -> p (f t)"),
                                             mask[:, b].rearrange("p f t -> p (f t)"),
                                             q_in[:, b].rearrange("p f t -> p (f t)"), 0.0,
                                             ALU.mult, ALU.add).then_inc(filled.h, 1)
                        v.wait_ge(*filled(g + 1))
                        v.tensor_copy(q_in[:, 1 - b, :, 0:1], q_all[:, :, G:G + 1]).then_inc(q_carried.h, 1)
                        v.wait_ge(*gathered[b](i * (16 * G) + 16 * G))
                        v.wait_ge(*e_loaded[b](i * 16 + 16))
                        v.tensor_tensor(prod[:], y[:, b], q_all[:, :, 1:G + 1].rearrange("p f t -> p t f"),
                                        ALU.mult).then_inc(multiplied.h, 1)
                        v.wait_ge(*multiplied(g + 1))
                        v.reduce_sum(s[:], prod[:], axis=AX.X).then_inc(scored.h, 1)
                        v.wait_ge(*scored(g + 1))
                        v.wait_ge(*m_carried(g))
                        v.tensor_tensor_scan(fm[:, b, 1:G + 1], pen[:, bass.ds(g * G, G)], s[:], fm[:, b, 0:1],
                                             ALU.add, ALU.max).then_inc(maxed.h, 1)
                        v.wait_ge(*maxed(g + 1))
                        if b == 0:
                            v.wait_ge(*row_ready[1](i))
                        else:
                            v.wait_ge(*row_ready[0](i + 1))
                        v.tensor_copy(fm[:, 1 - b, 0:1], fm[:, b, G:G + 1]).then_inc(m_carried.h, 1)
                        v.tensor_tensor(de[:, 0], fm[:, b, 0:G], fm[:, b, 1:G + 1], ALU.subtract)\
                            .then_inc(differed.h, 1)
                        v.tensor_tensor(de[:, 1], s[:], fm[:, b, 1:G + 1], ALU.subtract)
                        v.wait_ge(*differed(g + 1))
                        v.tensor_tensor(de[:, 0], de[:, 0], pen[:, bass.ds(g * G, G)], ALU.add)\
                            .then_inc(shifted.h, 1)
                        v.wait_ge(*exps(g + 1))
                        v.wait_ge(*carried(g))
                        v.tensor_tensor(w_in[:, :, 1:G + 1], y[:, b].rearrange("p t f -> p f t"),
                                        ex[:, 1].unsqueeze(1).to_broadcast([P, F, G]), ALU.mult)\
                            .then_inc(weighted[b].h, 1)
                        v.wait_ge(*weighted[b](i + 1))
                        v.wait_ge(*r_ready(g + 1))
                        v.wait_ge(*row_ready[b](i))
                        v.tensor_tensor_scan(acc[:, b].rearrange("p f t -> p (f t)"),
                                             r[:].rearrange("p f t -> p (f t)"),
                                             w_in[:].rearrange("p f t -> p (f t)"), 0.0,
                                             ALU.mult, ALU.add).then_inc(summed.h, 1)
                        v.wait_ge(*summed(g + 1))
                        v.tensor_copy(w_in[:, :, 0:1], acc[:, b, :, G:G + 1]).then_inc(carried.h, 1)
                v.wait_ge(*carried(NG))
                v.tensor_copy(carry_v[:, 0:F], w_in[:, :, 0])
                v.tensor_copy(carry_m[:, 0:1], fm[:, 0, 0:1])

            @block.scalar
            def _(act):
                def turn(i, b):
                    g = i * 2 + b
                    act.wait_ge(*q_loaded[b](i * 16 + 16))
                    if b == 0:
                        if not isinstance(i, int):
                            act.wait_ge(*filled(g - 1))
                    elif not isinstance(i, int):
                        act.wait_ge(*filled(g - 1))
                    act.activation(q_in[:, b, :, 1:G + 1], q_raw[:, b].rearrange("p t f -> p f t"), ACT.Copy)
                    act.activation(mask[:, b, :, 1:G + 1],
                                   same[:, bass.ds(g * G, G)].unsqueeze(1).to_broadcast([P, F, G]), ACT.Copy)\
                        .then_inc(q_turned[b].h, 1)

                def weights(i, b):
                    g = i * 2 + b
                    act.wait_ge(*shifted(g + 1))
                    if b == 1:
                        act.wait_ge(*weighted[0](i + 1))
                    else:
                        act.wait_ge(*weighted[1](i))
                    act.activation(ex[:], de[:], ACT.Exp).then_inc(exps.h, 1)
                    act.wait_ge(*exps(g + 1))
                    act.wait_ge(*summed(g))
                    act.activation(r[:, :, 1:G + 1], ex[:, 0].unsqueeze(1).to_broadcast([P, F, G]), ACT.Copy)\
                        .then_inc(r_ready.h, 1)

                def send(i, b):
                    g = i * 2 + b
                    act.wait_ge(*summed(g + 1))
                    act.wait_ge(*row_stored[b](i * 16))
                    act.activation(row[:, b, :, F:F + 1], fm[:, b, 1:G + 1].unsqueeze(2), ACT.Copy)
                    act.activation(row[:, b, :, 0:F], acc[:, b, :, 1:G + 1].rearrange("p f t -> p t f"), ACT.Copy)\
                        .then_inc(row_ready[b].h, 1)
                    act.wait_ge(*row_ready[b](i + 1))
                    act.dma_start(by_edge(rows)[:, bass.ds(g * G, G), :], row[:, b]).then_inc(row_stored[b].h, 16)

                turn(0, 0)
                weights(0, 0)
                turn(0, 1)
                send(0, 0)
                weights(0, 1)
                with act.Fori(1, half) as i:
                    turn(i, 0)
                    send(i - 1, 1)
                    weights(i, 0)
                    turn(i, 1)
                    send(i, 0)
                    weights(i, 1)
                send(half - 1, 1)
                for b in range(2):
                    act.wait_ge(*row_stored[b](16 * half))
        st.close()

    def join_softmax(tag, rows, H, J):
        F = H * (J + 1)
        st = Stage(nc, tag, signals)
        mrep, got = st.sb("mrep", [P, F]), st.sb("got", [P, F + H])
        vt, mt = st.sb("vt", [F, P]), st.sb("mt", [F, P])
        ms, vs_ = st.sb("ms", [F, P + 1]), st.sb("vs", [F, P + 1])
        rt, wt = st.sb("rt", [F, P]), st.sb("wt", [F, P])
        vin, min_, mall = st.sb("vin", [P, F]), st.sb("min", [P, F]), st.sb("mall", [P, F])
        e_in, e_row = st.sb("e_in", [P, F]), st.sb("e_row", [P, F])
        pa, pb = st.ps("pa", [P, 512]), st.ps("pb", [P, 512])
        got_row = st.sem("fix_got", 16)
        put_row = st.sem("fix_put", 16)
        ch = st.chain("fix_steps", """mrep turn_v turn_m copy_v copy_m edge_m edge_v scan_m dr pr dw exp_r exp_w wv scan_v
            back_v back_m copy_vin copy_min pen_in max din drow exp_in exp_row vin_w row_w row_new m_new""")

        with nc.Block() as block:
            @block.gpsimd
            def _(pool):
                nc.gpsimd.indirect_dma_start(got[:], None, rows, indexed(fix_at[:])).then_inc(got_row.h, 16)
                pool.wait_ge(*ch.upto(len(ch)))
                nc.gpsimd.indirect_dma_start(rows, indexed(fix_at[:]), got[:], None).then_inc(put_row.h, 16)
                pool.wait_ge(*put_row(16))

            @block.tensor
            def _(pe):
                for name, dst_, src_, n in (("turn_v", pa[0:F, 0:P], carry_v[:, 0:F], P),
                                            ("turn_m", pb[0:F, 0:P], mrep[:], P),
                                            ("back_v", pa[:, 0:F], vs_[:, 0:P], F),
                                            ("back_m", pb[:, 0:F], ms[:, 0:P], F)):
                    pe.wait_ge(*ch.before(name))
                    nc.tensor.transpose(dst_, src_, ident[0:n, 0:n]).then_inc(ch.h, 1)

            @block.scalar
            def _(act):
                for name, t in (("exp_r", rt), ("exp_w", wt), ("exp_in", e_in), ("exp_row", e_row)):
                    act.wait_ge(*ch.before(name))
                    act.activation(t[:], t[:], ACT.Exp).then_inc(ch.h, 1)

            @block.vector
            def _(v):

                def heads(t):
                    return t.rearrange("p (h j) -> p h j", h=H)

                mrow = got[:, F:F + H].unsqueeze(2).to_broadcast([P, H, J + 1])
                v.wait_ge(*ch.before("mrep"))
                v.tensor_copy(heads(mrep[:]), carry_m[:, 0:H].unsqueeze(2).to_broadcast([P, H, J + 1]))\
                    .then_inc(ch.h, 1)
                v.wait_ge(*ch.before("copy_v"))
                v.tensor_copy(vt[:], pa[0:F, 0:P]).then_inc(ch.h, 1)
                v.wait_ge(*ch.before("copy_m"))
                v.tensor_copy(mt[:], pb[0:F, 0:P]).then_inc(ch.h, 1)
                v.wait_ge(*ch.before("edge_m"))
                v.memset(ms[:, 0:1], -BIG).then_inc(ch.h, 1)
                v.wait_ge(*ch.before("edge_v"))
                v.memset(vs_[:, 0:1], 0.0).then_inc(ch.h, 1)
                v.wait_ge(*ch.before("scan_m"))
                v.tensor_tensor_scan(ms[:, 1:P + 1], whole_pen[0:F, :], mt[:], -BIG, ALU.add, ALU.max)\
                    .then_inc(ch.h, 1)
                v.wait_ge(*ch.before("dr"))
                v.tensor_tensor(rt[:], ms[:, 0:P], ms[:, 1:P + 1], ALU.subtract).then_inc(ch.h, 1)
                v.wait_ge(*ch.before("pr"))
                v.tensor_tensor(rt[:], rt[:], whole_pen[0:F, :], ALU.add).then_inc(ch.h, 1)
                v.wait_ge(*ch.before("dw"))
                v.tensor_tensor(wt[:], mt[:], ms[:, 1:P + 1], ALU.subtract).then_inc(ch.h, 1)
                v.wait_ge(*ch.before("wv"))
                v.tensor_tensor(wt[:], wt[:], vt[:], ALU.mult).then_inc(ch.h, 1)
                v.wait_ge(*ch.before("scan_v"))
                v.tensor_tensor_scan(vs_[:, 1:P + 1], rt[:], wt[:], 0.0, ALU.mult, ALU.add).then_inc(ch.h, 1)
                v.wait_ge(*ch.before("copy_vin"))
                v.tensor_copy(vin[:], pa[:, 0:F]).then_inc(ch.h, 1)
                v.wait_ge(*ch.before("copy_min"))
                v.tensor_copy(min_[:], pb[:, 0:F]).then_inc(ch.h, 1)
                v.wait_ge(*ch.before("pen_in"))
                v.tensor_scalar(min_[:], min_[:], contpen[:, 0:1], None, ALU.add).then_inc(ch.h, 1)
                v.wait_ge(*got_row(16))
                v.wait_ge(*ch.before("max"))
                v.tensor_tensor(heads(mall[:]), heads(min_[:]), mrow, ALU.max).then_inc(ch.h, 1)
                v.wait_ge(*ch.before("din"))
                v.tensor_tensor(e_in[:], min_[:], mall[:], ALU.subtract).then_inc(ch.h, 1)
                v.wait_ge(*ch.before("drow"))
                v.tensor_tensor(heads(e_row[:]), mrow, heads(mall[:]), ALU.subtract).then_inc(ch.h, 1)
                v.wait_ge(*ch.before("vin_w"))
                v.tensor_tensor(vin[:], vin[:], e_in[:], ALU.mult).then_inc(ch.h, 1)
                v.wait_ge(*ch.before("row_w"))
                v.tensor_tensor(got[:, 0:F], got[:, 0:F], e_row[:], ALU.mult).then_inc(ch.h, 1)
                v.wait_ge(*ch.before("row_new"))
                v.tensor_tensor(got[:, 0:F], got[:, 0:F], vin[:], ALU.add).then_inc(ch.h, 1)
                v.wait_ge(*ch.before("m_new"))
                v.tensor_copy(got[:, F:F + H], heads(mall[:])[:, :, 0]).then_inc(ch.h, 1)
        st.close()

    def finish_conv(tag, rows, wv, bv, we, ws, bs, skip=None):
        st = Stage(nc, tag, signals)
        w_agg, w_self = st.sb("w_agg", [YT, D]), st.sb("w_self", [D + 1, D])
        at = st.sb("at", [P, 2, NB], I32)
        got = st.sb("got", [P, 2, NB, YT + 1])
        rd, agg = st.sb("rd", [P, NB]), st.sb("agg", [P, NB, YT])
        at_, ht = st.sb("agg_t", [YT, NB, P]), st.sb("ht", [D + 1, NB, P])
        hs = st.sb("hs", [P, NB, D])
        ps_a, ps_h = st.ps("ps_a", [P, 8, P]), st.ps("ps_h", [P, 8, P])
        ps_o = st.ps("ps_o", [P, 512])
        o = ps_o[:, 0:NB * D].rearrange("p (k f) -> p k f", k=NB)
        loads = [(w_agg[0:D, :], wv), (w_agg[D:D + DE, :], we), (w_agg[D + DE:YT, :], bv.rearrange("(a n) -> a n", a=1)),
                 (w_self[0:D, :], ws), (w_self[D:D + 1, :], bs.rearrange("(a n) -> a n", a=1))]
        if skip:
            w_sk1, w_sk2 = st.sb("w_sk1", [D + 1, D]), st.sb("w_sk2", [D, D])
            h2, h2t = st.sb("h2", [P, NB, D]), st.sb("h2t", [D, NB, P])
            ps_s = st.ps("ps_s", [P, 512])
            o2 = ps_s[:, 0:NB * D].rearrange("p (k f) -> p k f", k=NB)
            loads += [(w_sk1[0:D, :], skip[0][0:D, :]), (w_sk1[D:D + 1, :], skip[1].rearrange("(a n) -> a n", a=1)),
                      (w_sk2[:], skip[0][D:2 * D, :])]
        loaded = st.sem("w_loaded", 16 * len(loads))
        made = st.sem("w_made", 1)
        at_loaded = st.slots("at_loaded", 16 * NBLK // 2)
        node_got = st.slots("node_got", 16 * NB * NBLK // 2)
        agg_made = st.slots("agg_made", NBLK // 2)
        names = ["den", "inv", "inv_has", "agg_turned", "agg_copied", "hs_ready", "h_turned", "ht_ready", "mixed", "done"]
        den, inv, inv_has, agg_turned, agg_copied, hs_ready, turned, ht_ready, mixed, done = (
            st.sem(n, NBLK) for n in names)
        if skip:
            h2_made, h2_turned, h2t_ready, skipped = (st.sem(n, NBLK) for n in
                                                      ("h2_made", "h2_turned", "h2t_ready", "skipped"))
        ht_used = skipped if skip else mixed

        with nc.Block() as block:
            @block.sync
            def _(sp):
                for dst_, src_ in loads:
                    sp.dma_start(dst_, src_).then_inc(loaded.h, 16)
                with sp.Fori(0, NBLK // 2) as i:
                    for b in range(2):
                        sp.wait_ge(*node_got[b](i * (16 * NB)))
                        sp.dma_start(at[:, b, :], last_d[:, bass.ds((i * 2 + b) * NB, NB)])\
                            .then_inc(at_loaded[b].h, 16)

            @block.gpsimd
            def _(pool):
                with pool.Fori(0, NBLK // 2) as i:
                    for b in range(2):
                        pool.wait_ge(*at_loaded[b](i * 16 + 16))
                        pool.nop(nofuse=True)
                        pool.wait_ge(*agg_made[b](i))
                        pool.nop(nofuse=True)
                        for k in range(NB):
                            nc.gpsimd.indirect_dma_start(got[:, b, k, :], None, rows, indexed(at[:, b, k:k + 1]))\
                                .then_inc(node_got[b].h, 16)

            @block.vector
            def _(v):
                v.memset(ht[D:D + 1], 1.0).then_inc(made.h, 1)
                with v.Fori(0, NBLK // 2) as i:
                    for b in range(2):
                        g = i * 2 + b
                        cols = bass.ds(g * NB, NB)
                        v.wait_ge(*node_got[b](i * (16 * NB) + 16 * NB))
                        v.tensor_scalar(rd[:], got[:, b, :, YT - 1], TINY, None, ALU.max).then_inc(den.h, 1)
                        v.wait_ge(*den(g + 1))
                        v.reciprocal(rd[:], rd[:]).then_inc(inv.h, 1)
                        v.wait_ge(*inv(g + 1))
                        v.tensor_tensor(rd[:], rd[:], has[:, cols], ALU.mult).then_inc(inv_has.h, 1)
                        v.wait_ge(*inv_has(g + 1))
                        v.wait_ge(*agg_turned(g))
                        v.tensor_tensor(agg[:], got[:, b, :, 0:YT], rd[:].unsqueeze(2).to_broadcast([P, NB, YT]),
                                        ALU.mult).then_inc(agg_made[b].h, 1)
                        v.wait_ge(*agg_turned(g + 1))
                        v.wait_ge(*mixed(g))
                        v.tensor_copy(at_[:], ps_a[0:YT, 0:NB, :]).then_inc(agg_copied.h, 1)
                        v.wait_ge(*mixed(g + 1))
                        if not skip:
                            v.tensor_scalar(h[:, cols, :], o, 0.0, None, ALU.max).then_inc(done.h, 1)
                        else:
                            v.wait_ge(*h2_turned(g))
                            v.tensor_scalar(h2[:], o, 0.0, None, ALU.max).then_inc(h2_made.h, 1)
                            v.wait_ge(*skipped(g + 1))
                            v.scalar_tensor_tensor(out=x[:, cols, :], in0=o2, scalar=0.0, in1=x[:, cols, :],
                                                   op0=ALU.max, op1=ALU.add).then_inc(done.h, 1)

            @block.scalar
            def _(act):
                with act.Fori(0, NBLK // 2) as i:
                    for b in range(2):
                        g = i * 2 + b
                        act.wait_ge(*turned(g))
                        act.activation(hs[:], h[:, bass.ds(g * NB, NB), :], ACT.Copy).then_inc(hs_ready.h, 1)
                        act.wait_ge(*turned(g + 1))
                        act.wait_ge(*ht_used(g))
                        act.activation(ht[0:D], ps_h[0:D, 0:NB, :], ACT.Copy).then_inc(ht_ready.h, 1)
                        if skip:
                            act.wait_ge(*h2_turned(g + 1))
                            act.wait_ge(*skipped(g))
                            act.activation(h2t[:], ps_a[0:D, 0:NB, :], ACT.Copy).then_inc(h2t_ready.h, 1)

            @block.tensor
            def _(pe):
                def need(signal, n):
                    pe.wait_ge(*signal(n))
                    pe.nop(nofuse=True)

                pe.wait_ge(*loaded(16 * len(loads)))
                pe.wait_ge(*made(1))
                with pe.Fori(0, NBLK // 2) as i:
                    for b in range(2):
                        g = i * 2 + b
                        need(hs_ready, g + 1)
                        need(ht_ready, g)
                        for k in range(NB):
                            last = nc.tensor.transpose(ps_h[0:D, k, :], hs[:, k, :], ident[:])
                        last.then_inc(turned.h, 1)
                        need(agg_made[b], i + 1)
                        need(h2t_ready if skip else agg_copied, g)
                        for k in range(NB):
                            last = nc.tensor.transpose(ps_a[0:YT, k, :], agg[:, k, :], ident[:])
                        last.then_inc(agg_turned.h, 1)
                        need(agg_copied, g + 1)
                        need(ht_ready, g + 1)
                        need(h2_made if skip else done, g)
                        for k in range(NB):
                            nc.tensor.matmul(o[:, k, :], at_[:, k, :], w_agg[:], start=True, stop=False)
                            last = nc.tensor.matmul(o[:, k, :], ht[:, k, :], w_self[:], start=False, stop=True)
                        last.then_inc(mixed.h, 1)
                        if skip:
                            need(h2_made, g + 1)
                            for k in range(NB):
                                last = nc.tensor.transpose(ps_a[0:D, k, :], h2[:, k, :], ident[:])
                            last.then_inc(h2_turned.h, 1)
                            need(h2t_ready, g + 1)
                            need(done, g)
                            for k in range(NB):
                                nc.tensor.matmul(o2[:, k, :], ht[:, k, :], w_sk1[:], start=True, stop=False)
                                last = nc.tensor.matmul(o2[:, k, :], h2t[:, k, :], w_sk2[:], start=False, stop=True)
                            last.then_inc(skipped.h, 1)
        st.close()

    def prepare_gat(tag, gt, w, a_src, a_dst, heads, edge=None):
        st = Stage(nc, tag, signals)
        wg = st.sb("wg", [D, TG])
        av = st.sb("av", [D, 2, D])
        pr = st.sb("pr", [D, 2, D])
        hs, ht = st.sb("hs", [P, NB, D]), st.sb("ht", [D, NB, P])
        adq = st.sb("adq", [P, 2, NB, HG])
        at = st.sb("at", [P, 2, NB], I32)
        ps_h, ps_q = st.ps("ps_h", [P, 8, P]), st.ps("ps_q", [P, 8, P])
        width = D // heads
        loads = [(wg[:, 0:D], w), (av[:, 0, :], row_of(a_src, D, D)), (av[:, 1, :], row_of(a_dst, D, D))]
        if edge:
            bd, w_e, a_e = edge
            wev, aev = st.sb("wev", [P, D]), st.sb("aev", [P, D])
            m8 = st.sb("m8", [P, HG])
            loads += [(wev[8 * k:8 * k + 8, :], w_e) for k in range(G)] + [(aev[:], row_of(a_e, D))]
        steps = "prod sum" + (" eprod esum spread" if edge else "")
        loaded = st.sem("w_loaded", 16 * len(loads))
        ch = st.chain("gat_steps", steps)
        diag = st.sem("diag", 1)
        at_loaded = st.slots("at_loaded", 16 * NBLK // 2)
        scattered = st.slots("scattered", 16 * NB * NBLK // 2)
        q_stored = st.slots("q_stored", 16 * NBLK // 2)
        hs_ready, turned, ht_ready = (st.sem(n, NBLK) for n in ("hs_ready", "h_turned", "ht_ready"))
        mixed = st.sem("mixed", NBLK)
        q_ready = st.slots("q_ready", NBLK // 2)

        with nc.Block() as block:
            @block.sync
            def _(sp):
                for dst_, src_ in loads:
                    sp.dma_start(dst_, src_).then_inc(loaded.h, 16)
                with sp.Fori(0, NBLK // 2) as i:
                    for b in range(2):
                        c0 = (i * 2 + b) * NB
                        sp.wait_ge(*scattered[b](i * (16 * NB)))
                        sp.dma_start(at[:, b, :], start_d[:, bass.ds(c0, NB)]).then_inc(at_loaded[b].h, 16)
                        sp.wait_ge(*q_ready[b](i + 1))
                        sp.dma_start(by_node(g_tab)[:, bass.ds(c0, NB), :], gt[:, bass.ds(c0, NB), :])\
                            .then_inc(q_stored[b].h, 16)
                for b in range(2):
                    sp.wait_ge(*q_stored[b](16 * NBLK // 2))
                    sp.wait_ge(*scattered[b](16 * NB * NBLK // 2))

            @block.gpsimd
            def _(pool):
                with pool.Fori(0, NBLK // 2) as i:
                    for b in range(2):
                        pool.wait_ge(*at_loaded[b](i * 16 + 16))
                        pool.nop(nofuse=True)
                        pool.wait_ge(*q_ready[b](i + 1))
                        pool.nop(nofuse=True)
                        for k in range(NB):
                            nc.gpsimd.indirect_dma_start(ad_start, indexed(at[:, b, k:k + 1]), adq[:, b, k, :],
                                                         None).then_inc(scattered[b].h, 16)

            @block.scalar
            def _(act):
                with act.Fori(0, NBLK // 2) as i:
                    for b in range(2):
                        g = i * 2 + b
                        act.wait_ge(*turned(g))
                        act.activation(hs[:], h[:, bass.ds(g * NB, NB), :], ACT.Copy).then_inc(hs_ready.h, 1)
                        act.wait_ge(*mixed(g + 1))
                        act.wait_ge(*scattered[b](i * (16 * NB)))
                        act.activation(gt[:, bass.ds(g * NB, NB), :], ps_q[:, 0:NB, 0:TG], ACT.Copy)
                        act.activation(adq[:, b], ps_q[:, 0:NB, D + HG:TG], ACT.Copy).then_inc(q_ready[b].h, 1)

            @block.vector
            def _(v):
                v.wait_ge(*loaded(16 * len(loads)))
                v.tensor_tensor(pr[:], wg[:, 0:D].unsqueeze(1).to_broadcast([D, 2, D]), av[:], ALU.mult)\
                    .then_inc(ch.h, 1)
                v.wait_ge(*ch.before("sum"))
                if heads == HG:
                    v.reduce_sum(wg[:, D:TG], pr[:].rearrange("p s (h j) -> p (s h) j", h=HG), axis=AX.X)\
                        .then_inc(ch.h, 1)
                else:
                    for k in range(HG):
                        last = v.reduce_sum(wg[:, D + k:TG:HG], pr[:], axis=AX.X)
                    last.then_inc(ch.h, 1)
                if edge:
                    v.wait_ge(*ch.before("eprod"))
                    v.tensor_tensor(wev[:], wev[:], aev[:], ALU.mult).then_inc(ch.h, 1)
                    v.wait_ge(*ch.before("esum"))
                    v.reduce_sum(m8[:], wev[:].rearrange("p (h j) -> p h j", h=HG), axis=AX.X).then_inc(ch.h, 1)
                    v.wait_ge(*ch.before("spread"))
                    v.tensor_copy(bd[:].rearrange("p (h t) -> p h t", h=HG),
                                  m8[:].unsqueeze(2).to_broadcast([P, HG, G])).then_inc(ch.h, 1)
                with v.Fori(0, NBLK // 2) as i:
                    for b in range(2):
                        g = i * 2 + b
                        v.wait_ge(*turned(g + 1))
                        v.wait_ge(*mixed(g))
                        v.tensor_copy(ht[:], ps_h[0:D, 0:NB, :]).then_inc(ht_ready.h, 1)

            @block.tensor
            def _(pe):
                pe.wait_ge(*ch.upto(len(ch)))
                with pe.Fori(0, NBLK // 2) as i:
                    for b in range(2):
                        g = i * 2 + b
                        pe.wait_ge(*hs_ready(g + 1))
                        pe.nop(nofuse=True)
                        pe.wait_ge(*ht_ready(g))
                        pe.nop(nofuse=True)
                        for k in range(NB):
                            last = nc.tensor.transpose(ps_h[0:D, k, :], hs[:, k, :], ident[:])
                        last.then_inc(turned.h, 1)
                        pe.wait_ge(*ht_ready(g + 1))
                        pe.nop(nofuse=True)
                        if b == 0:
                            pe.wait_ge(*q_ready[1](i))
                        else:
                            pe.wait_ge(*q_ready[0](i + 1))
                        pe.nop(nofuse=True)
                        for k in range(NB):
                            last = nc.tensor.matmul(ps_q[:, k, 0:TG], ht[:, k, :], wg[:], start=True, stop=True)
                        last.then_inc(mixed.h, 1)
        st.close()

    def block_diagonal(tag, bd):
        st = Stage(nc, tag, signals)
        cut = st.sem("cut", 2)
        v3 = bd[:].rearrange("p (h t) -> p h t", h=HG)
        with nc.Block() as block:
            @block.gpsimd
            def _(pool):
                nc.gpsimd.affine_select(out=v3, in_=v3, compare_op=ALU.is_ge, fill=0.0, base=0,
                                        pattern=[[0, HG], [-8, G]], channel_multiplier=1).then_inc(cut.h, 1)
                pool.wait_ge(*cut(1))
                nc.gpsimd.affine_select(out=v3, in_=v3, compare_op=ALU.is_ge, fill=0.0, base=7,
                                        pattern=[[0, HG], [8, G]], channel_multiplier=-1).then_inc(cut.h, 1)
                pool.wait_ge(*cut(2))
        st.close()

    def gat_edges(tag, rows, bd=None):
        H, J1 = HG, JG + 1
        F = H * J1
        st = Stage(nc, tag, signals)
        at = st.sb("at", [P, 2, G], I32)
        y = st.sb("y", [P, 2, G, TG])
        ad_raw, ad = st.sb("ad_raw", [P, ET, H]), st.sb("ad", [P, H, ET])
        s0, s, fm = st.sb("s0", [P, H, G]), st.sb("s", [P, H, G]), st.sb("fm", [P, 2, H, G + 1])
        de, ex = st.sb("de", [P, 2, H, G]), st.sb("ex", [P, 2, H, G])
        r, w_in = st.sb("r", [P, H, J1, G + 1]), st.sb("w_in", [P, H, J1, G + 1])
        acc = st.sb("acc", [P, 2, F, G + 1])
        row = st.sb("row", [P, 2, G, TG])
        g0 = st.sb("g0", [P, TG])
        half = NG // 2
        if bd is not None:
            ea = st.sb("ea", [P, 2, P])
            ps_e = [st.ps(f"ps_e{b}", [P, 512]) for b in range(2)]
        ready = st.sem("edges_ready", 3)
        g0_got, ad_loaded = st.sem("q0_got", 16), st.sem("ad_loaded", 16)
        ad_filled = st.sem("ad_filled", H)
        at_loaded = st.slots("at_loaded", 16 * half)
        if bd is not None:
            e_loaded, e_scored = st.slots("e_loaded", 16 * half), st.slots("e_scored", half)
            eadded = st.sem("eadded", NG)
        gathered = st.slots(f"gathered_{tag}_", 16 * G * half)
        weighted, row_ready, den_in = (st.slots(n, half) for n in ("weighted", "row_ready", "den_in"))
        row_stored = st.slots("row_stored", 16 * half)
        added, scored = (st.sem(n, NG) for n in ("added", "scored"))
        maxed, m_carried, shifted, exps, r_ready = (st.sem(n, NG) for n in
                                                    ("maxed", "m_carried", "shifted", "exps", "r_ready"))
        summed, carried = (st.sem(n, NG) for n in ("summed", "carried"))
        differed = st.sem("differed", NG)

        with nc.Block() as block:
            @block.sync
            def _(sp):
                sp.dma_start(ad_raw[:], by_edge(ad_start)).then_inc(ad_loaded.h, 16)
                with sp.Fori(0, half) as i:
                    for b in range(2):
                        g = i * 2 + b
                        sp.wait_ge(*gathered[b](i * (16 * G)))
                        sp.dma_start(at[:, b], a["src"].rearrange("(p t) -> p t", p=P)[:, bass.ds(g * G, G)])\
                            .then_inc(at_loaded[b].h, 16)
                        if bd is not None:
                            sp.wait_ge(*e_scored[b](i))
                            sp.dma_start(ea[:, b, :], a["edge_attr_8"][bass.ds(g * P, P), :])\
                                .then_inc(e_loaded[b].h, 16)

            @block.gpsimd
            def _(pool):
                nc.gpsimd.indirect_dma_start(g0[:], None, g_tab, indexed(dst0[:])).then_inc(g0_got.h, 16)
                with pool.Fori(0, half) as i:
                    for b in range(2):
                        pool.wait_ge(*at_loaded[b](i * 16 + 16))
                        pool.nop(nofuse=True)
                        pool.wait_ge(*weighted[b](i))
                        pool.nop(nofuse=True)
                        for k in range(G):
                            nc.gpsimd.indirect_dma_start(y[:, b, k, :], None, g_tab, indexed(at[:, b, k:k + 1]))\
                                .then_inc(gathered[b].h, 16)

            if bd is not None:
                @block.tensor
                def _(pe):
                    with pe.Fori(0, half) as i:
                        for b in range(2):
                            pe.wait_ge(*weighted[b](i))
                            pe.nop(nofuse=True)
                            pe.wait_ge(*e_loaded[b](i * 16 + 16))
                            pe.nop(nofuse=True)
                            nc.tensor.matmul(ps_e[b][:, 0:H * G], ea[:, b, :], bd[:], start=True,
                                             stop=True).then_inc(e_scored[b].h, 1)

            @block.vector
            def _(v):
                v.memset(r[:, :, :, 0:1], 0.0).then_inc(ready.h, 1)
                v.memset(w_in[:, :, :, 0:1], 0.0).then_inc(ready.h, 1)
                v.memset(fm[:, 0, :, 0:1], -BIG).then_inc(ready.h, 1)
                v.wait_ge(*g0_got(16))
                v.wait_ge(*ad_loaded(16))
                for k in range(H):
                    v.tensor_tensor_scan(ad[:, k, :], same[:], ad_raw[:, :, k], g0[:, D + H + k:D + H + k + 1],
                                         ALU.mult, ALU.add).then_inc(ad_filled.h, 1)
                v.wait_ge(*ad_filled(H))
                v.wait_ge(*ready(3))
                with v.Fori(0, half) as i:
                    for b in range(2):
                        g = i * 2 + b
                        cols = bass.ds(g * G, G)
                        v.wait_ge(*gathered[b](i * (16 * G) + 16 * G))
                        v.tensor_tensor(s0[:], y[:, b, :, D:D + H].rearrange("p t h -> p h t"), ad[:, :, cols],
                                        ALU.add).then_inc(added.h, 1)
                        v.wait_ge(*added(g + 1))
                        if bd is not None:
                            v.wait_ge(*e_scored[b](i + 1))
                            v.tensor_tensor(s0[:], s0[:], ps_e[b][:, 0:H * G].rearrange("p (h t) -> p h t", h=H),
                                            ALU.add).then_inc(eadded.h, 1)
                            v.wait_ge(*eadded(g + 1))
                        v.scalar_tensor_tensor(out=s[:], in0=s0[:], scalar=SLOPE, in1=s0[:], op0=ALU.mult,
                                               op1=ALU.max).then_inc(scored.h, 1)
                        v.wait_ge(*scored(g + 1))
                        v.wait_ge(*m_carried(g))
                        for k in range(H):
                            last = v.tensor_tensor_scan(fm[:, b, k, 1:G + 1], pen[:, cols], s[:, k, :],
                                                        fm[:, b, k, 0:1], ALU.add, ALU.max)
                        last.then_inc(maxed.h, 1)
                        v.wait_ge(*maxed(g + 1))
                        if b == 0:
                            v.wait_ge(*row_ready[1](i))
                        else:
                            v.wait_ge(*row_ready[0](i + 1))
                        v.tensor_copy(fm[:, 1 - b, :, 0:1], fm[:, b, :, G:G + 1]).then_inc(m_carried.h, 1)
                        v.tensor_tensor(de[:, 0], fm[:, b, :, 0:G], fm[:, b, :, 1:G + 1], ALU.subtract)\
                            .then_inc(differed.h, 1)
                        v.tensor_tensor(de[:, 1], s[:], fm[:, b, :, 1:G + 1], ALU.subtract)
                        v.wait_ge(*differed(g + 1))
                        v.tensor_tensor(de[:, 0], de[:, 0], pen[:, cols].unsqueeze(1).to_broadcast([P, H, G]),
                                        ALU.add).then_inc(shifted.h, 1)
                        v.wait_ge(*exps(g + 1))
                        v.wait_ge(*carried(g))
                        v.tensor_copy(w_in[:, :, JG, 1:G + 1], ex[:, 1]).then_inc(den_in[b].h, 1)
                        for k in range(H):
                            last = v.tensor_tensor(w_in[:, k, 0:JG, 1:G + 1],
                                                   y[:, b, :, JG * k:JG * (k + 1)].rearrange("p t j -> p j t"),
                                                   ex[:, 1, k, :].unsqueeze(1).to_broadcast([P, JG, G]), ALU.mult)
                        last.then_inc(weighted[b].h, 1)
                        v.wait_ge(*weighted[b](i + 1))
                        v.wait_ge(*r_ready(g + 1))
                        v.wait_ge(*row_ready[b](i))
                        v.tensor_tensor_scan(acc[:, b].rearrange("p f t -> p (f t)"),
                                             r[:].rearrange("p h j t -> p (h j t)"),
                                             w_in[:].rearrange("p h j t -> p (h j t)"), 0.0,
                                             ALU.mult, ALU.add).then_inc(summed.h, 1)
                        v.wait_ge(*summed(g + 1))
                        v.tensor_copy(w_in[:].rearrange("p h j t -> p (h j) t")[:, :, 0:1], acc[:, b, :, G:G + 1])\
                            .then_inc(carried.h, 1)
                v.wait_ge(*carried(NG))
                v.tensor_copy(carry_v[:, 0:F], w_in[:].rearrange("p h j t -> p (h j) t")[:, :, 0])
                v.tensor_copy(carry_m[:], fm[:, 0, :, 0])

            @block.scalar
            def _(act):
                def weights(i, b):
                    g = i * 2 + b
                    act.wait_ge(*shifted(g + 1))
                    if b == 1:
                        act.wait_ge(*weighted[0](i + 1))
                    else:
                        act.wait_ge(*weighted[1](i))
                    act.activation(ex[:], de[:], ACT.Exp).then_inc(exps.h, 1)
                    act.wait_ge(*exps(g + 1))
                    act.wait_ge(*summed(g))
                    act.activation(r[:, :, :, 1:G + 1], ex[:, 0].unsqueeze(2).to_broadcast([P, H, J1, G]), ACT.Copy)\
                        .then_inc(r_ready.h, 1)

                def send(i, b):
                    g = i * 2 + b
                    act.wait_ge(*summed(g + 1))
                    act.wait_ge(*row_stored[b](i * 16))
                    act.activation(row[:, b, :, F:F + H], fm[:, b, :, 1:G + 1].rearrange("p h t -> p t h"), ACT.Copy)
                    act.activation(row[:, b, :, 0:F], acc[:, b, :, 1:G + 1].rearrange("p f t -> p t f"), ACT.Copy)\
                        .then_inc(row_ready[b].h, 1)
                    act.wait_ge(*row_ready[b](i + 1))
                    act.dma_start(by_edge(rows)[:, bass.ds(g * G, G), :], row[:, b]).then_inc(row_stored[b].h, 16)

                with act.Fori(0, half) as i:
                    for b in range(2):
                        weights(i, b)
                        send(i, b)
                for b in range(2):
                    act.wait_ge(*row_stored[b](16 * half))
        st.close()

    def finish_gat(tag, rows, bias, gt=None, last=False):
        J1 = JG + 1
        st = Stage(nc, tag, signals)
        at = st.sb("at", [P, 2, NB], I32)
        got = st.sb("got", [P, 2, NB, TG])
        bv = st.sb("bv", [P, D])
        e, m = st.sb("e", [P, NB, HG]), st.sb("m", [P, NB, HG])
        de, ex = st.sb("de", [P, 2, NB, HG]), st.sb("ex", [P, 2, NB, HG])
        den, rd = st.sb("den", [P, NB, HG]), st.sb("rd", [P, NB, HG])
        o, own = st.sb("o", [P, NB, D]), st.sb("own", [P, NB, D])
        nrm = st.sb("nrm", [P, NB])
        if gt is None:
            names = "den inv inv_has mean bias done"
        else:
            names = "e leak m1 m2 mx d1 d2 exp den1 den2 eps inv accw own sum mean bias "
            names += "sq ssum root nmax ninv scaled done" if last else "neg elu_exp less1 done"
        names = names.split()
        steps = st.sem("node_steps", len(names) * NBLK)
        loaded = st.sem("w_loaded", 16)
        at_loaded = st.slots("at_loaded", 16 * NBLK // 2)
        node_got = st.slots("node_got", 16 * NB * NBLK // 2)
        used = st.slots("node_used", NBLK // 2)

        def before(g, name):
            return steps(g * len(names) + names.index(name))

        def wide(t):
            return t.unsqueeze(3).to_broadcast([P, NB, HG, JG])

        def split(t):
            return t.rearrange("p k (h j) -> p k h j", h=HG)

        with nc.Block() as block:
            @block.sync
            def _(sp):
                sp.dma_start(bv[:], row_of(bias, D)).then_inc(loaded.h, 16)
                with sp.Fori(0, NBLK // 2) as i:
                    for b in range(2):
                        sp.wait_ge(*node_got[b](i * (16 * NB)))
                        sp.dma_start(at[:, b, :], last_d[:, bass.ds((i * 2 + b) * NB, NB)])\
                            .then_inc(at_loaded[b].h, 16)

            @block.gpsimd
            def _(pool):
                with pool.Fori(0, NBLK // 2) as i:
                    for b in range(2):
                        pool.wait_ge(*at_loaded[b](i * 16 + 16))
                        pool.nop(nofuse=True)
                        pool.wait_ge(*used[b](i))
                        pool.nop(nofuse=True)
                        for k in range(NB):
                            nc.gpsimd.indirect_dma_start(got[:, b, k, :], None, rows, indexed(at[:, b, k:k + 1]))\
                                .then_inc(node_got[b].h, 16)

            if gt is not None:
                @block.scalar
                def _(act):
                    with act.Fori(0, NBLK // 2) as i:
                        for b in range(2):
                            g = i * 2 + b
                            act.wait_ge(*before(g, "exp"))
                            act.activation(ex[:], de[:], ACT.Exp).then_inc(steps.h, 1)
                            if last:
                                act.wait_ge(*before(g, "root"))
                                act.activation(nrm[:], nrm[:], ACT.Sqrt).then_inc(steps.h, 1)
                            else:
                                act.wait_ge(*before(g, "elu_exp"))
                                act.activation(own[:], own[:], ACT.Exp).then_inc(steps.h, 1)

            @block.vector
            def _(v):
                v.wait_ge(*loaded(16))
                with v.Fori(0, NBLK // 2) as i:
                    for b in range(2):
                        g = i * 2 + b
                        cols = bass.ds(g * NB, NB)


                        body = got[:, b, :, 0:HG * J1].rearrange("p k (h j) -> p k h j", h=HG)
                        acc, dn, mx = body[:, :, :, 0:JG], body[:, :, :, JG], got[:, b, :, HG * J1:TG]
                        has_w = has[:, cols].unsqueeze(2).to_broadcast([P, NB, HG])
                        v.wait_ge(*node_got[b](i * (16 * NB) + 16 * NB))
                        if gt is None:
                            v.wait_ge(*before(g, "den"))
                            v.tensor_scalar(rd[:], dn, TINY, None, ALU.max).then_inc(steps.h, 1)
                            v.wait_ge(*before(g, "inv"))
                            v.reciprocal(rd[:], rd[:]).then_inc(steps.h, 1)
                            v.wait_ge(*before(g, "inv_has"))
                            v.tensor_tensor(rd[:], rd[:], has_w, ALU.mult).then_inc(steps.h, 1)
                            v.wait_ge(*before(g, "mean"))
                            v.tensor_tensor(split(o[:]), acc, wide(rd[:]), ALU.mult).then_inc(steps.h, 1)
                        else:
                            own_h, own_s, own_t = (gt[:, cols, 0:D], gt[:, cols, D:D + HG], gt[:, cols, D + HG:TG])
                            hneg_w = hneg[:, cols].unsqueeze(2).to_broadcast([P, NB, HG])
                            v.wait_ge(*before(g, "e"))
                            v.tensor_tensor(e[:], own_s, own_t, ALU.add).then_inc(steps.h, 1)
                            v.wait_ge(*before(g, "leak"))
                            v.scalar_tensor_tensor(out=e[:], in0=e[:], scalar=SLOPE, in1=e[:],
                                                   op0=ALU.mult, op1=ALU.max).then_inc(steps.h, 1)
                            v.wait_ge(*before(g, "m1"))
                            v.tensor_tensor(m[:], mx, has_w, ALU.mult).then_inc(steps.h, 1)
                            v.wait_ge(*before(g, "m2"))
                            v.tensor_tensor(m[:], m[:], hneg_w, ALU.add).then_inc(steps.h, 1)
                            v.wait_ge(*before(g, "mx"))
                            v.tensor_tensor(rd[:], m[:], e[:], ALU.max).then_inc(steps.h, 1)
                            v.wait_ge(*before(g, "d1"))
                            v.tensor_tensor(de[:, 0], m[:], rd[:], ALU.subtract).then_inc(steps.h, 1)
                            v.wait_ge(*before(g, "d2"))
                            v.tensor_tensor(de[:, 1], e[:], rd[:], ALU.subtract).then_inc(steps.h, 1)
                            v.wait_ge(*before(g, "den1"))
                            v.tensor_tensor(den[:], dn, ex[:, 0], ALU.mult).then_inc(steps.h, 1)
                            v.wait_ge(*before(g, "den2"))
                            v.tensor_tensor(den[:], den[:], ex[:, 1], ALU.add).then_inc(steps.h, 1)
                            v.wait_ge(*before(g, "eps"))
                            v.tensor_scalar(den[:], den[:], 1e-16, None, ALU.add).then_inc(steps.h, 1)
                            v.wait_ge(*before(g, "inv"))
                            v.reciprocal(rd[:], den[:]).then_inc(steps.h, 1)
                            v.wait_ge(*before(g, "accw"))
                            v.tensor_tensor(split(o[:]), acc, wide(ex[:, 0]), ALU.mult).then_inc(steps.h, 1)
                            v.wait_ge(*before(g, "own"))
                            v.tensor_tensor(split(own[:]), split(own_h), wide(ex[:, 1]), ALU.mult).then_inc(steps.h, 1)
                            v.wait_ge(*before(g, "sum"))
                            v.tensor_tensor(o[:], o[:], own[:], ALU.add).then_inc(steps.h, 1)
                            v.wait_ge(*before(g, "mean"))
                            v.tensor_tensor(split(o[:]), split(o[:]), wide(rd[:]), ALU.mult).then_inc(steps.h, 1)
                        v.wait_ge(*before(g, "bias"))
                        v.tensor_tensor(o[:], o[:], bv[:].unsqueeze(1).to_broadcast([P, NB, D]), ALU.add)\
                            .then_inc(steps.h, 1)
                        if gt is None:
                            v.wait_ge(*before(g, "done"))
                            v.tensor_tensor(x[:, cols, :], x[:, cols, :], o[:], ALU.add).then_inc(steps.h, 1)
                        elif last:
                            v.wait_ge(*before(g, "sq"))
                            v.tensor_tensor(own[:], o[:], o[:], ALU.mult).then_inc(steps.h, 1)
                            v.wait_ge(*before(g, "ssum"))
                            v.reduce_sum(nrm[:], own[:], axis=AX.X).then_inc(steps.h, 1)
                            v.wait_ge(*before(g, "nmax"))
                            v.tensor_scalar(nrm[:], nrm[:], 1e-12, None, ALU.max).then_inc(steps.h, 1)
                            v.wait_ge(*before(g, "ninv"))
                            v.reciprocal(nrm[:], nrm[:]).then_inc(steps.h, 1)
                            v.wait_ge(*before(g, "scaled"))
                            v.tensor_tensor(o[:], o[:],
                                            nrm[:].unsqueeze(2).to_broadcast([P, NB, D]), ALU.mult)\
                                .then_inc(steps.h, 1)
                            v.wait_ge(*before(g, "done"))
                            v.tensor_tensor(x[:, cols, :], x[:, cols, :], o[:], ALU.add).then_inc(steps.h, 1)
                        else:
                            v.wait_ge(*before(g, "neg"))
                            v.tensor_scalar(own[:], o[:], 0.0, None, ALU.min).then_inc(steps.h, 1)
                            v.wait_ge(*before(g, "less1"))
                            v.tensor_scalar(own[:], own[:], -1.0, None, ALU.add).then_inc(steps.h, 1)
                            v.wait_ge(*before(g, "done"))
                            v.scalar_tensor_tensor(out=h[:, cols, :], in0=o[:], scalar=0.0,
                                                   in1=own[:], op0=ALU.max, op1=ALU.add).then_inc(steps.h, 1)
                        v.wait_ge(*steps(g * len(names) + len(names)))
                        v.sem_inc(used[b].h, 1)
        st.close()

    def store_table(tag):
        st = Stage(nc, tag, signals)
        tab = st.sem("tab_stored", 16)
        with nc.Block() as block:
            @block.sync
            def _(sp):
                sp.dma_start(by_node(h_tab), h[:]).then_inc(tab.h, 16)
                sp.wait_ge(*tab(16))
        st.close()

    def pna_edges(tag, rows):
        F = 2 * D
        st = Stage(nc, tag, signals)
        at = st.sb("at", [P, 2, G], I32)
        y, ea = st.sb("y", [P, 2, G, D]), st.sb("ea", [P, 2, G, D])
        mask, penm = st.sb("mask", [P, F, G + 1]), st.sb("penm", [P, F, G + 1])
        su, mu = st.sb("su", [P, F, G + 1]), st.sb("mu", [P, F, G + 1])
        acc_s, acc_m = st.sb("acc_s", [P, F, G + 1]), st.sb("acc_m", [P, F, G + 1])
        row = st.sb("row", [P, 2, G, 2 * F])
        half = NG // 2
        ready = st.sem("edges_ready", 4)
        at_loaded, e_loaded = (st.slots(n, 16 * half) for n in ("at_loaded", "e_loaded"))
        gathered = st.slots(f"gathered_{tag}_", 16 * G * half)
        added = st.slots("u_added", half)
        row_ready, row_stored = st.slots("row_ready", half), st.slots("row_stored", 16 * half)
        masks, squared, copied = (st.sem(n, NG) for n in ("masks", "squared", "u_copied"))
        summed, maxed, s_carried, m_carried = (st.sem(n, NG) for n in
                                               ("summed", "maxed", "carried", "m_carried"))

        with nc.Block() as block:
            @block.sync
            def _(sp):
                with sp.Fori(0, half) as i:
                    for b in range(2):
                        t0 = (i * 2 + b) * G
                        sp.wait_ge(*gathered[b](i * (16 * G)))
                        sp.dma_start(at[:, b], a["src"].rearrange("(p t) -> p t", p=P)[:, bass.ds(t0, G)])\
                            .then_inc(at_loaded[b].h, 16)
                        sp.wait_ge(*added[b](i))
                        sp.dma_start(ea[:, b], a["edge_attr_64"].rearrange("(p t) f -> p t f", p=P)[:, bass.ds(t0, G), :])\
                            .then_inc(e_loaded[b].h, 16)

            @block.gpsimd
            def _(pool):
                with pool.Fori(0, half) as i:
                    for b in range(2):
                        pool.wait_ge(*at_loaded[b](i * 16 + 16))
                        pool.nop(nofuse=True)
                        pool.wait_ge(*added[b](i))
                        pool.nop(nofuse=True)
                        for k in range(G):
                            nc.gpsimd.indirect_dma_start(y[:, b, k, :], None, h_tab, indexed(at[:, b, k:k + 1]))\
                                .then_inc(gathered[b].h, 16)

            @block.vector
            def _(v):
                v.memset(mask[:, :, 0:1], 0.0).then_inc(ready.h, 1)
                v.memset(penm[:, :, 0:1], -BIG).then_inc(ready.h, 1)
                v.memset(su[:, :, 0:1], 0.0).then_inc(ready.h, 1)
                v.memset(mu[:, :, 0:1], -BIG).then_inc(ready.h, 1)
                v.wait_ge(*ready(4))
                with v.Fori(0, half) as i:
                    for b in range(2):
                        g = i * 2 + b
                        v.wait_ge(*gathered[b](i * (16 * G) + 16 * G))
                        v.wait_ge(*e_loaded[b](i * 16 + 16))
                        v.wait_ge(*copied(g))
                        v.tensor_tensor(su[:, 0:D, 1:G + 1], y[:, b].rearrange("p t f -> p f t"),
                                        ea[:, b].rearrange("p t f -> p f t"), ALU.add).then_inc(added[b].h, 1)
                        if b == 0:
                            v.wait_ge(*row_ready[1](i))
                        else:
                            v.wait_ge(*row_ready[0](i + 1))
                        v.wait_ge(*squared(g + 1))
                        v.wait_ge(*s_carried(g))
                        v.tensor_tensor_scan(acc_s[:].rearrange("p f t -> p (f t)"),
                                             mask[:].rearrange("p f t -> p (f t)"),
                                             su[:].rearrange("p f t -> p (f t)"), 0.0,
                                             ALU.mult, ALU.add).then_inc(summed.h, 1)
                        v.wait_ge(*copied(g + 1))
                        v.wait_ge(*m_carried(g))
                        v.tensor_tensor_scan(acc_m[:].rearrange("p f t -> p (f t)"),
                                             penm[:].rearrange("p f t -> p (f t)"),
                                             mu[:].rearrange("p f t -> p (f t)"), 0.0,
                                             ALU.add, ALU.max).then_inc(maxed.h, 1)
                        v.wait_ge(*summed(g + 1))
                        v.tensor_copy(su[:, :, 0:1], acc_s[:, :, G:G + 1]).then_inc(s_carried.h, 1)
                        v.wait_ge(*maxed(g + 1))
                        v.tensor_copy(mu[:, :, 0:1], acc_m[:, :, G:G + 1]).then_inc(m_carried.h, 1)
                v.wait_ge(*s_carried(NG))
                v.wait_ge(*m_carried(NG))
                v.tensor_copy(carry_v[:, 0:F], su[:, :, 0])
                v.tensor_copy(carry_v[:, F:2 * F], mu[:, :, 0])

            @block.scalar
            def _(act):
                def operands(i, b):
                    g = i * 2 + b
                    cols = bass.ds(g * G, G)
                    act.wait_ge(*summed(g))
                    act.wait_ge(*maxed(g))
                    act.activation(mask[:, :, 1:G + 1], same[:, cols].unsqueeze(1).to_broadcast([P, F, G]), ACT.Copy)
                    act.activation(penm[:, :, 1:G + 1], pen[:, cols].unsqueeze(1).to_broadcast([P, F, G]), ACT.Copy)
                    act.wait_ge(*added[b](i + 1))
                    act.activation(su[:, D:F, 1:G + 1], su[:, 0:D, 1:G + 1], ACT.Square).then_inc(squared.h, 1)
                    act.activation(mu[:, 0:D, 1:G + 1], su[:, 0:D, 1:G + 1], ACT.Copy)
                    act.activation(mu[:, D:F, 1:G + 1], su[:, 0:D, 1:G + 1], ACT.Copy, scale=-1.0)\
                        .then_inc(copied.h, 1)

                def send(i, b):
                    g = i * 2 + b
                    act.wait_ge(*summed(g + 1))
                    act.wait_ge(*row_stored[b](i * 16))
                    act.activation(row[:, b, :, 0:F], acc_s[:, :, 1:G + 1].rearrange("p f t -> p t f"), ACT.Copy)
                    act.wait_ge(*maxed(g + 1))
                    act.activation(row[:, b, :, F:2 * F], acc_m[:, :, 1:G + 1].rearrange("p f t -> p t f"), ACT.Copy)\
                        .then_inc(row_ready[b].h, 1)
                    act.wait_ge(*row_ready[b](i + 1))
                    act.dma_start(by_edge(rows)[:, bass.ds(g * G, G), :], row[:, b]).then_inc(row_stored[b].h, 16)

                with act.Fori(0, half) as i:
                    for b in range(2):
                        operands(i, b)
                        send(i, b)
                for b in range(2):
                    act.wait_ge(*row_stored[b](16 * half))
        st.close()

    def join_pna(tag, rows):
        F = 2 * D
        st = Stage(nc, tag, signals)
        got = st.sb("got", [P, 2 * F])
        vt, mt = st.sb("vt", [F, P]), st.sb("mt", [F, P])
        ms, vs_ = st.sb("ms", [F, P + 1]), st.sb("vs", [F, P + 1])
        vin, min_ = st.sb("vin", [P, F]), st.sb("min", [P, F])
        pa, pb = st.ps("pa", [P, 512]), st.ps("pb", [P, 512])
        got_row, put_row = st.sem("fix_got", 16), st.sem("fix_put", 16)
        ch = st.chain("fix_steps", """turn_v turn_m copy_v copy_m edge_m edge_v scan_m scan_v back_v back_m
            vin min sum_new max_new""")

        with nc.Block() as block:
            @block.gpsimd
            def _(pool):
                nc.gpsimd.indirect_dma_start(got[:], None, rows, indexed(fix_at[:])).then_inc(got_row.h, 16)
                pool.wait_ge(*ch.upto(len(ch)))
                nc.gpsimd.indirect_dma_start(rows, indexed(fix_at[:]), got[:], None).then_inc(put_row.h, 16)
                pool.wait_ge(*put_row(16))

            @block.tensor
            def _(pe):
                for name, dst_, src_ in (("turn_v", pa[:, 0:P], carry_v[:, 0:F]), ("turn_m", pb[:, 0:P], carry_v[:, F:2 * F]),
                                         ("back_v", pa[:, 0:F], vs_[:, 0:P]), ("back_m", pb[:, 0:F], ms[:, 0:P])):
                    pe.wait_ge(*ch.before(name))
                    nc.tensor.transpose(dst_, src_, ident[:]).then_inc(ch.h, 1)

            @block.vector
            def _(v):

                v.wait_ge(*ch.before("copy_v"))
                v.tensor_copy(vt[:], pa[:, 0:P]).then_inc(ch.h, 1)
                v.wait_ge(*ch.before("copy_m"))
                v.tensor_copy(mt[:], pb[:, 0:P]).then_inc(ch.h, 1)
                v.wait_ge(*ch.before("edge_m"))
                v.memset(ms[:, 0:1], -BIG).then_inc(ch.h, 1)
                v.wait_ge(*ch.before("edge_v"))
                v.memset(vs_[:, 0:1], 0.0).then_inc(ch.h, 1)
                v.wait_ge(*ch.before("scan_m"))
                v.tensor_tensor_scan(ms[:, 1:P + 1], whole_pen[:], mt[:], -BIG, ALU.add, ALU.max).then_inc(ch.h, 1)
                v.wait_ge(*ch.before("scan_v"))
                v.tensor_tensor_scan(vs_[:, 1:P + 1], whole_t[:], vt[:], 0.0, ALU.mult, ALU.add).then_inc(ch.h, 1)
                v.wait_ge(*ch.before("vin"))
                v.tensor_scalar(vin[:], pa[:, 0:F], cont[:, 0:1], None, ALU.mult).then_inc(ch.h, 1)
                v.wait_ge(*ch.before("min"))
                v.tensor_scalar(min_[:], pb[:, 0:F], contpen[:, 0:1], None, ALU.add).then_inc(ch.h, 1)
                v.wait_ge(*got_row(16))
                v.wait_ge(*ch.before("sum_new"))
                v.tensor_tensor(got[:, 0:F], got[:, 0:F], vin[:], ALU.add).then_inc(ch.h, 1)
                v.wait_ge(*ch.before("max_new"))
                v.tensor_tensor(got[:, F:2 * F], got[:, F:2 * F], min_[:], ALU.max).then_inc(ch.h, 1)
        st.close()

    def finish_pna(tag, rows):
        st = Stage(nc, tag, signals)
        at = st.sb("at", [P, 2, NB], I32)
        got = st.sb("got", [P, 2, NB, 4 * D])
        rdeg, ld, fac = (st.sb(n, [P, NC]) for n in ("rdeg", "ld", "fac"))
        mean, msq, t = (st.sb(n, [P, NB, D]) for n in ("mean", "msq", "t"))
        pre = st.chain("pre_steps", "deg1 rdeg ln none none2 inv amp fac1 fac2 fac3")
        names = "mean msq sq var relu root max min h3 std fac h13".split()
        steps = st.sem("node_steps", len(names) * NBLK)
        at_loaded = st.slots("at_loaded", 16 * NBLK // 2)
        node_got = st.slots("node_got", 16 * NB * NBLK // 2)
        used = st.slots("node_used", NBLK // 2)

        def before(g, name):
            return steps(g * len(names) + names.index(name))

        with nc.Block() as block:
            @block.sync
            def _(sp):
                with sp.Fori(0, NBLK // 2) as i:
                    for b in range(2):
                        sp.wait_ge(*node_got[b](i * (16 * NB)))
                        sp.dma_start(at[:, b, :], last_d[:, bass.ds((i * 2 + b) * NB, NB)])\
                            .then_inc(at_loaded[b].h, 16)

            @block.gpsimd
            def _(pool):
                with pool.Fori(0, NBLK // 2) as i:
                    for b in range(2):
                        pool.wait_ge(*at_loaded[b](i * 16 + 16))
                        pool.nop(nofuse=True)
                        pool.wait_ge(*used[b](i))
                        pool.nop(nofuse=True)
                        for k in range(NB):
                            nc.gpsimd.indirect_dma_start(got[:, b, k, :], None, rows, indexed(at[:, b, k:k + 1]))\
                                .then_inc(node_got[b].h, 16)

            @block.scalar
            def _(act):
                act.wait_ge(*pre.before("ln"))
                act.activation(ld[:], deg[:], ACT.Ln, bias=ones[:, 0:1], scale=1.0).then_inc(pre.h, 1)
                with act.Fori(0, NBLK // 2) as i:
                    for b in range(2):
                        act.wait_ge(*before(i * 2 + b, "root"))
                        act.activation(t[:], t[:], ACT.Sqrt, bias=eps[:]).then_inc(steps.h, 1)

            @block.vector
            def _(v):

                v.wait_ge(*pre.before("deg1"))
                v.tensor_scalar(rdeg[:], deg[:], 1.0, None, ALU.max).then_inc(pre.h, 1)
                v.wait_ge(*pre.before("rdeg"))
                v.reciprocal(rdeg[:], rdeg[:]).then_inc(pre.h, 1)
                v.wait_ge(*pre.before("none"))
                v.tensor_scalar(fac[:], has[:], -1.0, 1.0, ALU.mult, ALU.add).then_inc(pre.h, 1)
                v.wait_ge(*pre.before("none2"))
                v.tensor_tensor(fac[:], fac[:], ld[:], ALU.add).then_inc(pre.h, 1)
                v.wait_ge(*pre.before("inv"))
                v.reciprocal(fac[:], fac[:]).then_inc(pre.h, 1)
                v.wait_ge(*pre.before("amp"))
                v.tensor_scalar(ld[:], ld[:], 1.0 / AVG_D, 1.0, ALU.mult, ALU.add).then_inc(pre.h, 1)
                v.wait_ge(*pre.before("fac1"))
                v.tensor_scalar(fac[:], fac[:], AVG_D, None, ALU.mult).then_inc(pre.h, 1)
                v.wait_ge(*pre.before("fac2"))
                v.tensor_tensor(fac[:], fac[:], ld[:], ALU.add).then_inc(pre.h, 1)
                v.wait_ge(*pre.before("fac3"))
                v.scalar_tensor_tensor(out=fac[:], in0=fac[:], scalar=1.0 / 13.0, in1=has[:],
                                       op0=ALU.mult, op1=ALU.mult).then_inc(pre.h, 1)
                v.wait_ge(*pre.upto(len(pre)))
                with v.Fori(0, NBLK // 2) as i:
                    for b in range(2):
                        g = i * 2 + b
                        cols = bass.ds(g * NB, NB)


                        rd = rdeg[:, cols].unsqueeze(2).to_broadcast([P, NB, D])
                        s_, q_, mx, nmn = (got[:, b, :, D * k:D * (k + 1)] for k in range(4))
                        v.wait_ge(*node_got[b](i * (16 * NB) + 16 * NB))
                        v.wait_ge(*before(g, "mean"))
                        v.tensor_tensor(mean[:], s_, rd, ALU.mult).then_inc(steps.h, 1)
                        v.wait_ge(*before(g, "msq"))
                        v.tensor_tensor(msq[:], q_, rd, ALU.mult).then_inc(steps.h, 1)
                        v.wait_ge(*before(g, "sq"))
                        v.tensor_tensor(t[:], mean[:], mean[:], ALU.mult).then_inc(steps.h, 1)
                        v.wait_ge(*before(g, "var"))
                        v.tensor_tensor(t[:], msq[:], t[:], ALU.subtract).then_inc(steps.h, 1)
                        v.wait_ge(*before(g, "relu"))
                        v.tensor_scalar(t[:], t[:], 0.0, None, ALU.max).then_inc(steps.h, 1)
                        v.wait_ge(*before(g, "max"))
                        v.tensor_tensor(msq[:], mean[:], mx, ALU.add).then_inc(steps.h, 1)
                        v.wait_ge(*before(g, "min"))
                        v.tensor_tensor(msq[:], msq[:], nmn, ALU.subtract).then_inc(steps.h, 1)
                        v.wait_ge(*before(g, "h3"))
                        v.scalar_tensor_tensor(out=msq[:], in0=h[:, cols, :], scalar=3.0, in1=msq[:],
                                               op0=ALU.mult, op1=ALU.add).then_inc(steps.h, 1)
                        v.wait_ge(*before(g, "std"))
                        v.tensor_tensor(msq[:], msq[:], t[:], ALU.add).then_inc(steps.h, 1)
                        v.wait_ge(*before(g, "fac"))
                        v.tensor_tensor(msq[:], msq[:],
                                        fac[:, cols].unsqueeze(2).to_broadcast([P, NB, D]), ALU.mult)\
                            .then_inc(steps.h, 1)
                        v.wait_ge(*before(g, "h13"))
                        v.scalar_tensor_tensor(out=h[:, cols, :], in0=h[:, cols, :], scalar=1.0 / 13.0,
                                               in1=msq[:], op0=ALU.mult, op1=ALU.add).then_inc(steps.h, 1)
                        v.wait_ge(*steps(g * len(names) + len(names)))
                        v.sem_inc(used[b].h, 1)
        st.close()

    def batch_norm(tag):
        st = Stage(nc, tag, signals)
        sq = st.sb("sq", [P, NC, D])
        part, mu, sc = (st.sb(n, [P, D]) for n in ("part", "mu", "sc"))
        gb = st.sb("gb", [P, 2, D])
        ps = st.ps("ps", [P, 512])
        loaded = st.sem("w_loaded", 32)
        stored = st.sem("out_stored", 32)
        ch = st.chain("bn_steps", "cut part sum mu centre cut2 square part2 sum2 var root inv scale mul beta add")

        def wide(t):
            return t.unsqueeze(1).to_broadcast([P, NC, D])

        valid_w = valid[:].unsqueeze(2).to_broadcast([P, NC, D])
        full = N_NODES // NC
        rest = N_NODES - full * NC
        with nc.Block() as block:
            @block.sync
            def _(sp):
                sp.dma_start(gb[:, 0, :], row_of(a["L3_gnn_gamma"], D)).then_inc(loaded.h, 16)
                sp.dma_start(gb[:, 1, :], row_of(a["L3_gnn_beta"], D)).then_inc(loaded.h, 16)
                sp.wait_ge(*ch.upto(len(ch)))
                sp.dma_start(out[0:full * NC, :].rearrange("(p c) f -> p c f", p=full), x[0:full])\
                    .then_inc(stored.h, 16)
                sp.dma_start(out[full * NC:N_NODES, :].rearrange("(p c) f -> p c f", p=1),
                             x[full:full + 1, 0:rest, :]).then_inc(stored.h, 16)
                sp.wait_ge(*stored(32))

            @block.tensor
            def _(pe):
                for name in ("sum", "sum2"):
                    pe.wait_ge(*ch.before(name))
                    nc.tensor.matmul(ps[:, 0:D], ones[:], part[:], start=True, stop=True).then_inc(ch.h, 1)

            @block.scalar
            def _(act):
                act.wait_ge(*ch.before("square"))
                act.activation(sq[:], h[:], ACT.Square).then_inc(ch.h, 1)
                act.wait_ge(*ch.before("root"))
                act.activation(sc[:], sc[:], ACT.Sqrt, bias=eps[:]).then_inc(ch.h, 1)

            @block.vector
            def _(v):

                v.wait_ge(*ch.before("cut"))
                v.tensor_tensor(h[:], h[:], valid_w, ALU.mult).then_inc(ch.h, 1)
                v.wait_ge(*ch.before("part"))
                v.reduce_sum(part[:], h[:].rearrange("p c f -> p f c"), axis=AX.X).then_inc(ch.h, 1)
                v.wait_ge(*ch.before("mu"))
                v.tensor_scalar(mu[:], ps[:, 0:D], 1.0 / N_NODES, None, ALU.mult).then_inc(ch.h, 1)
                v.wait_ge(*ch.before("centre"))
                v.tensor_tensor(h[:], h[:], wide(mu[:]), ALU.subtract).then_inc(ch.h, 1)
                v.wait_ge(*ch.before("cut2"))
                v.tensor_tensor(h[:], h[:], valid_w, ALU.mult).then_inc(ch.h, 1)
                v.wait_ge(*ch.before("part2"))
                v.reduce_sum(part[:], sq[:].rearrange("p c f -> p f c"), axis=AX.X).then_inc(ch.h, 1)
                v.wait_ge(*ch.before("var"))
                v.tensor_scalar(sc[:], ps[:, 0:D], 1.0 / N_NODES, None, ALU.mult).then_inc(ch.h, 1)
                v.wait_ge(*ch.before("inv"))
                v.reciprocal(sc[:], sc[:]).then_inc(ch.h, 1)
                v.wait_ge(*loaded(32))
                v.wait_ge(*ch.before("scale"))
                v.tensor_tensor(sc[:], sc[:], gb[:, 0, :], ALU.mult).then_inc(ch.h, 1)
                v.wait_ge(*ch.before("mul"))
                v.tensor_tensor(h[:], h[:], wide(sc[:]), ALU.mult).then_inc(ch.h, 1)
                v.wait_ge(*ch.before("beta"))
                v.tensor_tensor(h[:], h[:], wide(gb[:, 1, :]), ALU.add).then_inc(ch.h, 1)
                v.wait_ge(*ch.before("add"))
                v.tensor_tensor(x[:], x[:], h[:], ALU.add).then_inc(ch.h, 1)
        st.close()

    setup()
    layer_norm("ln0")
    prepare_conv("p1", a["q1_wt"], a["L0_gnn_q1_b"], a["k1_wt"], a["L0_gnn_k1_b"], a["e1_wt"])
    conv_edges("c1", rows_d[0])
    join_softmax("j1", rows_d[0], 1, YT - 1)
    finish_conv("f1", rows_d[0], a["L0_gnn_v1_w"], a["L0_gnn_v1_b"], a["L0_gnn_e1_w"], a["L0_gnn_s1_w"],
                a["L0_gnn_s1_b"])
    prepare_conv("p2", a["q2_wt"], a["L0_gnn_q2_b"], a["k2_wt"], a["L0_gnn_k2_b"], a["e2_wt"])
    conv_edges("c2", rows_d[1])
    join_softmax("j2", rows_d[1], 1, YT - 1)
    finish_conv("f2", rows_d[1], a["L0_gnn_v2_w"], a["L0_gnn_v2_b"], a["L0_gnn_e2_w"], a["L0_gnn_s2_w"],
                a["L0_gnn_s2_b"], skip=(a["L0_gnn_skip_w"], a["L0_gnn_skip_b"]))

    with ExitStack() as gat:
        gt = gat.enter_context(nc.sbuf_tensor("gt", [P, NC, TG], F32))
        bd = gat.enter_context(nc.sbuf_tensor("bd", [P, HG * G], F32))
        layer_norm("ln1")
        prepare_gat("p3", gt, a["gat_w"], a["L1_gnn_a_s"].rearrange("h o -> (h o)"),
                    a["L1_gnn_a_t"].rearrange("h o -> (h o)"), HG,
                    (bd, a["gat_we"], a["L1_gnn_a_e"].rearrange("h o -> (h o)")))
        block_diagonal("bd", bd)
        gat_edges("c3", rows_d[2], bd)
        join_softmax("j3", rows_d[2], HG, JG)
        finish_gat("f3", rows_d[2], a["L1_gnn_b_GAT"].rearrange("h o -> (h o)"))
        layer_norm("ln2")
        prepare_gat("p4", gt, a["L2_gnn_W1"], a["L2_gnn_a_src1"].rearrange("h o -> (h o)"),
                    a["L2_gnn_a_dst1"].rearrange("h o -> (h o)"), HG)
        gat_edges("c4", rows_d[3])
        join_softmax("j4", rows_d[3], HG, JG)
        finish_gat("f4", rows_d[3], a["L2_gnn_b1"], gt)
        prepare_gat("p5", gt, a["L2_gnn_W2"], a["L2_gnn_a_src2"].rearrange("h o -> (h o)"),
                    a["L2_gnn_a_dst2"].rearrange("h o -> (h o)"), 1)
        gat_edges("c5", rows_d[4])
        join_softmax("j5", rows_d[4], HG, JG)
        finish_gat("f5", rows_d[4], a["L2_gnn_b2"], gt, last=True)

    layer_norm("ln3")
    store_table("t6")
    pna_edges("c6", rows_d[5])
    join_pna("j6", rows_d[5])
    finish_pna("f6", rows_d[5])
    batch_norm("bn")
    root.close()


def kernel(**inputs):
    import concourse.bacc as bacc
    from concourse.bass_utils import run_bass_kernel_spmd

    def pad(v, n, fill=0):
        v = np.asarray(v)
        return np.concatenate([v, np.full((n - v.shape[0],) + v.shape[1:], fill, v.dtype)])

    arrays = {k: np.ascontiguousarray(v) for k, v in inputs.items()}
    arrays["x"] = pad(arrays["x"], NP_)
    arrays["src"] = pad(arrays["src"], EP)
    dst = pad(arrays["dst"], EP, N_NODES)
    arrays["dst"] = np.concatenate([np.full(1, -1, dst.dtype), dst])
    arrays["edge_attr_32"] = pad(arrays["edge_attr_32"], EP)
    arrays["edge_attr_64"] = pad(arrays["edge_attr_64"], EP)
    e8 = pad(arrays["edge_attr_8"], EP).reshape(P, NG, G, 8)
    arrays["edge_attr_8"] = np.ascontiguousarray(e8.transpose(1, 2, 3, 0)).reshape(NG * G * 8, P)
    for n in ("1", "2"):
        for w in ("q", "k", "e"):
            full = arrays[f"L0_gnn_{w}{n}_w"]
            arrays[f"{w}{n}_wt"] = np.ascontiguousarray(full.T)
    arrays["gat_w"] = np.ascontiguousarray(arrays.pop("L1_gnn_W").transpose(1, 0, 2)).reshape(D, D)
    arrays["gat_we"] = np.ascontiguousarray(arrays.pop("L1_gnn_W_e").transpose(1, 0, 2)).reshape(8, D)
    for name in ("L0_gnn_q1_w", "L0_gnn_k1_w", "L0_gnn_q2_w", "L0_gnn_k2_w"):
        arrays.pop(name)

    nc = bacc.Bacc("TRN2", target_bir_lowering=False, num_devices=1)
    aps = {k: nc.dram_tensor(f"in_{k}", v.shape, mybir.dt.from_np(v.dtype), kind="ExternalInput").ap()
           for k, v in arrays.items()}
    out = nc.dram_tensor("out_0", (N_NODES, D), F32, kind="ExternalOutput").ap()
    build(nc, aps, out)
    result = run_bass_kernel_spmd(nc, [{f"in_{k}": v for k, v in arrays.items()}], core_ids=[0])
    return result.results[0]["out_0"]
```

```python
from contextlib import ExitStack

import numpy as np

import concourse.bass as bass
from concourse import mybir

F32 = mybir.dt.float32
I32 = mybir.dt.int32
ALU = mybir.AluOpType
ACT = mybir.ActivationFunctionType
AX = mybir.AxisListType

P = 128
D = 64
N_NODES, N_EDGES = 12500, 200000
NC = 98
NP_ = P * NC
G = 16
NG = 98
ET = G * NG
EP = P * ET
NB = 7
NBLK = NC // NB
NW = 14
NWBLK = NC // NW
DE = 32
YT = D + DE + 1
BIG = 1.0e30
TINY = 1.0e-30
SLOPE = 0.2
AVG_D = float(np.log(17.0))
HG, JG = 4, 16
TG = D + 2 * HG
CH = 256
NCH = EP // CH
NS = 100
SC = 10
assert NP_ >= N_NODES and EP >= N_EDGES and NBLK % 2 == 0 and NG % 2 == 0 \
    and EP % CH == 0 and NS > NC and NS % (2 * SC) == 0


COUNTED = """
    zeroed patterns chunk_counted chunk_less chunk_at placed0 placed1 setup_steps ln_summed ln_scaled ln_centred ln_squared
    ln_var ln_rooted ln_inverted ln_done w_made ones_set hs_ready0 hs_ready1 h_turned0 h_turned1 ht_ready0
    ht_ready1 mixed0 mixed1 q_ready0 q_ready1 edges_ready q_turned0 q_turned1 weighted0 weighted1 row_ready0
    row_ready1 q_filled q_carried multiplied scored maxed m_carried shifted exps r_ready summed carried differed
    fix_steps agg_made0 agg_made1 agg_turned0 agg_turned1 agg_copied0 agg_copied1 done0 done1 den inv inv_has
    h2_made0 h2_made1 h2_turned0 h2_turned1 h2t_ready0 h2t_ready1 skipped0 skipped1 gat_steps diag cut ad_filled
    e_scored0 e_scored1 eadded den_in0 den_in1 added node_steps node_used0 node_used1 u_added0 u_added1 mask_ready0 mask_ready1
    squared u_copied pre_steps bn_steps
""".split()


class Signal:

    def __init__(self, h, base):
        self.h, self.base = h, base

    def __call__(self, n):
        return self.h, n + self.base


def over_wide_blocks(eng, body):
    with eng.Fori(0, NWBLK // 2) as i:
        for b in range(2):
            body(i, b)
    for b in range(NWBLK % 2):
        body(NWBLK // 2, b)


class Chain:

    def __init__(self, signal, names):
        self.upto, self.names = signal, names.split()
        self.h = signal.h

    def before(self, name):
        return self.upto(self.names.index(name))

    def __len__(self):
        return len(self.names)


class Stage:

    def __init__(self, nc, tag, signals):
        self.nc, self.tag, self.signals, self.used = nc, tag, signals, {}
        self.ctx = ExitStack()

    def sb(self, name, shape, dt=F32):
        return self.ctx.enter_context(self.nc.sbuf_tensor(f"{self.tag}_{name}", shape, dt))

    def ps(self, name, shape, dt=F32):
        return self.ctx.enter_context(self.nc.psum_tensor(f"{self.tag}_{name}", shape, dt))

    def sem(self, name, total):
        assert name in COUNTED, name
        self.used[name] = total
        return self.signals[name]

    def dma(self, name, total):
        if name not in self.signals:
            self.signals[name] = Signal(self.nc.alloc_semaphore(name), 0)
        self.used[name] = total
        return self.signals[name]

    def slots(self, name, total):
        return [self.sem(f"{name}{b}", total) for b in range(2)]

    def wide_slots(self, make, name, each):
        return [make(f"{name}{b}", each * ((NWBLK + 1 - b) // 2)) for b in range(2)]

    def dma_slots(self, name, total):
        return [self.dma(f"{name}{b}", total) for b in range(2)]

    def chain(self, name, names):
        c = Chain(self.sem(name, len(names.split())), names)
        return c

    def close(self):
        for name, total in self.used.items():
            self.signals[name].base += total
        self.ctx.close()


def build(nc, a, out):
    root = ExitStack()
    signals = {}

    def keep(name, shape, dt=F32):
        return root.enter_context(nc.sbuf_tensor(name, shape, dt))

    def dram(name, shape, dt=F32):
        return nc.dram_tensor(name, shape, dt, kind="Internal").ap()

    x = keep("x", [P, NC, D])
    h = keep("h", [P, NC, D])
    same = keep("same", [P, ET])
    pen = keep("pen", [P, ET])
    deg = keep("deg", [P, NC])
    has = keep("has", [P, NC])
    hneg = keep("hneg", [P, NC])
    valid = keep("valid", [P, NC])
    dst0 = keep("dst0", [P, 1], I32)
    fix_at = keep("fix_at", [P, 1], I32)
    cont = keep("cont", [P, 1])
    contpen = keep("contpen", [P, 1])
    ident = keep("ident", [P, P])
    ones = keep("ones", [P, P])
    whole_t = keep("whole_t", [P, P])
    whole_pen = keep("whole_pen", [P, P])
    eps = keep("eps", [P, 1])
    carry_v = keep("carry_v", [P, 4 * D])
    carry_m = keep("carry_m", [P, HG])

    h_tab = dram("h_tab", (NP_, D))
    q_tab = dram("q_tab", (NP_, YT))
    g_tab = dram("g_tab", (NP_, TG))
    q_start = dram("q_start", (EP + NP_, YT))
    ad_start = dram("ad_start", (EP + NP_, HG))
    start_d = dram("start_d", (P, NC), I32)
    last_d = dram("last_d", (P, NC), I32)
    rows_d = [dram(f"rows{n}_d", (EP, w)) for n, w in enumerate([YT + 1, YT + 1, TG, TG, TG, 4 * D])]

    def by_edge(t):
        return t[0:EP, :].rearrange("(p t) f -> p t f", p=P)

    def by_node(t):
        return t.rearrange("(p c) f -> p c f", p=P)

    def row_of(v, n, parts=P):
        return v.rearrange("(a n) -> a n", a=1).to_broadcast([parts, n])

    def indexed(ap):
        return bass.IndirectOffsetOnAxis(ap=ap, axis=0)

    def first_counts():
        for name in COUNTED:
            signals[name] = Signal(nc.alloc_semaphore(name), 1)
        with nc.Block() as block:
            @block.sync
            def _(sp):
                for name in COUNTED[0::5]:
                    sp.sem_inc(signals[name].h, 1)

            @block.tensor
            def _(pe):
                for name in COUNTED[1::5]:
                    pe.sem_inc(signals[name].h, 1)

            @block.scalar
            def _(act):
                for name in COUNTED[2::5]:
                    act.sem_inc(signals[name].h, 1)

            @block.vector
            def _(v):
                for name in COUNTED[3::5]:
                    v.sem_inc(signals[name].h, 1)

            @block.gpsimd
            def _(pool):
                for name in COUNTED[4::5]:
                    pool.sem_inc(signals[name].h, 1)

    def setup():
        st = Stage(nc, "setup", signals)
        sb = st.sb
        cur_i, prev_i = sb("cur_i", [P, ET], I32), sb("prev_i", [P, ET], I32)
        cur, prev = sb("cur", [P, ET]), sb("prev", [P, ET])
        row_i, row = sb("row_i", [P, 1], I32), sb("row", [P, 1])
        node_i, node = sb("node_i", [P, NS], I32), sb("node", [P, NS])
        zero = sb("zero", [P, ET // 2 * HG])
        firsts, chunk = sb("firsts", [P, NCH], I32), sb("chunk", [P, 2, SC, CH], I32)
        below, ones_w = sb("below", [P, 2, NCH]), sb("ones_w", [P, NCH])
        below_in = sb("below_in", [P, 2, 2, CH])
        chunk_f, chunk_i = sb("chunk_f", [P, NS]), sb("chunk_i", [P, 2, SC], I32)
        chunks_before, inside = sb("chunks_before", [P, NS]), sb("inside", [P, NS])
        first = sb("first", [P, NS])
        cnt, whole, fixf = (sb(n, [P, 1]) for n in ("cnt", "whole", "fixf"))
        startf, lastf, none_at = sb("startf", [P, NC]), sb("lastf", [P, NC]), sb("none_at", [P, NC])
        start_i, last_i = sb("start_i", [P, NC], I32), sb("last_i", [P, NC], I32)
        wide, none_row = sb("wide", [P, P]), sb("none_row", [1, 2, D])
        turned = st.ps("turned", [P, 512])

        loaded = st.dma("loaded", 4 * 16)
        zeroed = st.sem("zeroed", 3)
        filled = [st.dma(f"zeros_stored{b}", 16 * ((NG // 2 + 1 - b) // 2)) for b in range(2)]
        q_stored, row_stored = st.dma_slots("q_stored", 16), st.dma_slots("row_stored", 16)
        scattered = st.dma_slots("scattered", 16)
        patterns = st.sem("patterns", 6)
        chunk_counted = st.sem("chunk_counted", NS)
        chunk_less, chunk_at = st.sem("chunk_less", NS // SC), st.sem("chunk_at", NS // SC)
        placed = st.slots("placed", NS // 2)
        chunk_got = st.dma_slots("chunk_got", 16 * (NS // 2))
        normed, rooted_part = layer_norm_parts(st)
        vs = st.chain("setup_steps", """cur prev same pen eq cnt cont contpen whole1 whole dst0 row fixf fix_at
            valid none_at wide turned whole_t whole_pen first1 first deg has hneg last lastc lasti none1 none2 start2 starti""")

        with nc.Block() as block:
            @block.sync
            def _(sp):
                sp.dma_start(firsts[:], row_of(a["chunk_firsts"], NCH)).then_inc(loaded.h, 16)
                sp.dma_start(x[:], by_node(a["x"])).then_inc(loaded.h, 16)
                sp.dma_start(cur_i[:], a["dst"][1:EP + 1].rearrange("(p t) -> p t", p=P)).then_inc(loaded.h, 16)
                sp.dma_start(prev_i[:], a["dst"][0:EP].rearrange("(p t) -> p t", p=P)).then_inc(loaded.h, 16)
                sp.wait_ge(*zeroed(1))

                def fill(n, b):
                    sp.dma_start(by_edge(q_start)[:, bass.ds(n * (2 * G), 2 * G), :].rearrange("p t f -> p (t f)"),
                                 zero[:, 0:2 * G * YT]).then_inc(filled[b].h, 16)

                fill(0, 0)
                fill(1, 1)
                with sp.Fori(0, NG // 4 - 1) as i:
                    for b in range(2):
                        sp.wait_ge(*filled[b](i * 16 + 16))
                        fill((i + 1) * 2 + b, b)
                for b in range((NG // 2) % 2):
                    fill(NG // 2 - 1, b)
                sp.dma_start(ad_start[0:EP // 2, :].rearrange("(p t) f -> p (t f)", p=P), zero[:])\
                    .then_inc(q_stored[0].h, 16)
                sp.dma_start(ad_start[EP // 2:EP, :].rearrange("(p t) f -> p (t f)", p=P), zero[:])\
                    .then_inc(q_stored[1].h, 16)
                sp.wait_ge(*q_stored[0](16))
                sp.wait_ge(*q_stored[1](16))
                for b in range(2):
                    sp.wait_ge(*filled[b](16 * ((NG // 2 + 1 - b) // 2)))

            @block.gpsimd
            def _(pool):
                nc.gpsimd.iota(row_i[:], pattern=[[0, 1]], base=0, channel_multiplier=ET).then_inc(patterns.h, 1)
                nc.gpsimd.iota(node_i[:], pattern=[[1, NS]], base=0, channel_multiplier=NC).then_inc(patterns.h, 1)
                nc.gpsimd.memset(ident[:], 0.0).then_inc(patterns.h, 1)
                nc.gpsimd.memset(ones[:], 1.0).then_inc(patterns.h, 1)
                nc.gpsimd.memset(eps[:], 1e-5).then_inc(patterns.h, 1)
                pool.wait_ge(*patterns(5))
                nc.gpsimd.affine_select(out=ident[:], in_=ident[:], compare_op=ALU.not_equal, fill=1.0, base=0,
                                        pattern=[[-1, P]], channel_multiplier=1).then_inc(patterns.h, 1)
                for b in range(2):
                    nc.gpsimd.dma_start(none_row[:, b, :], a["x"][0:1, :]).then_inc(scattered[b].h, 16)
                for b in range(2):
                    pool.wait_ge(*scattered[b](16))
                with pool.Fori(0, NS // SC // 2) as i:
                    for b in range(2):
                        pool.wait_ge(*chunk_at(i * 2 + b + 1))
                        pool.nop(nofuse=True)
                        pool.wait_ge(*placed[b](i * SC))
                        pool.nop(nofuse=True)
                        for k in range(SC):
                            nc.gpsimd.indirect_dma_start(chunk[:, b, k, :], None, a["dst_chunks"],
                                                         indexed(chunk_i[:, b, k:k + 1]))\
                                .then_inc(chunk_got[b].h, 16)

            @block.vector
            def _(v):

                v.memset(zero[:], 0.0).then_inc(zeroed.h, 1)
                v.memset(ones_w[:], 1.0).then_inc(zeroed.h, 1)
                v.wait_ge(*patterns(6))
                v.tensor_copy(node[:], node_i[:]).then_inc(zeroed.h, 1)
                v.wait_ge(*zeroed(3))
                v.wait_ge(*loaded(64))

                def find(i, b):
                    g = i * 2 + b
                    for k in range(SC):
                        c = bass.ds(g * SC + k, 1)
                        if k >= 1:
                            v.wait_ge(*chunk_counted(g * SC + k - 1))
                        v.scalar_tensor_tensor(out=below[:, k % 2], in0=firsts[:], scalar=node[:, c], in1=ones_w[:],
                                               op0=ALU.is_lt, op1=ALU.mult, accum_out=chunks_before[:, c])\
                            .then_inc(chunk_counted.h, 1)
                    cols = bass.ds(g * SC, SC)
                    v.wait_ge(*chunk_counted(g * SC + SC))
                    v.tensor_scalar(chunk_f[:, cols], chunks_before[:, cols], -1.0, 0.0, ALU.add, ALU.max)\
                        .then_inc(chunk_less.h, 1)
                    v.wait_ge(*chunk_less(g + 1))
                    v.tensor_scalar(chunk_i[:, b], chunk_f[:, cols], 1.0, None, ALU.mult).then_inc(chunk_at.h, 1)

                def place(i, b):
                    v.wait_ge(*chunk_got[b](i * (16 * SC) + 16 * SC))
                    for k in range(SC):
                        c = bass.ds((i * 2 + b) * SC + k, 1)
                        v.wait_ge(*placed[b](i * SC + max(k - 1, 0)))
                        v.scalar_tensor_tensor(out=below_in[:, b, k % 2], in0=chunk[:, b, k, :], scalar=node[:, c],
                                               in1=ones_w[:, 0:CH], op0=ALU.is_lt, op1=ALU.mult,
                                               accum_out=inside[:, c]).then_inc(placed[b].h, 1)

                find(0, 0)
                find(0, 1)
                with v.Fori(0, NS // SC // 2 - 1) as i:
                    for b in range(2):
                        place(i, b)
                        find(i + 1, b)
                for b in range(2):
                    place(NS // SC // 2 - 1, b)
                v.wait_ge(*vs.before("cur"))
                v.tensor_copy(cur[:], cur_i[:]).then_inc(vs.h, 1)
                v.wait_ge(*vs.before("prev"))
                v.tensor_copy(prev[:], prev_i[:]).then_inc(vs.h, 1)
                v.wait_ge(*vs.before("same"))
                v.tensor_tensor(same[:], cur[:], prev[:], ALU.is_equal).then_inc(vs.h, 1)
                v.wait_ge(*vs.before("pen"))
                v.tensor_scalar(pen[:], same[:], -1.0, BIG, ALU.add, ALU.mult).then_inc(vs.h, 1)
                v.wait_ge(*vs.before("eq"))
                v.tensor_scalar(prev[:], cur[:], cur[:, 0:1], None, ALU.is_equal).then_inc(vs.h, 1)
                v.wait_ge(*vs.before("cnt"))
                v.reduce_sum(cnt[:], prev[:], axis=AX.X).then_inc(vs.h, 1)
                v.wait_ge(*vs.before("cont"))
                v.tensor_copy(cont[:], same[:, 0:1]).then_inc(vs.h, 1)
                v.wait_ge(*vs.before("contpen"))
                v.tensor_copy(contpen[:], pen[:, 0:1]).then_inc(vs.h, 1)
                v.wait_ge(*vs.before("whole1"))
                v.tensor_scalar(whole[:], cnt[:], float(ET), None, ALU.is_equal).then_inc(vs.h, 1)
                v.wait_ge(*vs.before("whole"))
                v.tensor_tensor(whole[:], whole[:], cont[:], ALU.mult).then_inc(vs.h, 1)
                v.wait_ge(*vs.before("dst0"))
                v.tensor_copy(dst0[:], cur_i[:, 0:1]).then_inc(vs.h, 1)
                v.wait_ge(*vs.before("row"))
                v.tensor_copy(row[:], row_i[:]).then_inc(vs.h, 1)
                v.wait_ge(*vs.before("fixf"))
                v.scalar_tensor_tensor(out=fixf[:], in0=cnt[:], scalar=-1.0, in1=row[:],
                                       op0=ALU.add, op1=ALU.add).then_inc(vs.h, 1)
                v.wait_ge(*vs.before("fix_at"))
                v.tensor_copy(fix_at[:], fixf[:]).then_inc(vs.h, 1)
                v.wait_ge(*vs.before("valid"))
                v.tensor_scalar(valid[:], node[:, 0:NC], float(N_NODES), None, ALU.is_lt).then_inc(vs.h, 1)
                v.wait_ge(*vs.before("none_at"))
                v.tensor_scalar(none_at[:], node[:, 0:NC], float(EP), None, ALU.add).then_inc(vs.h, 1)
                v.wait_ge(*vs.before("wide"))
                v.tensor_copy(wide[:], whole[:].to_broadcast([P, P])).then_inc(vs.h, 1)
                v.wait_ge(*vs.before("whole_t"))
                v.tensor_copy(whole_t[:], turned[:, 0:P]).then_inc(vs.h, 1)
                v.wait_ge(*vs.before("whole_pen"))
                v.tensor_scalar(whole_pen[:], whole_t[:], -1.0, BIG, ALU.add, ALU.mult).then_inc(vs.h, 1)
                for b in range(2):
                    v.wait_ge(*placed[b](NS // 2))
                v.wait_ge(*chunk_at(NS // SC))
                v.wait_ge(*vs.before("first1"))
                v.tensor_scalar(first[:], chunk_f[:], float(CH), None, ALU.mult).then_inc(vs.h, 1)
                v.wait_ge(*vs.before("first"))
                v.tensor_tensor(first[:], first[:], inside[:], ALU.add).then_inc(vs.h, 1)
                v.wait_ge(*vs.before("deg"))
                v.tensor_tensor(deg[:], first[:, 1:NC + 1], first[:, 0:NC], ALU.subtract).then_inc(vs.h, 1)
                v.wait_ge(*vs.before("has"))
                v.tensor_scalar(has[:], deg[:], 1.0, None, ALU.min).then_inc(vs.h, 1)
                v.wait_ge(*vs.before("hneg"))
                v.tensor_scalar(hneg[:], has[:], -1.0, BIG, ALU.add, ALU.mult).then_inc(vs.h, 1)
                v.wait_ge(*vs.before("last"))
                v.tensor_copy(lastf[:], first[:, 1:NC + 1]).then_inc(vs.h, 1)
                v.wait_ge(*vs.before("lastc"))
                v.tensor_scalar(lastf[:], lastf[:], -1.0, 0.0, ALU.add, ALU.max).then_inc(vs.h, 1)
                v.wait_ge(*vs.before("lasti"))
                v.tensor_copy(last_i[:], lastf[:]).then_inc(vs.h, 1)
                v.wait_ge(*vs.before("none1"))
                v.tensor_tensor(startf[:], first[:, 0:NC], none_at[:], ALU.subtract).then_inc(vs.h, 1)
                v.wait_ge(*vs.before("none2"))
                v.tensor_tensor(startf[:], startf[:], has[:], ALU.mult).then_inc(vs.h, 1)
                v.wait_ge(*vs.before("start2"))
                v.tensor_tensor(startf[:], startf[:], none_at[:], ALU.add).then_inc(vs.h, 1)
                v.wait_ge(*vs.before("starti"))
                v.tensor_copy(start_i[:], startf[:]).then_inc(vs.h, 1)
                normed(v)

            @block.tensor
            def _(pe):
                pe.wait_ge(*patterns(6))
                pe.wait_ge(*vs.before("turned"))
                nc.tensor.transpose(turned[:, 0:P], wide[:], ident[:]).then_inc(vs.h, 1)

            @block.scalar
            def _(act):
                act.wait_ge(*vs.before("none1"))
                act.dma_start(last_d, last_i[:]).then_inc(row_stored[0].h, 16)
                act.wait_ge(*vs.upto(len(vs)))
                act.dma_start(start_d, start_i[:]).then_inc(row_stored[1].h, 16)
                rooted_part(act)
                act.wait_ge(*row_stored[0](16))
                act.wait_ge(*row_stored[1](16))
        st.close()

    def layer_norm_parts(st):
        sq = st.sb("sq", [P, NC, D])
        mean, var, sd, rs = (st.sb(n, [P, NC]) for n in ("mean", "var", "sd", "rs"))
        summed, scaled, centred = (st.sem(n, 2) for n in ("ln_summed", "ln_scaled", "ln_centred"))
        squared, var_ready, rooted = (st.sem(n, 2) for n in ("ln_squared", "ln_var", "ln_rooted"))
        inverted, done = (st.sem(n, 2) for n in ("ln_inverted", "ln_done"))
        half = [slice(0, NC // 2), slice(NC // 2, NC)]

        def wide(t, s):
            return t[:, s].unsqueeze(2).to_broadcast([P, NC // 2, D])

        def vector_part(v):
            for n, s in enumerate(half):
                v.reduce_sum(mean[:, s], x[:, s, :], axis=AX.X).then_inc(summed.h, 1)
                v.wait_ge(*summed(n + 1))
                v.tensor_scalar(mean[:, s], mean[:, s], 1.0 / D, None, ALU.mult).then_inc(scaled.h, 1)
                v.wait_ge(*scaled(n + 1))
                v.tensor_tensor(h[:, s, :], x[:, s, :], wide(mean, s), ALU.subtract).then_inc(centred.h, 1)
            for n, s in enumerate(half):
                v.wait_ge(*squared(n + 1))
                v.reduce_sum(var[:, s], sq[:, s, :], axis=AX.X).then_inc(var_ready.h, 1)
            for n, s in enumerate(half):
                v.wait_ge(*rooted(n + 1))
                v.reciprocal(rs[:, s], sd[:, s]).then_inc(inverted.h, 1)
                v.wait_ge(*inverted(n + 1))
                v.scalar_tensor_tensor(out=h[:, s, :], in0=h[:, s, :], scalar=0.0, in1=wide(rs, s),
                                       op0=ALU.max, op1=ALU.mult).then_inc(done.h, 1)
            v.wait_ge(*done(2))

        def scalar_part(act):
            for n, s in enumerate(half):
                act.wait_ge(*centred(n + 1))
                act.activation(sq[:, s, :], h[:, s, :], ACT.Square).then_inc(squared.h, 1)
            for n, s in enumerate(half):
                act.wait_ge(*var_ready(n + 1))
                act.activation(sd[:, s], var[:, s], ACT.Sqrt, bias=eps[:], scale=1.0 / D).then_inc(rooted.h, 1)
        return vector_part, scalar_part

    def layer_norm(tag):
        st = Stage(nc, tag, signals)
        vector_part, scalar_part = layer_norm_parts(st)
        with nc.Block() as block:
            @block.vector
            def _(v):
                vector_part(v)

            @block.scalar
            def _(act):
                scalar_part(act)
        st.close()

    def prepare_conv(tag, wq_t, bq, wk_t, bk, we_t):
        st = Stage(nc, tag, signals)
        wq1 = st.sb("wq1", [D, D + 1])
        wk1 = st.sb("wk1", [D, YT])
        wqq = st.sb("wqq", [D + 1, YT])
        hs, ht = st.sb("hs", [P, 2, NB, D]), st.sb("ht", [D + 1, 2, NB, P])
        qs = st.sb("qs", [P, 2, NB, YT])
        at = st.sb("at", [P, 2, NB], I32)
        ps_h, ps_q = ([st.ps(f"{n}{b}", [P, 8, P]) for b in range(2)] for n in ("ps_h", "ps_q"))
        loaded = st.dma("w_loaded", 5 * 16)
        made = st.sem("w_made", 2)
        ones_set = st.sem("ones_set", 1)
        tab = st.dma("tab_stored", 16)
        at_loaded = st.dma_slots("at_loaded", 16 * NBLK // 2)
        scattered = st.dma_slots("scattered", 16 * NB * NBLK // 2)
        q_stored = st.dma_slots("q_stored", 16 * NBLK // 2)
        hs_ready, turned, ht_ready, mixed = (st.slots(n, NBLK // 2) for n in ("hs_ready", "h_turned", "ht_ready", "mixed"))
        q_ready = st.slots("q_ready", NBLK // 2)

        with nc.Block() as block:
            @block.sync
            def _(sp):
                for dst_, src_ in ((wq1[:, 0:D], wq_t), (wq1[:, D:D + 1], bq.rearrange("(n a) -> n a", a=1)),
                                   (wk1[:, 0:D], wk_t), (wk1[:, D:D + DE], we_t),
                                   (wk1[:, D + DE:YT], bk.rearrange("(n a) -> n a", a=1))):
                    sp.dma_start(dst_, src_).then_inc(loaded.h, 16)
                def indices(i, b):
                    sp.dma_start(at[:, b, :], start_d[:, bass.ds((i * 2 + b) * NB, NB)]).then_inc(at_loaded[b].h, 16)

                def table(i, b):
                    sp.wait_ge(*q_ready[b](i + 1))
                    sp.dma_start(by_node(q_tab)[:, bass.ds((i * 2 + b) * NB, NB), :],
                                 qs[:, b]).then_inc(q_stored[b].h, 16)

                indices(0, 0)
                indices(0, 1)
                sp.dma_start(by_node(h_tab), h[:]).then_inc(tab.h, 16)
                with sp.Fori(0, NBLK // 2 - 1) as i:
                    for b in range(2):
                        table(i, b)
                        sp.wait_ge(*scattered[b](i * (16 * NB) + 16 * NB))
                        indices(i + 1, b)
                for b in range(2):
                    table(NBLK // 2 - 1, b)
                sp.wait_ge(*tab(16))
                for b in range(2):
                    sp.wait_ge(*q_stored[b](16 * NBLK // 2))
                    sp.wait_ge(*scattered[b](16 * NB * NBLK // 2))

            @block.gpsimd
            def _(pool):
                with pool.Fori(0, NBLK // 2) as i:
                    for b in range(2):
                        pool.wait_ge(*at_loaded[b](i * 16 + 16))
                        pool.nop(nofuse=True)
                        pool.wait_ge(*q_ready[b](i + 1))
                        pool.nop(nofuse=True)
                        for k in range(NB):
                            nc.gpsimd.indirect_dma_start(q_start, indexed(at[:, b, k:k + 1]), qs[:, b, k, :],
                                                         None).then_inc(scattered[b].h, 16)

            @block.scalar
            def _(act):
                act.wait_ge(*made(1))
                act.activation(wqq[:], ps_q[0][0:D + 1, 0, 0:YT], ACT.Copy, scale=1.0 / 8.0).then_inc(made.h, 1)
                def take(i, b):
                    act.wait_ge(*turned[b](i))
                    act.activation(hs[:, b], h[:, bass.ds((i * 2 + b) * NB, NB), :], ACT.Copy)\
                        .then_inc(hs_ready[b].h, 1)

                def rows_out(i, b):
                    act.wait_ge(*mixed[b](i + 1))
                    act.wait_ge(*scattered[b](i * (16 * NB)))
                    act.wait_ge(*q_stored[b](i * 16))
                    act.activation(qs[:, b], ps_q[b][:, 0:NB, 0:YT], ACT.Copy).then_inc(q_ready[b].h, 1)

                take(0, 0)
                take(0, 1)
                with act.Fori(0, NBLK // 2 - 1) as i:
                    for b in range(2):
                        rows_out(i, b)
                        take(i + 1, b)
                for b in range(2):
                    rows_out(NBLK // 2 - 1, b)

            @block.vector
            def _(v):
                v.memset(ht[D:D + 1], 1.0).then_inc(ones_set.h, 1)
                with v.Fori(0, NBLK // 2) as i:
                    for b in range(2):
                        v.wait_ge(*turned[b](i + 1))
                        v.wait_ge(*mixed[b](i))
                        v.tensor_copy(ht[0:D, b], ps_h[b][0:D, 0:NB, :]).then_inc(ht_ready[b].h, 1)

            @block.tensor
            def _(pe):
                pe.wait_ge(*loaded(80))
                nc.tensor.matmul(ps_q[0][0:D + 1, 0, 0:YT], wq1[:], wk1[:], start=True, stop=True).then_inc(made.h, 1)
                pe.wait_ge(*made(2))
                pe.wait_ge(*ones_set(1))
                def turn(i, b):
                    pe.wait_ge(*hs_ready[b](i + 1))
                    pe.nop(nofuse=True)
                    pe.wait_ge(*ht_ready[b](i))
                    pe.nop(nofuse=True)
                    for k in range(NB):
                        last = nc.tensor.transpose(ps_h[b][0:D, k, :], hs[:, b, k, :], ident[:])
                    last.then_inc(turned[b].h, 1)

                def mix(i, b):
                    pe.wait_ge(*ht_ready[b](i + 1))
                    pe.nop(nofuse=True)
                    pe.wait_ge(*q_ready[b](i))
                    pe.nop(nofuse=True)
                    for k in range(NB):
                        last = nc.tensor.matmul(ps_q[b][:, k, 0:YT], ht[:, b, k, :], wqq[:], start=True, stop=True)
                    last.then_inc(mixed[b].h, 1)

                turn(0, 0)
                turn(0, 1)
                with pe.Fori(0, NBLK // 2 - 1) as i:
                    for b in range(2):
                        mix(i, b)
                        turn(i + 1, b)
                for b in range(2):
                    mix(NBLK // 2 - 1, b)
        st.close()

    def conv_edges(tag, rows):
        H, F = 1, YT
        st = Stage(nc, tag, signals)
        at = st.sb("at", [P, 2, G], I32)
        q_raw, y = st.sb("q_raw", [P, 2, G, F]), st.sb("y", [P, 2, G, F])
        q_in, mask = st.sb("q_in", [P, 2, F, G + 1]), st.sb("mask", [P, 2, F, G + 1])
        q_all, prod = st.sb("q_all", [P, F, G + 1]), st.sb("prod", [P, G, F])
        s, fm = st.sb("s", [P, G]), st.sb("fm", [P, 2, G + 1])
        de, ex = st.sb("de", [P, 2, G]), st.sb("ex", [P, 2, G])
        r, w_in = st.sb("r", [P, F, G + 1]), st.sb("w_in", [P, F, G + 1])
        acc = st.sb("acc", [P, 2, F, G + 1])
        row = st.sb("row", [P, 2, G, F + 1])
        q0 = st.sb("q0", [P, F])
        half = NG // 2
        ready = st.sem("edges_ready", 8)
        q0_got = st.dma("q0_got", 16)
        at_loaded, q_loaded, e_loaded = (st.dma_slots(n, 16 * half) for n in ("at_loaded", "q_loaded", "e_loaded"))
        gathered = st.dma_slots(f"gathered_{tag}_", 16 * G * half)
        q_turned, weighted, row_ready = (st.slots(n, half) for n in ("q_turned", "weighted", "row_ready"))
        row_stored = st.dma_slots("row_stored", 16 * half)
        filled, q_carried, multiplied, scored = (st.sem(n, NG) for n in
                                                 ("q_filled", "q_carried", "multiplied", "scored"))
        maxed, m_carried, shifted, exps, r_ready = (st.sem(n, NG) for n in
                                                    ("maxed", "m_carried", "shifted", "exps", "r_ready"))
        summed, carried = (st.sem(n, NG) for n in ("summed", "carried"))
        differed = st.sem("differed", NG)

        with nc.Block() as block:
            @block.sync
            def _(sp):
                with sp.Fori(0, half) as i:
                    for b in range(2):
                        t0 = (i * 2 + b) * G
                        sp.wait_ge(*weighted[b](i))
                        sp.dma_start(at[:, b], a["src"].rearrange("(p t) -> p t", p=P)[:, bass.ds(t0, G)])\
                            .then_inc(at_loaded[b].h, 16)
                        sp.wait_ge(*q_turned[b](i))
                        sp.dma_start(q_raw[:, b], by_edge(q_start)[:, bass.ds(t0, G), :]).then_inc(q_loaded[b].h, 16)
                        sp.wait_ge(*weighted[b](i))
                        sp.dma_start(y[:, b, :, D:D + DE],
                                     a["edge_attr_32"].rearrange("(p t) f -> p t f", p=P)[:, bass.ds(t0, G), :])\
                            .then_inc(e_loaded[b].h, 16)

            @block.gpsimd
            def _(pool):
                nc.gpsimd.indirect_dma_start(q0[:], None, q_tab, indexed(dst0[:])).then_inc(q0_got.h, 16)
                with pool.Fori(0, half) as i:
                    for b in range(2):
                        pool.wait_ge(*at_loaded[b](i * 16 + 16))
                        pool.nop(nofuse=True)
                        pool.wait_ge(*weighted[b](i))
                        pool.nop(nofuse=True)
                        for k in range(G):
                            nc.gpsimd.indirect_dma_start(y[:, b, k, 0:D], None, h_tab, indexed(at[:, b, k:k + 1]))\
                                .then_inc(gathered[b].h, 16)

            @block.vector
            def _(v):
                v.memset(mask[:, 0, :, 0:1], 0.0).then_inc(ready.h, 1)
                v.memset(mask[:, 1, :, 0:1], 0.0).then_inc(ready.h, 1)
                v.memset(r[:, :, 0:1], 0.0).then_inc(ready.h, 1)
                v.memset(w_in[:, :, 0:1], 0.0).then_inc(ready.h, 1)
                v.memset(fm[:, 0, 0:1], -BIG).then_inc(ready.h, 1)
                v.memset(y[:, 0, :, F - 1:F], 1.0).then_inc(ready.h, 1)
                v.memset(y[:, 1, :, F - 1:F], 1.0).then_inc(ready.h, 1)
                v.wait_ge(*q0_got(16))
                v.tensor_copy(q_in[:, 0, :, 0:1], q0[:].unsqueeze(2)).then_inc(ready.h, 1)
                v.wait_ge(*ready(8))
                with v.Fori(0, half) as i:
                    for b in range(2):
                        g = i * 2 + b
                        v.wait_ge(*q_turned[b](i + 1))
                        v.wait_ge(*q_carried(g))
                        v.tensor_tensor_scan(q_all[:].rearrange("p f t -> p (f t)"),
                                             mask[:, b].rearrange("p f t -> p (f t)"),
                                             q_in[:, b].rearrange("p f t -> p (f t)"), 0.0,
                                             ALU.mult, ALU.add).then_inc(filled.h, 1)
                        v.wait_ge(*filled(g + 1))
                        v.tensor_copy(q_in[:, 1 - b, :, 0:1], q_all[:, :, G:G + 1]).then_inc(q_carried.h, 1)
                        v.wait_ge(*gathered[b](i * (16 * G) + 16 * G))
                        v.wait_ge(*e_loaded[b](i * 16 + 16))
                        v.tensor_tensor(prod[:], y[:, b], q_all[:, :, 1:G + 1].rearrange("p f t -> p t f"),
                                        ALU.mult).then_inc(multiplied.h, 1)
                        v.wait_ge(*multiplied(g + 1))
                        v.reduce_sum(s[:], prod[:], axis=AX.X).then_inc(scored.h, 1)
                        v.wait_ge(*scored(g + 1))
                        v.wait_ge(*m_carried(g))
                        v.tensor_tensor_scan(fm[:, b, 1:G + 1], pen[:, bass.ds(g * G, G)], s[:], fm[:, b, 0:1],
                                             ALU.add, ALU.max).then_inc(maxed.h, 1)
                        v.wait_ge(*maxed(g + 1))
                        if b == 0:
                            v.wait_ge(*row_ready[1](i))
                        else:
                            v.wait_ge(*row_ready[0](i + 1))
                        v.tensor_copy(fm[:, 1 - b, 0:1], fm[:, b, G:G + 1]).then_inc(m_carried.h, 1)
                        v.tensor_tensor(de[:, 0], fm[:, b, 0:G], fm[:, b, 1:G + 1], ALU.subtract)\
                            .then_inc(differed.h, 1)
                        v.tensor_tensor(de[:, 1], s[:], fm[:, b, 1:G + 1], ALU.subtract)
                        v.wait_ge(*differed(g + 1))
                        v.tensor_tensor(de[:, 0], de[:, 0], pen[:, bass.ds(g * G, G)], ALU.add)\
                            .then_inc(shifted.h, 1)
                        v.wait_ge(*exps(g + 1))
                        v.wait_ge(*carried(g))
                        v.tensor_tensor(w_in[:, :, 1:G + 1], y[:, b].rearrange("p t f -> p f t"),
                                        ex[:, 1].unsqueeze(1).to_broadcast([P, F, G]), ALU.mult)\
                            .then_inc(weighted[b].h, 1)
                        v.wait_ge(*weighted[b](i + 1))
                        v.wait_ge(*r_ready(g + 1))
                        v.wait_ge(*row_ready[b](i))
                        v.tensor_tensor_scan(acc[:, b].rearrange("p f t -> p (f t)"),
                                             r[:].rearrange("p f t -> p (f t)"),
                                             w_in[:].rearrange("p f t -> p (f t)"), 0.0,
                                             ALU.mult, ALU.add).then_inc(summed.h, 1)
                        v.wait_ge(*summed(g + 1))
                        v.tensor_copy(w_in[:, :, 0:1], acc[:, b, :, G:G + 1]).then_inc(carried.h, 1)
                v.wait_ge(*carried(NG))
                v.tensor_copy(carry_v[:, 0:F], w_in[:, :, 0])
                v.tensor_copy(carry_m[:, 0:1], fm[:, 0, 0:1])

            @block.scalar
            def _(act):
                def turn(i, b):
                    g = i * 2 + b
                    act.wait_ge(*q_loaded[b](i * 16 + 16))
                    if b == 0:
                        if not isinstance(i, int):
                            act.wait_ge(*filled(g - 1))
                    elif not isinstance(i, int):
                        act.wait_ge(*filled(g - 1))
                    act.activation(q_in[:, b, :, 1:G + 1], q_raw[:, b].rearrange("p t f -> p f t"), ACT.Copy)
                    act.activation(mask[:, b, :, 1:G + 1],
                                   same[:, bass.ds(g * G, G)].unsqueeze(1).to_broadcast([P, F, G]), ACT.Copy)\
                        .then_inc(q_turned[b].h, 1)

                def weights(i, b):
                    g = i * 2 + b
                    act.wait_ge(*shifted(g + 1))
                    if b == 1:
                        act.wait_ge(*weighted[0](i + 1))
                    else:
                        act.wait_ge(*weighted[1](i))
                    act.activation(ex[:], de[:], ACT.Exp).then_inc(exps.h, 1)
                    act.wait_ge(*exps(g + 1))
                    act.wait_ge(*summed(g))
                    act.activation(r[:, :, 1:G + 1], ex[:, 0].unsqueeze(1).to_broadcast([P, F, G]), ACT.Copy)\
                        .then_inc(r_ready.h, 1)

                def send(i, b):
                    g = i * 2 + b
                    act.wait_ge(*summed(g + 1))
                    act.wait_ge(*row_stored[b](i * 16))
                    act.activation(row[:, b, :, F:F + 1], fm[:, b, 1:G + 1].unsqueeze(2), ACT.Copy)
                    act.activation(row[:, b, :, 0:F], acc[:, b, :, 1:G + 1].rearrange("p f t -> p t f"), ACT.Copy)\
                        .then_inc(row_ready[b].h, 1)
                    act.wait_ge(*row_ready[b](i + 1))
                    act.dma_start(by_edge(rows)[:, bass.ds(g * G, G), :], row[:, b]).then_inc(row_stored[b].h, 16)

                turn(0, 0)
                weights(0, 0)
                turn(0, 1)
                send(0, 0)
                weights(0, 1)
                with act.Fori(1, half) as i:
                    turn(i, 0)
                    send(i - 1, 1)
                    weights(i, 0)
                    turn(i, 1)
                    send(i, 0)
                    weights(i, 1)
                send(half - 1, 1)
                for b in range(2):
                    act.wait_ge(*row_stored[b](16 * half))
        st.close()

    def join_softmax(tag, rows, H, J):
        F = H * (J + 1)
        st = Stage(nc, tag, signals)
        mrep, got = st.sb("mrep", [P, F]), st.sb("got", [P, F + H])
        vt, mt = st.sb("vt", [F, P]), st.sb("mt", [F, P])
        ms, vs_ = st.sb("ms", [F, P + 1]), st.sb("vs", [F, P + 1])
        rt, wt = st.sb("rt", [F, P]), st.sb("wt", [F, P])
        vin, min_, mall = st.sb("vin", [P, F]), st.sb("min", [P, F]), st.sb("mall", [P, F])
        e_in, e_row = st.sb("e_in", [P, F]), st.sb("e_row", [P, F])
        pa, pb = st.ps("pa", [P, 512]), st.ps("pb", [P, 512])
        got_row = st.dma("fix_got", 16)
        put_row = st.dma("fix_put", 16)
        ch = st.chain("fix_steps", """mrep turn_v turn_m copy_v copy_m edge_m edge_v scan_m dr pr dw exp_r exp_w wv scan_v
            back_v back_m copy_vin copy_min pen_in max din drow exp_in exp_row vin_w row_w row_new m_new""")

        with nc.Block() as block:
            @block.gpsimd
            def _(pool):
                nc.gpsimd.indirect_dma_start(got[:], None, rows, indexed(fix_at[:])).then_inc(got_row.h, 16)
                pool.wait_ge(*ch.upto(len(ch)))
                nc.gpsimd.indirect_dma_start(rows, indexed(fix_at[:]), got[:], None).then_inc(put_row.h, 16)
                pool.wait_ge(*put_row(16))

            @block.tensor
            def _(pe):
                for name, dst_, src_, n in (("turn_v", pa[0:F, 0:P], carry_v[:, 0:F], P),
                                            ("turn_m", pb[0:F, 0:P], mrep[:], P),
                                            ("back_v", pa[:, 0:F], vs_[:, 0:P], F),
                                            ("back_m", pb[:, 0:F], ms[:, 0:P], F)):
                    pe.wait_ge(*ch.before(name))
                    nc.tensor.transpose(dst_, src_, ident[0:n, 0:n]).then_inc(ch.h, 1)

            @block.scalar
            def _(act):
                for name, t in (("exp_r", rt), ("exp_w", wt), ("exp_in", e_in), ("exp_row", e_row)):
                    act.wait_ge(*ch.before(name))
                    act.activation(t[:], t[:], ACT.Exp).then_inc(ch.h, 1)

            @block.vector
            def _(v):

                def heads(t):
                    return t.rearrange("p (h j) -> p h j", h=H)

                mrow = got[:, F:F + H].unsqueeze(2).to_broadcast([P, H, J + 1])
                v.wait_ge(*ch.before("mrep"))
                v.tensor_copy(heads(mrep[:]), carry_m[:, 0:H].unsqueeze(2).to_broadcast([P, H, J + 1]))\
                    .then_inc(ch.h, 1)
                v.wait_ge(*ch.before("copy_v"))
                v.tensor_copy(vt[:], pa[0:F, 0:P]).then_inc(ch.h, 1)
                v.wait_ge(*ch.before("copy_m"))
                v.tensor_copy(mt[:], pb[0:F, 0:P]).then_inc(ch.h, 1)
                v.wait_ge(*ch.before("edge_m"))
                v.memset(ms[:, 0:1], -BIG).then_inc(ch.h, 1)
                v.wait_ge(*ch.before("edge_v"))
                v.memset(vs_[:, 0:1], 0.0).then_inc(ch.h, 1)
                v.wait_ge(*ch.before("scan_m"))
                v.tensor_tensor_scan(ms[:, 1:P + 1], whole_pen[0:F, :], mt[:], -BIG, ALU.add, ALU.max)\
                    .then_inc(ch.h, 1)
                v.wait_ge(*ch.before("dr"))
                v.tensor_tensor(rt[:], ms[:, 0:P], ms[:, 1:P + 1], ALU.subtract).then_inc(ch.h, 1)
                v.wait_ge(*ch.before("pr"))
                v.tensor_tensor(rt[:], rt[:], whole_pen[0:F, :], ALU.add).then_inc(ch.h, 1)
                v.wait_ge(*ch.before("dw"))
                v.tensor_tensor(wt[:], mt[:], ms[:, 1:P + 1], ALU.subtract).then_inc(ch.h, 1)
                v.wait_ge(*ch.before("wv"))
                v.tensor_tensor(wt[:], wt[:], vt[:], ALU.mult).then_inc(ch.h, 1)
                v.wait_ge(*ch.before("scan_v"))
                v.tensor_tensor_scan(vs_[:, 1:P + 1], rt[:], wt[:], 0.0, ALU.mult, ALU.add).then_inc(ch.h, 1)
                v.wait_ge(*ch.before("copy_vin"))
                v.tensor_copy(vin[:], pa[:, 0:F]).then_inc(ch.h, 1)
                v.wait_ge(*ch.before("copy_min"))
                v.tensor_copy(min_[:], pb[:, 0:F]).then_inc(ch.h, 1)
                v.wait_ge(*ch.before("pen_in"))
                v.tensor_scalar(min_[:], min_[:], contpen[:, 0:1], None, ALU.add).then_inc(ch.h, 1)
                v.wait_ge(*got_row(16))
                v.wait_ge(*ch.before("max"))
                v.tensor_tensor(heads(mall[:]), heads(min_[:]), mrow, ALU.max).then_inc(ch.h, 1)
                v.wait_ge(*ch.before("din"))
                v.tensor_tensor(e_in[:], min_[:], mall[:], ALU.subtract).then_inc(ch.h, 1)
                v.wait_ge(*ch.before("drow"))
                v.tensor_tensor(heads(e_row[:]), mrow, heads(mall[:]), ALU.subtract).then_inc(ch.h, 1)
                v.wait_ge(*ch.before("vin_w"))
                v.tensor_tensor(vin[:], vin[:], e_in[:], ALU.mult).then_inc(ch.h, 1)
                v.wait_ge(*ch.before("row_w"))
                v.tensor_tensor(got[:, 0:F], got[:, 0:F], e_row[:], ALU.mult).then_inc(ch.h, 1)
                v.wait_ge(*ch.before("row_new"))
                v.tensor_tensor(got[:, 0:F], got[:, 0:F], vin[:], ALU.add).then_inc(ch.h, 1)
                v.wait_ge(*ch.before("m_new"))
                v.tensor_copy(got[:, F:F + H], heads(mall[:])[:, :, 0]).then_inc(ch.h, 1)
        st.close()

    def finish_conv(tag, rows, wv, bv, we, ws, bs, skip=None):
        st = Stage(nc, tag, signals)
        w_agg, w_self = st.sb("w_agg", [YT, D]), st.sb("w_self", [D + 1, D])
        at = st.sb("at", [P, 2, NB], I32)
        got = st.sb("got", [P, 2, NB, YT + 1])
        rd, agg = st.sb("rd", [P, NB]), st.sb("agg", [P, 2, NB, YT])
        agg_t, ht = st.sb("agg_t", [YT, 2, NB, P]), st.sb("ht", [D + 1, 2, NB, P])
        hs = st.sb("hs", [P, 2, NB, D])
        ps_a, ps_h = st.ps("ps_a", [P, 8, P]), st.ps("ps_h", [P, 8, P])
        ps_o = [st.ps(f"ps_o{b}", [P, 512]) for b in range(1 if skip else 2)] * 2
        o = [ps_o[b][:, 0:NB * D].rearrange("p (k f) -> p k f", k=NB) for b in range(2)]
        loads = [(w_agg[0:D, :], wv), (w_agg[D:D + DE, :], we), (w_agg[D + DE:YT, :], bv.rearrange("(a n) -> a n", a=1)),
                 (w_self[0:D, :], ws), (w_self[D:D + 1, :], bs.rearrange("(a n) -> a n", a=1))]
        if skip:
            w_sk1, w_sk2 = st.sb("w_sk1", [D + 1, D]), st.sb("w_sk2", [D, D])
            h2, h2t = st.sb("h2", [P, 2, NB, D]), st.sb("h2t", [D, 2, NB, P])
            ps_s, ps_2 = st.ps("ps_s", [P, 512]), st.ps("ps_2", [P, 8, P])
            o2 = ps_s[:, 0:NB * D].rearrange("p (k f) -> p k f", k=NB)
            loads += [(w_sk1[0:D, :], skip[0][0:D, :]), (w_sk1[D:D + 1, :], skip[1].rearrange("(a n) -> a n", a=1)),
                      (w_sk2[:], skip[0][D:2 * D, :])]
        loaded = st.dma("w_loaded", 16 * len(loads))
        made = st.sem("w_made", 1)
        at_loaded = st.dma_slots("at_loaded", 16 * NBLK // 2)
        node_got = st.dma_slots("node_got", 16 * NB * NBLK // 2)
        half = NBLK // 2
        (agg_made, agg_turned, agg_copied, hs_ready, turned, ht_ready, mixed, done) = (st.slots(n, half) for n in (
            "agg_made", "agg_turned", "agg_copied", "hs_ready", "h_turned", "ht_ready", "mixed", "done"))
        den, inv, inv_has = (st.sem(n, NBLK) for n in ("den", "inv", "inv_has"))
        if skip:
            h2_made, h2_turned, h2t_ready, skipped = (st.slots(n, half) for n in
                                                      ("h2_made", "h2_turned", "h2t_ready", "skipped"))
        ht_used, o_read = (skipped, h2_made) if skip else (mixed, done)

        def over_blocks(eng, first, body):
            first()
            body(0, 0, (0, 1), None)
            body(0, 1, (1, 0), (0, 0))
            with eng.Fori(1, half - 1) as i:
                body(i, 0, (i, 1), (i - 1, 1))
                body(i, 1, (i + 1, 0), (i, 0))
            body(half - 1, 0, (half - 1, 1), (half - 2, 1))
            body(half - 1, 1, None, (half - 1, 0))

        with nc.Block() as block:
            @block.sync
            def _(sp):
                for dst_, src_ in loads:
                    sp.dma_start(dst_, src_).then_inc(loaded.h, 16)
                with sp.Fori(0, NBLK // 2) as i:
                    for b in range(2):
                        sp.wait_ge(*agg_made[b](i))
                        sp.dma_start(at[:, b, :], last_d[:, bass.ds((i * 2 + b) * NB, NB)])\
                            .then_inc(at_loaded[b].h, 16)

            @block.gpsimd
            def _(pool):
                with pool.Fori(0, NBLK // 2) as i:
                    for b in range(2):
                        pool.wait_ge(*at_loaded[b](i * 16 + 16))
                        pool.nop(nofuse=True)
                        pool.wait_ge(*agg_made[b](i))
                        pool.nop(nofuse=True)
                        for k in range(NB):
                            nc.gpsimd.indirect_dma_start(got[:, b, k, :], None, rows, indexed(at[:, b, k:k + 1]))\
                                .then_inc(node_got[b].h, 16)

            @block.vector
            def _(v):
                def aggregate(i, b):
                    g = i * 2 + b
                    v.wait_ge(*node_got[b](i * (16 * NB) + 16 * NB))
                    v.wait_ge(*agg_turned[b](i))
                    v.tensor_scalar(rd[:], got[:, b, :, YT - 1], TINY, None, ALU.max).then_inc(den.h, 1)
                    v.wait_ge(*den(g + 1))
                    v.reciprocal(rd[:], rd[:]).then_inc(inv.h, 1)
                    v.wait_ge(*inv(g + 1))
                    v.tensor_tensor(rd[:], rd[:], has[:, bass.ds(g * NB, NB)], ALU.mult).then_inc(inv_has.h, 1)
                    v.wait_ge(*inv_has(g + 1))
                    v.tensor_tensor(agg[:, b], got[:, b, :, 0:YT], rd[:].unsqueeze(2).to_broadcast([P, NB, YT]),
                                    ALU.mult).then_inc(agg_made[b].h, 1)

                def add_layer(i, b):
                    v.wait_ge(*skipped[b](i + 1))
                    cols = bass.ds((i * 2 + b) * NB, NB)
                    v.scalar_tensor_tensor(out=x[:, cols, :], in0=o2, scalar=0.0, in1=x[:, cols, :],
                                           op0=ALU.max, op1=ALU.add).then_inc(done[b].h, 1)

                def body(i, b, after, ahead):
                    v.wait_ge(*agg_turned[b](i + 1))
                    v.wait_ge(*mixed[b](i))
                    v.tensor_copy(agg_t[:, b], ps_a[0:YT, 0:NB, :]).then_inc(agg_copied[b].h, 1)
                    if after:
                        aggregate(*after)
                    v.wait_ge(*mixed[b](i + 1))
                    if not skip:
                        v.tensor_scalar(h[:, bass.ds((i * 2 + b) * NB, NB), :], o[b], 0.0, None, ALU.max)\
                            .then_inc(done[b].h, 1)
                        return
                    v.wait_ge(*h2_turned[b](i))
                    v.tensor_scalar(h2[:, b], o[b], 0.0, None, ALU.max).then_inc(h2_made[b].h, 1)
                    if ahead:
                        add_layer(*ahead)

                v.memset(ht[D:D + 1], 1.0).then_inc(made.h, 1)
                over_blocks(v, lambda: aggregate(0, 0), body)
                if skip:
                    add_layer(half - 1, 1)

            @block.scalar
            def _(act):
                def take(i, b):
                    act.wait_ge(*turned[b](i))
                    act.activation(hs[:, b], h[:, bass.ds((i * 2 + b) * NB, NB), :], ACT.Copy)\
                        .then_inc(hs_ready[b].h, 1)
                    act.wait_ge(*turned[b](i + 1))
                    act.wait_ge(*ht_used[b](i))
                    act.activation(ht[0:D, b], ps_h[0:D, 0:NB, :], ACT.Copy).then_inc(ht_ready[b].h, 1)

                def body(i, b, after, ahead):
                    if after:
                        take(*after)
                    if skip:
                        act.wait_ge(*h2_turned[b](i + 1))
                        act.wait_ge(*skipped[b](i))
                        act.activation(h2t[:, b], ps_2[0:D, 0:NB, :], ACT.Copy).then_inc(h2t_ready[b].h, 1)

                over_blocks(act, lambda: take(0, 0), body)

            @block.tensor
            def _(pe):
                def turn_h(i, b, ahead):
                    pe.wait_ge(*hs_ready[b](i + 1))
                    pe.nop(nofuse=True)
                    if ahead:
                        pe.wait_ge(*ht_ready[ahead[1]](ahead[0] + 1))
                        pe.nop(nofuse=True)
                    for k in range(NB):
                        last = nc.tensor.transpose(ps_h[0:D, k, :], hs[:, b, k, :], ident[:])
                    last.then_inc(turned[b].h, 1)

                def turn_agg(i, b):
                    pe.wait_ge(*agg_made[b](i + 1))
                    pe.nop(nofuse=True)
                    for k in range(NB):
                        last = nc.tensor.transpose(ps_a[0:YT, k, :], agg[:, b, k, :], ident[:])
                    last.then_inc(agg_turned[b].h, 1)

                def skip_product(i, b, ahead):
                    pe.wait_ge(*h2t_ready[b](i + 1))
                    pe.nop(nofuse=True)
                    if ahead:
                        pe.wait_ge(*done[ahead[1]](ahead[0] + 1))
                        pe.nop(nofuse=True)
                    for k in range(NB):
                        nc.tensor.matmul(o2[:, k, :], ht[:, b, k, :], w_sk1[:], start=True, stop=False)
                        last = nc.tensor.matmul(o2[:, k, :], h2t[:, b, k, :], w_sk2[:], start=False, stop=True)
                    last.then_inc(skipped[b].h, 1)

                def body(i, b, after, ahead):
                    if after:
                        turn_h(*after, (i, b))
                    pe.wait_ge(*agg_copied[b](i + 1))
                    pe.nop(nofuse=True)
                    pe.wait_ge(*ht_ready[b](i + 1))
                    pe.nop(nofuse=True)
                    pe.wait_ge(*o_read[b](i))
                    pe.nop(nofuse=True)
                    if skip and ahead:
                        pe.wait_ge(*o_read[ahead[1]](ahead[0] + 1))
                        pe.nop(nofuse=True)
                    for k in range(NB):
                        nc.tensor.matmul(o[b][:, k, :], agg_t[:, b, k, :], w_agg[:], start=True, stop=False)
                        last = nc.tensor.matmul(o[b][:, k, :], ht[:, b, k, :], w_self[:], start=False, stop=True)
                    last.then_inc(mixed[b].h, 1)
                    if after:
                        turn_agg(*after)
                    if skip:
                        if ahead:
                            first = isinstance(ahead[0], int) and ahead == (0, 0)
                            skip_product(*ahead, None if first else (i - 1, b))
                        pe.wait_ge(*h2_made[b](i + 1))
                        pe.nop(nofuse=True)
                        if ahead:
                            pe.wait_ge(*h2t_ready[ahead[1]](ahead[0] + 1))
                            pe.nop(nofuse=True)
                        for k in range(NB):
                            last = nc.tensor.transpose(ps_2[0:D, k, :], h2[:, b, k, :], ident[:])
                        last.then_inc(h2_turned[b].h, 1)

                pe.wait_ge(*loaded(16 * len(loads)))
                pe.wait_ge(*made(1))

                def first():
                    turn_h(0, 0, None)
                    turn_agg(0, 0)

                over_blocks(pe, first, body)
                if skip:
                    skip_product(half - 1, 1, (half - 1, 0))
        st.close()

    def prepare_gat(tag, gt, w, a_src, a_dst, heads, edge=None):
        st = Stage(nc, tag, signals)
        wg = st.sb("wg", [D, TG])
        av = st.sb("av", [D, 2, D])
        pr = st.sb("pr", [D, 2, D])
        hs, ht = st.sb("hs", [P, 2, NB, D]), st.sb("ht", [D, 2, NB, P])
        adq = st.sb("adq", [P, 2, NB, HG])
        at = st.sb("at", [P, 2, NB], I32)
        ps_h, ps_q = ([st.ps(f"{n}{b}", [P, 8, P]) for b in range(2)] for n in ("ps_h", "ps_q"))
        width = D // heads
        loads = [(wg[:, 0:D], w), (av[:, 0, :], row_of(a_src, D, D)), (av[:, 1, :], row_of(a_dst, D, D))]
        if edge:
            bd, w_e, a_e = edge
            wev, aev = st.sb("wev", [P, D]), st.sb("aev", [P, D])
            m8 = st.sb("m8", [P, HG])
            loads += [(wev[8 * k:8 * k + 8, :], w_e) for k in range(G)] + [(aev[:], row_of(a_e, D))]
        steps = "prod sum" + (" eprod esum spread" if edge else "")
        loaded = st.dma("w_loaded", 16 * len(loads))
        ch = st.chain("gat_steps", steps)
        diag = st.sem("diag", 1)
        at_loaded = st.dma_slots("at_loaded", 16 * NBLK // 2)
        scattered = st.dma_slots("scattered", 16 * NB * NBLK // 2)
        q_stored = st.dma_slots("q_stored", 16 * NBLK // 2)
        hs_ready, turned, ht_ready, mixed = (st.slots(n, NBLK // 2) for n in ("hs_ready", "h_turned", "ht_ready", "mixed"))
        q_ready = st.slots("q_ready", NBLK // 2)

        with nc.Block() as block:
            @block.sync
            def _(sp):
                for dst_, src_ in loads:
                    sp.dma_start(dst_, src_).then_inc(loaded.h, 16)
                def indices(i, b):
                    sp.dma_start(at[:, b, :], start_d[:, bass.ds((i * 2 + b) * NB, NB)]).then_inc(at_loaded[b].h, 16)

                def table(i, b):
                    sp.wait_ge(*q_ready[b](i + 1))
                    sp.dma_start(by_node(g_tab)[:, bass.ds((i * 2 + b) * NB, NB), :],
                                 gt[:, bass.ds((i * 2 + b) * NB, NB), :]).then_inc(q_stored[b].h, 16)

                indices(0, 0)
                indices(0, 1)
                with sp.Fori(0, NBLK // 2 - 1) as i:
                    for b in range(2):
                        table(i, b)
                        sp.wait_ge(*scattered[b](i * (16 * NB) + 16 * NB))
                        indices(i + 1, b)
                for b in range(2):
                    table(NBLK // 2 - 1, b)
                for b in range(2):
                    sp.wait_ge(*q_stored[b](16 * NBLK // 2))
                    sp.wait_ge(*scattered[b](16 * NB * NBLK // 2))

            @block.gpsimd
            def _(pool):
                with pool.Fori(0, NBLK // 2) as i:
                    for b in range(2):
                        pool.wait_ge(*at_loaded[b](i * 16 + 16))
                        pool.nop(nofuse=True)
                        pool.wait_ge(*q_ready[b](i + 1))
                        pool.nop(nofuse=True)
                        for k in range(NB):
                            nc.gpsimd.indirect_dma_start(ad_start, indexed(at[:, b, k:k + 1]), adq[:, b, k, :],
                                                         None).then_inc(scattered[b].h, 16)

            @block.scalar
            def _(act):
                def take(i, b):
                    act.wait_ge(*turned[b](i))
                    act.activation(hs[:, b], h[:, bass.ds((i * 2 + b) * NB, NB), :], ACT.Copy)\
                        .then_inc(hs_ready[b].h, 1)

                def rows_out(i, b):
                    act.wait_ge(*mixed[b](i + 1))
                    act.wait_ge(*scattered[b](i * (16 * NB)))
                    act.wait_ge(*q_stored[b](i * 16))
                    cols = bass.ds((i * 2 + b) * NB, NB)
                    act.activation(gt[:, cols, :], ps_q[b][:, 0:NB, 0:TG], ACT.Copy)
                    act.activation(adq[:, b], ps_q[b][:, 0:NB, D + HG:TG], ACT.Copy).then_inc(q_ready[b].h, 1)

                take(0, 0)
                take(0, 1)
                with act.Fori(0, NBLK // 2 - 1) as i:
                    for b in range(2):
                        rows_out(i, b)
                        take(i + 1, b)
                for b in range(2):
                    rows_out(NBLK // 2 - 1, b)

            @block.vector
            def _(v):
                v.wait_ge(*loaded(16 * len(loads)))
                v.tensor_tensor(pr[:], wg[:, 0:D].unsqueeze(1).to_broadcast([D, 2, D]), av[:], ALU.mult)\
                    .then_inc(ch.h, 1)
                v.wait_ge(*ch.before("sum"))
                if heads == HG:
                    v.reduce_sum(wg[:, D:TG], pr[:].rearrange("p s (h j) -> p (s h) j", h=HG), axis=AX.X)\
                        .then_inc(ch.h, 1)
                else:
                    for k in range(HG):
                        last = v.reduce_sum(wg[:, D + k:TG:HG], pr[:], axis=AX.X)
                    last.then_inc(ch.h, 1)
                if edge:
                    v.wait_ge(*ch.before("eprod"))
                    v.tensor_tensor(wev[:], wev[:], aev[:], ALU.mult).then_inc(ch.h, 1)
                    v.wait_ge(*ch.before("esum"))
                    v.reduce_sum(m8[:], wev[:].rearrange("p (h j) -> p h j", h=HG), axis=AX.X).then_inc(ch.h, 1)
                    v.wait_ge(*ch.before("spread"))
                    v.tensor_copy(bd[:].rearrange("p (h t) -> p h t", h=HG),
                                  m8[:].unsqueeze(2).to_broadcast([P, HG, G])).then_inc(ch.h, 1)
                with v.Fori(0, NBLK // 2) as i:
                    for b in range(2):
                        v.wait_ge(*turned[b](i + 1))
                        v.wait_ge(*mixed[b](i))
                        v.tensor_copy(ht[:, b], ps_h[b][0:D, 0:NB, :]).then_inc(ht_ready[b].h, 1)

            @block.tensor
            def _(pe):
                pe.wait_ge(*ch.upto(len(ch)))
                def turn(i, b):
                    pe.wait_ge(*hs_ready[b](i + 1))
                    pe.nop(nofuse=True)
                    pe.wait_ge(*ht_ready[b](i))
                    pe.nop(nofuse=True)
                    for k in range(NB):
                        last = nc.tensor.transpose(ps_h[b][0:D, k, :], hs[:, b, k, :], ident[:])
                    last.then_inc(turned[b].h, 1)

                def mix(i, b):
                    pe.wait_ge(*ht_ready[b](i + 1))
                    pe.nop(nofuse=True)
                    pe.wait_ge(*q_ready[b](i))
                    pe.nop(nofuse=True)
                    for k in range(NB):
                        last = nc.tensor.matmul(ps_q[b][:, k, 0:TG], ht[:, b, k, :], wg[:], start=True, stop=True)
                    last.then_inc(mixed[b].h, 1)

                turn(0, 0)
                turn(0, 1)
                with pe.Fori(0, NBLK // 2 - 1) as i:
                    for b in range(2):
                        mix(i, b)
                        turn(i + 1, b)
                for b in range(2):
                    mix(NBLK // 2 - 1, b)
        st.close()

    def block_diagonal(tag, bd):
        st = Stage(nc, tag, signals)
        cut = st.sem("cut", 2)
        v3 = bd[:].rearrange("p (h t) -> p h t", h=HG)
        with nc.Block() as block:
            @block.gpsimd
            def _(pool):
                nc.gpsimd.affine_select(out=v3, in_=v3, compare_op=ALU.is_ge, fill=0.0, base=0,
                                        pattern=[[0, HG], [-8, G]], channel_multiplier=1).then_inc(cut.h, 1)
                pool.wait_ge(*cut(1))
                nc.gpsimd.affine_select(out=v3, in_=v3, compare_op=ALU.is_ge, fill=0.0, base=7,
                                        pattern=[[0, HG], [8, G]], channel_multiplier=-1).then_inc(cut.h, 1)
                pool.wait_ge(*cut(2))
        st.close()

    def gat_edges(tag, rows, bd=None):
        H, J1 = HG, JG + 1
        F = H * J1
        st = Stage(nc, tag, signals)
        at = st.sb("at", [P, 2, G], I32)
        y = st.sb("y", [P, 2, G, TG])
        ad_raw, ad = st.sb("ad_raw", [P, ET, H]), st.sb("ad", [P, H, ET])
        s0, s, fm = st.sb("s0", [P, H, G]), st.sb("s", [P, H, G]), st.sb("fm", [P, 2, H, G + 1])
        de, ex = st.sb("de", [P, 2, H, G]), st.sb("ex", [P, 2, H, G])
        r, w_in = st.sb("r", [P, H, J1, G + 1]), st.sb("w_in", [P, H, J1, G + 1])
        acc = st.sb("acc", [P, 2, F, G + 1])
        row = st.sb("row", [P, 2, G, TG])
        g0 = st.sb("g0", [P, TG])
        half = NG // 2
        if bd is not None:
            ea = st.sb("ea", [P, 2, P])
            ps_e = [st.ps(f"ps_e{b}", [P, 512]) for b in range(2)]
        ready = st.sem("edges_ready", 3)
        g0_got, ad_loaded = st.dma("q0_got", 16), st.dma("ad_loaded", 16)
        ad_filled = st.sem("ad_filled", H)
        at_loaded = st.dma_slots("at_loaded", 16 * half)
        if bd is not None:
            e_loaded, e_scored = st.dma_slots("e_loaded", 16 * half), st.slots("e_scored", half)
            eadded = st.sem("eadded", NG)
        gathered = st.dma_slots(f"gathered_{tag}_", 16 * G * half)
        weighted, row_ready, den_in = (st.slots(n, half) for n in ("weighted", "row_ready", "den_in"))
        row_stored = st.dma_slots("row_stored", 16 * half)
        added, scored = (st.sem(n, NG) for n in ("added", "scored"))
        maxed, m_carried, shifted, exps, r_ready = (st.sem(n, NG) for n in
                                                    ("maxed", "m_carried", "shifted", "exps", "r_ready"))
        summed, carried = (st.sem(n, NG) for n in ("summed", "carried"))
        differed = st.sem("differed", NG)

        with nc.Block() as block:
            @block.sync
            def _(sp):
                sp.dma_start(ad_raw[:], by_edge(ad_start)).then_inc(ad_loaded.h, 16)
                with sp.Fori(0, half) as i:
                    for b in range(2):
                        g = i * 2 + b
                        sp.wait_ge(*weighted[b](i))
                        sp.dma_start(at[:, b], a["src"].rearrange("(p t) -> p t", p=P)[:, bass.ds(g * G, G)])\
                            .then_inc(at_loaded[b].h, 16)
                        if bd is not None:
                            sp.wait_ge(*e_scored[b](i))
                            sp.dma_start(ea[:, b, :], a["edge_attr_8"][bass.ds(g * P, P), :])\
                                .then_inc(e_loaded[b].h, 16)

            @block.gpsimd
            def _(pool):
                nc.gpsimd.indirect_dma_start(g0[:], None, g_tab, indexed(dst0[:])).then_inc(g0_got.h, 16)
                with pool.Fori(0, half) as i:
                    for b in range(2):
                        pool.wait_ge(*at_loaded[b](i * 16 + 16))
                        pool.nop(nofuse=True)
                        pool.wait_ge(*weighted[b](i))
                        pool.nop(nofuse=True)
                        for k in range(G):
                            nc.gpsimd.indirect_dma_start(y[:, b, k, :], None, g_tab, indexed(at[:, b, k:k + 1]))\
                                .then_inc(gathered[b].h, 16)

            if bd is not None:
                @block.tensor
                def _(pe):
                    with pe.Fori(0, half) as i:
                        for b in range(2):
                            pe.wait_ge(*weighted[b](i))
                            pe.nop(nofuse=True)
                            pe.wait_ge(*e_loaded[b](i * 16 + 16))
                            pe.nop(nofuse=True)
                            nc.tensor.matmul(ps_e[b][:, 0:H * G], ea[:, b, :], bd[:], start=True,
                                             stop=True).then_inc(e_scored[b].h, 1)

            @block.vector
            def _(v):
                v.memset(r[:, :, :, 0:1], 0.0).then_inc(ready.h, 1)
                v.memset(w_in[:, :, :, 0:1], 0.0).then_inc(ready.h, 1)
                v.memset(fm[:, 0, :, 0:1], -BIG).then_inc(ready.h, 1)
                v.wait_ge(*g0_got(16))
                v.wait_ge(*ad_loaded(16))
                for k in range(H):
                    v.tensor_tensor_scan(ad[:, k, :], same[:], ad_raw[:, :, k], g0[:, D + H + k:D + H + k + 1],
                                         ALU.mult, ALU.add).then_inc(ad_filled.h, 1)
                v.wait_ge(*ad_filled(H))
                v.wait_ge(*ready(3))
                with v.Fori(0, half) as i:
                    for b in range(2):
                        g = i * 2 + b
                        cols = bass.ds(g * G, G)
                        v.wait_ge(*gathered[b](i * (16 * G) + 16 * G))
                        v.tensor_tensor(s0[:], y[:, b, :, D:D + H].rearrange("p t h -> p h t"), ad[:, :, cols],
                                        ALU.add).then_inc(added.h, 1)
                        v.wait_ge(*added(g + 1))
                        if bd is not None:
                            v.wait_ge(*e_scored[b](i + 1))
                            v.tensor_tensor(s0[:], s0[:], ps_e[b][:, 0:H * G].rearrange("p (h t) -> p h t", h=H),
                                            ALU.add).then_inc(eadded.h, 1)
                            v.wait_ge(*eadded(g + 1))
                        v.scalar_tensor_tensor(out=s[:], in0=s0[:], scalar=SLOPE, in1=s0[:], op0=ALU.mult,
                                               op1=ALU.max).then_inc(scored.h, 1)
                        v.wait_ge(*scored(g + 1))
                        v.wait_ge(*m_carried(g))
                        for k in range(H):
                            last = v.tensor_tensor_scan(fm[:, b, k, 1:G + 1], pen[:, cols], s[:, k, :],
                                                        fm[:, b, k, 0:1], ALU.add, ALU.max)
                        last.then_inc(maxed.h, 1)
                        v.wait_ge(*maxed(g + 1))
                        if b == 0:
                            v.wait_ge(*row_ready[1](i))
                        else:
                            v.wait_ge(*row_ready[0](i + 1))
                        v.tensor_copy(fm[:, 1 - b, :, 0:1], fm[:, b, :, G:G + 1]).then_inc(m_carried.h, 1)
                        v.tensor_tensor(de[:, 0], fm[:, b, :, 0:G], fm[:, b, :, 1:G + 1], ALU.subtract)\
                            .then_inc(differed.h, 1)
                        v.tensor_tensor(de[:, 1], s[:], fm[:, b, :, 1:G + 1], ALU.subtract)
                        v.wait_ge(*differed(g + 1))
                        v.tensor_tensor(de[:, 0], de[:, 0], pen[:, cols].unsqueeze(1).to_broadcast([P, H, G]),
                                        ALU.add).then_inc(shifted.h, 1)
                        v.wait_ge(*exps(g + 1))
                        v.wait_ge(*carried(g))
                        v.tensor_copy(w_in[:, :, JG, 1:G + 1], ex[:, 1]).then_inc(den_in[b].h, 1)
                        for k in range(H):
                            last = v.tensor_tensor(w_in[:, k, 0:JG, 1:G + 1],
                                                   y[:, b, :, JG * k:JG * (k + 1)].rearrange("p t j -> p j t"),
                                                   ex[:, 1, k, :].unsqueeze(1).to_broadcast([P, JG, G]), ALU.mult)
                        last.then_inc(weighted[b].h, 1)
                        v.wait_ge(*weighted[b](i + 1))
                        v.wait_ge(*r_ready(g + 1))
                        v.wait_ge(*row_ready[b](i))
                        v.tensor_tensor_scan(acc[:, b].rearrange("p f t -> p (f t)"),
                                             r[:].rearrange("p h j t -> p (h j t)"),
                                             w_in[:].rearrange("p h j t -> p (h j t)"), 0.0,
                                             ALU.mult, ALU.add).then_inc(summed.h, 1)
                        v.wait_ge(*summed(g + 1))
                        v.tensor_copy(w_in[:].rearrange("p h j t -> p (h j) t")[:, :, 0:1], acc[:, b, :, G:G + 1])\
                            .then_inc(carried.h, 1)
                v.wait_ge(*carried(NG))
                v.tensor_copy(carry_v[:, 0:F], w_in[:].rearrange("p h j t -> p (h j) t")[:, :, 0])
                v.tensor_copy(carry_m[:], fm[:, 0, :, 0])

            @block.scalar
            def _(act):
                def weights(i, b):
                    g = i * 2 + b
                    act.wait_ge(*shifted(g + 1))
                    if b == 1:
                        act.wait_ge(*weighted[0](i + 1))
                    else:
                        act.wait_ge(*weighted[1](i))
                    act.activation(ex[:], de[:], ACT.Exp).then_inc(exps.h, 1)
                    act.wait_ge(*exps(g + 1))
                    act.wait_ge(*summed(g))
                    act.activation(r[:, :, :, 1:G + 1], ex[:, 0].unsqueeze(2).to_broadcast([P, H, J1, G]), ACT.Copy)\
                        .then_inc(r_ready.h, 1)

                def send(i, b):
                    g = i * 2 + b
                    act.wait_ge(*summed(g + 1))
                    act.wait_ge(*row_stored[b](i * 16))
                    act.activation(row[:, b, :, F:F + H], fm[:, b, :, 1:G + 1].rearrange("p h t -> p t h"), ACT.Copy)
                    act.activation(row[:, b, :, 0:F], acc[:, b, :, 1:G + 1].rearrange("p f t -> p t f"), ACT.Copy)\
                        .then_inc(row_ready[b].h, 1)
                    act.wait_ge(*row_ready[b](i + 1))
                    act.dma_start(by_edge(rows)[:, bass.ds(g * G, G), :], row[:, b]).then_inc(row_stored[b].h, 16)

                with act.Fori(0, half) as i:
                    for b in range(2):
                        weights(i, b)
                        send(i, b)
                for b in range(2):
                    act.wait_ge(*row_stored[b](16 * half))
        st.close()

    def finish_gat(tag, rows, bias, gt=None, last=False, norm=False):
        J1 = JG + 1
        st = Stage(nc, tag, signals)
        at = st.sb("at", [P, 2, NW], I32)
        got = st.sb("got", [P, 2, NW, TG])
        bv = st.sb("bv", [P, D])
        e, m = st.sb("e", [P, NW, HG]), st.sb("m", [P, NW, HG])
        de, ex = st.sb("de", [P, 2, NW, HG]), st.sb("ex", [P, 2, NW, HG])
        den, rd = st.sb("den", [P, NW, HG]), st.sb("rd", [P, NW, HG])
        o, own = st.sb("o", [P, NW, D]), st.sb("own", [P, NW, D])
        nrm = st.sb("nrm", [P, NW])
        if gt is None:
            names = "den inv inv_has mean bias done"
        else:
            names = "e leak m1 m2 mx d1 d2 exp den1 den2 eps inv accw own sum mean bias "
            names += "sq ssum root nmax ninv scaled done" if last else "neg elu_exp less1 done"
        if norm:
            names += " ln_take ln_sum ln_scale ln_centre ln_square ln_var ln_root ln_inv ln_done"
            mu = st.sb("mu", [P, NW])
        names = names.split()
        steps = st.sem("node_steps", len(names) * NWBLK)
        loaded = st.dma("w_loaded", 16)
        at_loaded = st.wide_slots(st.dma, "at_loaded", 16)
        node_got = st.wide_slots(st.dma, "node_got", 16 * NW)
        used = st.wide_slots(st.sem, "node_used", 1)

        def before(g, name):
            return steps(g * len(names) + names.index(name))

        def wide(t):
            return t.unsqueeze(3).to_broadcast([P, NW, HG, JG])

        def split(t):
            return t.rearrange("p k (h j) -> p k h j", h=HG)

        with nc.Block() as block:
            @block.sync
            def _(sp):
                sp.dma_start(bv[:], row_of(bias, D)).then_inc(loaded.h, 16)
                def body(i, b):
                    sp.wait_ge(*used[b](i))
                    sp.dma_start(at[:, b, :], last_d[:, bass.ds((i * 2 + b) * NW, NW)])\
                        .then_inc(at_loaded[b].h, 16)

                over_wide_blocks(sp, body)

            @block.gpsimd
            def _(pool):
                def body(i, b):
                    pool.wait_ge(*at_loaded[b](i * 16 + 16))
                    pool.nop(nofuse=True)
                    pool.wait_ge(*used[b](i))
                    pool.nop(nofuse=True)
                    for k in range(NW):
                        nc.gpsimd.indirect_dma_start(got[:, b, k, :], None, rows, indexed(at[:, b, k:k + 1]))\
                            .then_inc(node_got[b].h, 16)

                over_wide_blocks(pool, body)

            @block.scalar
            def _(act):
                def body(i, b):
                    g = i * 2 + b
                    if gt is not None:
                        act.wait_ge(*before(g, "exp"))
                        act.activation(ex[:], de[:], ACT.Exp).then_inc(steps.h, 1)
                    if last:
                        act.wait_ge(*before(g, "root"))
                        act.activation(nrm[:], nrm[:], ACT.Sqrt).then_inc(steps.h, 1)
                    elif gt is not None:
                        act.wait_ge(*before(g, "elu_exp"))
                        act.activation(own[:], own[:], ACT.Exp).then_inc(steps.h, 1)
                    if norm:
                        act.wait_ge(*before(g, "ln_square"))
                        act.activation(own[:], o[:], ACT.Square).then_inc(steps.h, 1)
                        act.wait_ge(*before(g, "ln_root"))
                        act.activation(mu[:], mu[:], ACT.Sqrt, bias=eps[:], scale=1.0 / D).then_inc(steps.h, 1)

                over_wide_blocks(act, body)

            @block.vector
            def _(v):
                v.wait_ge(*loaded(16))
                def body(i, b):
                    g = i * 2 + b
                    cols = bass.ds(g * NW, NW)


                    parts = got[:, b, :, 0:HG * J1].rearrange("p k (h j) -> p k h j", h=HG)
                    acc, dn, mx = parts[:, :, :, 0:JG], parts[:, :, :, JG], got[:, b, :, HG * J1:TG]
                    has_w = has[:, cols].unsqueeze(2).to_broadcast([P, NW, HG])
                    v.wait_ge(*node_got[b](i * (16 * NW) + 16 * NW))
                    if gt is None:
                        v.wait_ge(*before(g, "den"))
                        v.tensor_scalar(rd[:], dn, TINY, None, ALU.max).then_inc(steps.h, 1)
                        v.wait_ge(*before(g, "inv"))
                        v.reciprocal(rd[:], rd[:]).then_inc(steps.h, 1)
                        v.wait_ge(*before(g, "inv_has"))
                        v.tensor_tensor(rd[:], rd[:], has_w, ALU.mult).then_inc(steps.h, 1)
                        v.wait_ge(*before(g, "mean"))
                        v.tensor_tensor(split(o[:]), acc, wide(rd[:]), ALU.mult).then_inc(steps.h, 1)
                    else:
                        own_h, own_s, own_t = (gt[:, cols, 0:D], gt[:, cols, D:D + HG], gt[:, cols, D + HG:TG])
                        hneg_w = hneg[:, cols].unsqueeze(2).to_broadcast([P, NW, HG])
                        v.wait_ge(*before(g, "e"))
                        v.tensor_tensor(e[:], own_s, own_t, ALU.add).then_inc(steps.h, 1)
                        v.wait_ge(*before(g, "leak"))
                        v.scalar_tensor_tensor(out=e[:], in0=e[:], scalar=SLOPE, in1=e[:],
                                               op0=ALU.mult, op1=ALU.max).then_inc(steps.h, 1)
                        v.wait_ge(*before(g, "m1"))
                        v.tensor_tensor(m[:], mx, has_w, ALU.mult).then_inc(steps.h, 1)
                        v.wait_ge(*before(g, "m2"))
                        v.tensor_tensor(m[:], m[:], hneg_w, ALU.add).then_inc(steps.h, 1)
                        v.wait_ge(*before(g, "mx"))
                        v.tensor_tensor(rd[:], m[:], e[:], ALU.max).then_inc(steps.h, 1)
                        v.wait_ge(*before(g, "d1"))
                        v.tensor_tensor(de[:, 0], m[:], rd[:], ALU.subtract).then_inc(steps.h, 1)
                        v.wait_ge(*before(g, "d2"))
                        v.tensor_tensor(de[:, 1], e[:], rd[:], ALU.subtract).then_inc(steps.h, 1)
                        v.wait_ge(*before(g, "den1"))
                        v.tensor_tensor(den[:], dn, ex[:, 0], ALU.mult).then_inc(steps.h, 1)
                        v.wait_ge(*before(g, "den2"))
                        v.tensor_tensor(den[:], den[:], ex[:, 1], ALU.add).then_inc(steps.h, 1)
                        v.wait_ge(*before(g, "eps"))
                        v.tensor_scalar(den[:], den[:], 1e-16, None, ALU.add).then_inc(steps.h, 1)
                        v.wait_ge(*before(g, "inv"))
                        v.reciprocal(rd[:], den[:]).then_inc(steps.h, 1)
                        v.wait_ge(*before(g, "accw"))
                        v.tensor_tensor(split(o[:]), acc, wide(ex[:, 0]), ALU.mult).then_inc(steps.h, 1)
                        v.wait_ge(*before(g, "own"))
                        v.tensor_tensor(split(own[:]), split(own_h), wide(ex[:, 1]), ALU.mult).then_inc(steps.h, 1)
                        v.wait_ge(*before(g, "sum"))
                        v.tensor_tensor(o[:], o[:], own[:], ALU.add).then_inc(steps.h, 1)
                        v.wait_ge(*before(g, "mean"))
                        v.tensor_tensor(split(o[:]), split(o[:]), wide(rd[:]), ALU.mult).then_inc(steps.h, 1)
                    v.wait_ge(*before(g, "bias"))
                    v.tensor_tensor(o[:], o[:], bv[:].unsqueeze(1).to_broadcast([P, NW, D]), ALU.add)\
                        .then_inc(steps.h, 1)
                    if gt is None:
                        v.wait_ge(*before(g, "done"))
                        v.tensor_tensor(x[:, cols, :], x[:, cols, :], o[:], ALU.add).then_inc(steps.h, 1)
                    elif last:
                        v.wait_ge(*before(g, "sq"))
                        v.tensor_tensor(own[:], o[:], o[:], ALU.mult).then_inc(steps.h, 1)
                        v.wait_ge(*before(g, "ssum"))
                        v.reduce_sum(nrm[:], own[:], axis=AX.X).then_inc(steps.h, 1)
                        v.wait_ge(*before(g, "nmax"))
                        v.tensor_scalar(nrm[:], nrm[:], 1e-12, None, ALU.max).then_inc(steps.h, 1)
                        v.wait_ge(*before(g, "ninv"))
                        v.reciprocal(nrm[:], nrm[:]).then_inc(steps.h, 1)
                        v.wait_ge(*before(g, "scaled"))
                        v.tensor_tensor(o[:], o[:],
                                        nrm[:].unsqueeze(2).to_broadcast([P, NW, D]), ALU.mult)\
                            .then_inc(steps.h, 1)
                        v.wait_ge(*before(g, "done"))
                        v.tensor_tensor(x[:, cols, :], x[:, cols, :], o[:], ALU.add).then_inc(steps.h, 1)
                    else:
                        v.wait_ge(*before(g, "neg"))
                        v.tensor_scalar(own[:], o[:], 0.0, None, ALU.min).then_inc(steps.h, 1)
                        v.wait_ge(*before(g, "less1"))
                        v.tensor_scalar(own[:], own[:], -1.0, None, ALU.add).then_inc(steps.h, 1)
                        v.wait_ge(*before(g, "done"))
                        v.scalar_tensor_tensor(out=h[:, cols, :], in0=o[:], scalar=0.0,
                                               in1=own[:], op0=ALU.max, op1=ALU.add).then_inc(steps.h, 1)
                    if norm:
                        v.wait_ge(*before(g, "ln_take"))
                        v.tensor_scalar(own[:], x[:, cols, :], 1.0, None, ALU.mult).then_inc(steps.h, 1)
                        v.wait_ge(*before(g, "ln_sum"))
                        v.reduce_sum(mu[:], own[:], axis=AX.X).then_inc(steps.h, 1)
                        v.wait_ge(*before(g, "ln_scale"))
                        v.tensor_scalar(mu[:], mu[:], 1.0 / D, None, ALU.mult).then_inc(steps.h, 1)
                        v.wait_ge(*before(g, "ln_centre"))
                        v.tensor_tensor(o[:], own[:], mu[:].unsqueeze(2).to_broadcast([P, NW, D]),
                                        ALU.subtract).then_inc(steps.h, 1)
                        v.wait_ge(*before(g, "ln_var"))
                        v.reduce_sum(mu[:], own[:], axis=AX.X).then_inc(steps.h, 1)
                        v.wait_ge(*before(g, "ln_inv"))
                        v.reciprocal(mu[:], mu[:]).then_inc(steps.h, 1)
                        v.wait_ge(*before(g, "ln_done"))
                        v.scalar_tensor_tensor(out=h[:, cols, :], in0=o[:], scalar=0.0,
                                               in1=mu[:].unsqueeze(2).to_broadcast([P, NW, D]),
                                               op0=ALU.max, op1=ALU.mult).then_inc(steps.h, 1)
                    v.wait_ge(*steps(g * len(names) + len(names)))
                    v.sem_inc(used[b].h, 1)

                over_wide_blocks(v, body)
        st.close()

    def store_table(tag):
        st = Stage(nc, tag, signals)
        tab = st.dma("tab_stored", 16)
        with nc.Block() as block:
            @block.sync
            def _(sp):
                sp.dma_start(by_node(h_tab), h[:]).then_inc(tab.h, 16)
                sp.wait_ge(*tab(16))
        st.close()

    def pna_edges(tag, rows):
        F = 2 * D
        st = Stage(nc, tag, signals)
        at = st.sb("at", [P, 2, G], I32)
        y, ea = st.sb("y", [P, 2, G, D]), st.sb("ea", [P, 2, G, D])
        mask, penm = st.sb("mask", [P, 2, F, G + 1]), st.sb("penm", [P, 2, F, G + 1])
        su, mu = st.sb("su", [P, F, G + 1]), st.sb("mu", [P, F, G + 1])
        acc_s, acc_m = st.sb("acc_s", [P, F, G + 1]), st.sb("acc_m", [P, F, G + 1])
        row = st.sb("row", [P, 2, G, 2 * F])
        half = NG // 2
        ready = st.sem("edges_ready", 4)
        mask_ready = st.slots("mask_ready", half)
        at_loaded, e_loaded = (st.dma_slots(n, 16 * half) for n in ("at_loaded", "e_loaded"))
        gathered = st.dma_slots(f"gathered_{tag}_", 16 * G * half)
        added = st.slots("u_added", half)
        row_ready, row_stored = st.slots("row_ready", half), st.dma_slots("row_stored", 16 * half)
        squared, copied = (st.sem(n, NG) for n in ("squared", "u_copied"))
        summed, maxed, s_carried, m_carried = (st.sem(n, NG) for n in
                                               ("summed", "maxed", "carried", "m_carried"))

        with nc.Block() as block:
            @block.sync
            def _(sp):
                with sp.Fori(0, half) as i:
                    for b in range(2):
                        t0 = (i * 2 + b) * G
                        sp.wait_ge(*added[b](i))
                        sp.dma_start(at[:, b], a["src"].rearrange("(p t) -> p t", p=P)[:, bass.ds(t0, G)])\
                            .then_inc(at_loaded[b].h, 16)
                        sp.wait_ge(*added[b](i))
                        sp.dma_start(ea[:, b], a["edge_attr_64"].rearrange("(p t) f -> p t f", p=P)[:, bass.ds(t0, G), :])\
                            .then_inc(e_loaded[b].h, 16)

            @block.gpsimd
            def _(pool):
                with pool.Fori(0, half) as i:
                    for b in range(2):
                        pool.wait_ge(*at_loaded[b](i * 16 + 16))
                        pool.nop(nofuse=True)
                        pool.wait_ge(*added[b](i))
                        pool.nop(nofuse=True)
                        for k in range(G):
                            nc.gpsimd.indirect_dma_start(y[:, b, k, :], None, h_tab, indexed(at[:, b, k:k + 1]))\
                                .then_inc(gathered[b].h, 16)

            @block.vector
            def _(v):
                v.memset(mask[:, :, :, 0:1], 0.0).then_inc(ready.h, 1)
                v.memset(penm[:, :, :, 0:1], -BIG).then_inc(ready.h, 1)
                v.memset(su[:, :, 0:1], 0.0).then_inc(ready.h, 1)
                v.memset(mu[:, :, 0:1], -BIG).then_inc(ready.h, 1)
                v.wait_ge(*ready(4))
                with v.Fori(0, half) as i:
                    for b in range(2):
                        g = i * 2 + b
                        v.wait_ge(*gathered[b](i * (16 * G) + 16 * G))
                        v.wait_ge(*e_loaded[b](i * 16 + 16))
                        v.wait_ge(*copied(g))
                        v.tensor_tensor(su[:, 0:D, 1:G + 1], y[:, b].rearrange("p t f -> p f t"),
                                        ea[:, b].rearrange("p t f -> p f t"), ALU.add).then_inc(added[b].h, 1)
                        if b == 0:
                            v.wait_ge(*row_ready[1](i))
                        else:
                            v.wait_ge(*row_ready[0](i + 1))
                        v.wait_ge(*squared(g + 1))
                        v.wait_ge(*mask_ready[b](i + 1))
                        v.wait_ge(*s_carried(g))
                        v.tensor_tensor_scan(acc_s[:].rearrange("p f t -> p (f t)"),
                                             mask[:, b].rearrange("p f t -> p (f t)"),
                                             su[:].rearrange("p f t -> p (f t)"), 0.0,
                                             ALU.mult, ALU.add).then_inc(summed.h, 1)
                        v.wait_ge(*copied(g + 1))
                        v.wait_ge(*m_carried(g))
                        v.tensor_tensor_scan(acc_m[:].rearrange("p f t -> p (f t)"),
                                             penm[:, b].rearrange("p f t -> p (f t)"),
                                             mu[:].rearrange("p f t -> p (f t)"), 0.0,
                                             ALU.add, ALU.max).then_inc(maxed.h, 1)
                        v.wait_ge(*summed(g + 1))
                        v.tensor_copy(su[:, :, 0:1], acc_s[:, :, G:G + 1]).then_inc(s_carried.h, 1)
                        v.wait_ge(*maxed(g + 1))
                        v.tensor_copy(mu[:, :, 0:1], acc_m[:, :, G:G + 1]).then_inc(m_carried.h, 1)
                v.wait_ge(*s_carried(NG))
                v.wait_ge(*m_carried(NG))
                v.tensor_copy(carry_v[:, 0:F], su[:, :, 0])
                v.tensor_copy(carry_v[:, F:2 * F], mu[:, :, 0])

            @block.scalar
            def _(act):
                def masks_of(i, b):
                    cols = bass.ds((i * 2 + b) * G, G)
                    act.activation(mask[:, b, :, 1:G + 1], same[:, cols].unsqueeze(1).to_broadcast([P, F, G]), ACT.Copy)
                    act.activation(penm[:, b, :, 1:G + 1], pen[:, cols].unsqueeze(1).to_broadcast([P, F, G]), ACT.Copy)\
                        .then_inc(mask_ready[b].h, 1)

                def operands(i, b):
                    g = i * 2 + b
                    act.wait_ge(*summed(g))
                    act.wait_ge(*maxed(g))
                    act.wait_ge(*added[b](i + 1))
                    act.activation(su[:, D:F, 1:G + 1], su[:, 0:D, 1:G + 1], ACT.Square).then_inc(squared.h, 1)
                    act.activation(mu[:, 0:D, 1:G + 1], su[:, 0:D, 1:G + 1], ACT.Copy)
                    act.activation(mu[:, D:F, 1:G + 1], su[:, 0:D, 1:G + 1], ACT.Copy, scale=-1.0)\
                        .then_inc(copied.h, 1)

                def send(i, b):
                    g = i * 2 + b
                    act.wait_ge(*summed(g + 1))
                    act.wait_ge(*row_stored[b](i * 16))
                    act.activation(row[:, b, :, 0:F], acc_s[:, :, 1:G + 1].rearrange("p f t -> p t f"), ACT.Copy)
                    act.wait_ge(*maxed(g + 1))
                    act.activation(row[:, b, :, F:2 * F], acc_m[:, :, 1:G + 1].rearrange("p f t -> p t f"), ACT.Copy)\
                        .then_inc(row_ready[b].h, 1)
                    act.wait_ge(*row_ready[b](i + 1))
                    act.dma_start(by_edge(rows)[:, bass.ds(g * G, G), :], row[:, b]).then_inc(row_stored[b].h, 16)

                masks_of(0, 0)
                operands(0, 0)
                with act.Fori(0, half - 1) as i:
                    masks_of(i, 1)
                    send(i, 0)
                    operands(i, 1)
                    masks_of(i + 1, 0)
                    send(i, 1)
                    operands(i + 1, 0)
                masks_of(half - 1, 1)
                send(half - 1, 0)
                operands(half - 1, 1)
                send(half - 1, 1)
                for b in range(2):
                    act.wait_ge(*row_stored[b](16 * half))
        st.close()

    def join_pna(tag, rows):
        F = 2 * D
        st = Stage(nc, tag, signals)
        got = st.sb("got", [P, 2 * F])
        vt, mt = st.sb("vt", [F, P]), st.sb("mt", [F, P])
        ms, vs_ = st.sb("ms", [F, P + 1]), st.sb("vs", [F, P + 1])
        vin, min_ = st.sb("vin", [P, F]), st.sb("min", [P, F])
        pa, pb = st.ps("pa", [P, 512]), st.ps("pb", [P, 512])
        got_row, put_row = st.dma("fix_got", 16), st.dma("fix_put", 16)
        ch = st.chain("fix_steps", """turn_v turn_m copy_v copy_m edge_m edge_v scan_m scan_v back_v back_m
            vin min sum_new max_new""")

        with nc.Block() as block:
            @block.gpsimd
            def _(pool):
                nc.gpsimd.indirect_dma_start(got[:], None, rows, indexed(fix_at[:])).then_inc(got_row.h, 16)
                pool.wait_ge(*ch.upto(len(ch)))
                nc.gpsimd.indirect_dma_start(rows, indexed(fix_at[:]), got[:], None).then_inc(put_row.h, 16)
                pool.wait_ge(*put_row(16))

            @block.tensor
            def _(pe):
                for name, dst_, src_ in (("turn_v", pa[:, 0:P], carry_v[:, 0:F]), ("turn_m", pb[:, 0:P], carry_v[:, F:2 * F]),
                                         ("back_v", pa[:, 0:F], vs_[:, 0:P]), ("back_m", pb[:, 0:F], ms[:, 0:P])):
                    pe.wait_ge(*ch.before(name))
                    nc.tensor.transpose(dst_, src_, ident[:]).then_inc(ch.h, 1)

            @block.vector
            def _(v):

                v.wait_ge(*ch.before("copy_v"))
                v.tensor_copy(vt[:], pa[:, 0:P]).then_inc(ch.h, 1)
                v.wait_ge(*ch.before("copy_m"))
                v.tensor_copy(mt[:], pb[:, 0:P]).then_inc(ch.h, 1)
                v.wait_ge(*ch.before("edge_m"))
                v.memset(ms[:, 0:1], -BIG).then_inc(ch.h, 1)
                v.wait_ge(*ch.before("edge_v"))
                v.memset(vs_[:, 0:1], 0.0).then_inc(ch.h, 1)
                v.wait_ge(*ch.before("scan_m"))
                v.tensor_tensor_scan(ms[:, 1:P + 1], whole_pen[:], mt[:], -BIG, ALU.add, ALU.max).then_inc(ch.h, 1)
                v.wait_ge(*ch.before("scan_v"))
                v.tensor_tensor_scan(vs_[:, 1:P + 1], whole_t[:], vt[:], 0.0, ALU.mult, ALU.add).then_inc(ch.h, 1)
                v.wait_ge(*ch.before("vin"))
                v.tensor_scalar(vin[:], pa[:, 0:F], cont[:, 0:1], None, ALU.mult).then_inc(ch.h, 1)
                v.wait_ge(*ch.before("min"))
                v.tensor_scalar(min_[:], pb[:, 0:F], contpen[:, 0:1], None, ALU.add).then_inc(ch.h, 1)
                v.wait_ge(*got_row(16))
                v.wait_ge(*ch.before("sum_new"))
                v.tensor_tensor(got[:, 0:F], got[:, 0:F], vin[:], ALU.add).then_inc(ch.h, 1)
                v.wait_ge(*ch.before("max_new"))
                v.tensor_tensor(got[:, F:2 * F], got[:, F:2 * F], min_[:], ALU.max).then_inc(ch.h, 1)
        st.close()

    def finish_pna(tag, rows):
        st = Stage(nc, tag, signals)
        at = st.sb("at", [P, 2, NW], I32)
        got = st.sb("got", [P, 2, NW, 4 * D])
        rdeg, ld, fac = (st.sb(n, [P, NC]) for n in ("rdeg", "ld", "fac"))
        mean, msq, t = (st.sb(n, [P, NW, D]) for n in ("mean", "msq", "t"))
        pre = st.chain("pre_steps", "deg1 rdeg ln none none2 inv amp fac1 fac2 fac3")
        names = "mean msq sq var relu root max min h3 std fac h13".split()
        steps = st.sem("node_steps", len(names) * NWBLK)
        at_loaded = st.wide_slots(st.dma, "at_loaded", 16)
        node_got = st.wide_slots(st.dma, "node_got", 16 * NW)
        used = st.wide_slots(st.sem, "node_used", 1)

        def before(g, name):
            return steps(g * len(names) + names.index(name))

        with nc.Block() as block:
            @block.sync
            def _(sp):
                def body(i, b):
                    sp.wait_ge(*used[b](i))
                    sp.dma_start(at[:, b, :], last_d[:, bass.ds((i * 2 + b) * NW, NW)])\
                        .then_inc(at_loaded[b].h, 16)

                over_wide_blocks(sp, body)

            @block.gpsimd
            def _(pool):
                def body(i, b):
                    pool.wait_ge(*at_loaded[b](i * 16 + 16))
                    pool.nop(nofuse=True)
                    pool.wait_ge(*used[b](i))
                    pool.nop(nofuse=True)
                    for k in range(NW):
                        nc.gpsimd.indirect_dma_start(got[:, b, k, :], None, rows, indexed(at[:, b, k:k + 1]))\
                            .then_inc(node_got[b].h, 16)

                over_wide_blocks(pool, body)

            @block.scalar
            def _(act):
                act.wait_ge(*pre.before("ln"))
                act.activation(ld[:], deg[:], ACT.Ln, bias=ones[:, 0:1], scale=1.0).then_inc(pre.h, 1)
                def body(i, b):
                    act.wait_ge(*before(i * 2 + b, "root"))
                    act.activation(t[:], t[:], ACT.Sqrt, bias=eps[:]).then_inc(steps.h, 1)

                over_wide_blocks(act, body)

            @block.vector
            def _(v):

                v.wait_ge(*pre.before("deg1"))
                v.tensor_scalar(rdeg[:], deg[:], 1.0, None, ALU.max).then_inc(pre.h, 1)
                v.wait_ge(*pre.before("rdeg"))
                v.reciprocal(rdeg[:], rdeg[:]).then_inc(pre.h, 1)
                v.wait_ge(*pre.before("none"))
                v.tensor_scalar(fac[:], has[:], -1.0, 1.0, ALU.mult, ALU.add).then_inc(pre.h, 1)
                v.wait_ge(*pre.before("none2"))
                v.tensor_tensor(fac[:], fac[:], ld[:], ALU.add).then_inc(pre.h, 1)
                v.wait_ge(*pre.before("inv"))
                v.reciprocal(fac[:], fac[:]).then_inc(pre.h, 1)
                v.wait_ge(*pre.before("amp"))
                v.tensor_scalar(ld[:], ld[:], 1.0 / AVG_D, 1.0, ALU.mult, ALU.add).then_inc(pre.h, 1)
                v.wait_ge(*pre.before("fac1"))
                v.tensor_scalar(fac[:], fac[:], AVG_D, None, ALU.mult).then_inc(pre.h, 1)
                v.wait_ge(*pre.before("fac2"))
                v.tensor_tensor(fac[:], fac[:], ld[:], ALU.add).then_inc(pre.h, 1)
                v.wait_ge(*pre.before("fac3"))
                v.scalar_tensor_tensor(out=fac[:], in0=fac[:], scalar=1.0 / 13.0, in1=has[:],
                                       op0=ALU.mult, op1=ALU.mult).then_inc(pre.h, 1)
                v.wait_ge(*pre.upto(len(pre)))
                def body(i, b):
                    g = i * 2 + b
                    cols = bass.ds(g * NW, NW)


                    rd = rdeg[:, cols].unsqueeze(2).to_broadcast([P, NW, D])
                    s_, q_, mx, nmn = (got[:, b, :, D * k:D * (k + 1)] for k in range(4))
                    v.wait_ge(*node_got[b](i * (16 * NW) + 16 * NW))
                    v.wait_ge(*before(g, "mean"))
                    v.tensor_tensor(mean[:], s_, rd, ALU.mult).then_inc(steps.h, 1)
                    v.wait_ge(*before(g, "msq"))
                    v.tensor_tensor(msq[:], q_, rd, ALU.mult).then_inc(steps.h, 1)
                    v.wait_ge(*before(g, "sq"))
                    v.tensor_tensor(t[:], mean[:], mean[:], ALU.mult).then_inc(steps.h, 1)
                    v.wait_ge(*before(g, "var"))
                    v.tensor_tensor(t[:], msq[:], t[:], ALU.subtract).then_inc(steps.h, 1)
                    v.wait_ge(*before(g, "relu"))
                    v.tensor_scalar(t[:], t[:], 0.0, None, ALU.max).then_inc(steps.h, 1)
                    v.wait_ge(*before(g, "max"))
                    v.tensor_tensor(msq[:], mean[:], mx, ALU.add).then_inc(steps.h, 1)
                    v.wait_ge(*before(g, "min"))
                    v.tensor_tensor(msq[:], msq[:], nmn, ALU.subtract).then_inc(steps.h, 1)
                    v.wait_ge(*before(g, "h3"))
                    v.scalar_tensor_tensor(out=msq[:], in0=h[:, cols, :], scalar=3.0, in1=msq[:],
                                           op0=ALU.mult, op1=ALU.add).then_inc(steps.h, 1)
                    v.wait_ge(*before(g, "std"))
                    v.tensor_tensor(msq[:], msq[:], t[:], ALU.add).then_inc(steps.h, 1)
                    v.wait_ge(*before(g, "fac"))
                    v.tensor_tensor(msq[:], msq[:],
                                    fac[:, cols].unsqueeze(2).to_broadcast([P, NW, D]), ALU.mult)\
                        .then_inc(steps.h, 1)
                    v.wait_ge(*before(g, "h13"))
                    v.scalar_tensor_tensor(out=h[:, cols, :], in0=h[:, cols, :], scalar=1.0 / 13.0,
                                           in1=msq[:], op0=ALU.mult, op1=ALU.add).then_inc(steps.h, 1)
                    v.wait_ge(*steps(g * len(names) + len(names)))
                    v.sem_inc(used[b].h, 1)

                over_wide_blocks(v, body)
        st.close()

    def batch_norm(tag):
        st = Stage(nc, tag, signals)
        sq = st.sb("sq", [P, NC, D])
        part, mu, sc = (st.sb(n, [P, D]) for n in ("part", "mu", "sc"))
        gb = st.sb("gb", [P, 2, D])
        ps = st.ps("ps", [P, 512])
        loaded = st.dma("w_loaded", 32)
        stored = st.dma("out_stored", 32)
        ch = st.chain("bn_steps", "cut part sum mu centre cut2 square part2 sum2 var root inv scale mul beta add")

        def wide(t):
            return t.unsqueeze(1).to_broadcast([P, NC, D])

        valid_w = valid[:].unsqueeze(2).to_broadcast([P, NC, D])
        full = N_NODES // NC
        rest = N_NODES - full * NC
        with nc.Block() as block:
            @block.sync
            def _(sp):
                sp.dma_start(gb[:, 0, :], row_of(a["L3_gnn_gamma"], D)).then_inc(loaded.h, 16)
                sp.dma_start(gb[:, 1, :], row_of(a["L3_gnn_beta"], D)).then_inc(loaded.h, 16)
                sp.wait_ge(*ch.upto(len(ch)))
                sp.dma_start(out[0:full * NC, :].rearrange("(p c) f -> p c f", p=full), x[0:full])\
                    .then_inc(stored.h, 16)
                sp.dma_start(out[full * NC:N_NODES, :].rearrange("(p c) f -> p c f", p=1),
                             x[full:full + 1, 0:rest, :]).then_inc(stored.h, 16)
                sp.wait_ge(*stored(32))

            @block.tensor
            def _(pe):
                for name in ("sum", "sum2"):
                    pe.wait_ge(*ch.before(name))
                    nc.tensor.matmul(ps[:, 0:D], ones[:], part[:], start=True, stop=True).then_inc(ch.h, 1)

            @block.scalar
            def _(act):
                act.wait_ge(*ch.before("square"))
                act.activation(sq[:], h[:], ACT.Square).then_inc(ch.h, 1)
                act.wait_ge(*ch.before("root"))
                act.activation(sc[:], sc[:], ACT.Sqrt, bias=eps[:]).then_inc(ch.h, 1)

            @block.vector
            def _(v):

                v.wait_ge(*ch.before("cut"))
                v.tensor_tensor(h[:], h[:], valid_w, ALU.mult).then_inc(ch.h, 1)
                v.wait_ge(*ch.before("part"))
                v.reduce_sum(part[:], h[:].rearrange("p c f -> p f c"), axis=AX.X).then_inc(ch.h, 1)
                v.wait_ge(*ch.before("mu"))
                v.tensor_scalar(mu[:], ps[:, 0:D], 1.0 / N_NODES, None, ALU.mult).then_inc(ch.h, 1)
                v.wait_ge(*ch.before("centre"))
                v.tensor_tensor(h[:], h[:], wide(mu[:]), ALU.subtract).then_inc(ch.h, 1)
                v.wait_ge(*ch.before("cut2"))
                v.tensor_tensor(h[:], h[:], valid_w, ALU.mult).then_inc(ch.h, 1)
                v.wait_ge(*ch.before("part2"))
                v.reduce_sum(part[:], sq[:].rearrange("p c f -> p f c"), axis=AX.X).then_inc(ch.h, 1)
                v.wait_ge(*ch.before("var"))
                v.tensor_scalar(sc[:], ps[:, 0:D], 1.0 / N_NODES, None, ALU.mult).then_inc(ch.h, 1)
                v.wait_ge(*ch.before("inv"))
                v.reciprocal(sc[:], sc[:]).then_inc(ch.h, 1)
                v.wait_ge(*loaded(32))
                v.wait_ge(*ch.before("scale"))
                v.tensor_tensor(sc[:], sc[:], gb[:, 0, :], ALU.mult).then_inc(ch.h, 1)
                v.wait_ge(*ch.before("mul"))
                v.tensor_tensor(h[:], h[:], wide(sc[:]), ALU.mult).then_inc(ch.h, 1)
                v.wait_ge(*ch.before("beta"))
                v.tensor_tensor(h[:], h[:], wide(gb[:, 1, :]), ALU.add).then_inc(ch.h, 1)
                v.wait_ge(*ch.before("add"))
                v.tensor_tensor(x[:], x[:], h[:], ALU.add).then_inc(ch.h, 1)
        st.close()

    first_counts()
    setup()
    prepare_conv("p1", a["q1_wt"], a["L0_gnn_q1_b"], a["k1_wt"], a["L0_gnn_k1_b"], a["e1_wt"])
    conv_edges("c1", rows_d[0])
    join_softmax("j1", rows_d[0], 1, YT - 1)
    finish_conv("f1", rows_d[0], a["L0_gnn_v1_w"], a["L0_gnn_v1_b"], a["L0_gnn_e1_w"], a["L0_gnn_s1_w"],
                a["L0_gnn_s1_b"])
    prepare_conv("p2", a["q2_wt"], a["L0_gnn_q2_b"], a["k2_wt"], a["L0_gnn_k2_b"], a["e2_wt"])
    conv_edges("c2", rows_d[1])
    join_softmax("j2", rows_d[1], 1, YT - 1)
    finish_conv("f2", rows_d[1], a["L0_gnn_v2_w"], a["L0_gnn_v2_b"], a["L0_gnn_e2_w"], a["L0_gnn_s2_w"],
                a["L0_gnn_s2_b"], skip=(a["L0_gnn_skip_w"], a["L0_gnn_skip_b"]))

    with ExitStack() as gat:
        gt = gat.enter_context(nc.sbuf_tensor("gt", [P, NC, TG], F32))
        bd = gat.enter_context(nc.sbuf_tensor("bd", [P, HG * G], F32))
        layer_norm("ln1")
        prepare_gat("p3", gt, a["gat_w"], a["L1_gnn_a_s"].rearrange("h o -> (h o)"),
                    a["L1_gnn_a_t"].rearrange("h o -> (h o)"), HG,
                    (bd, a["gat_we"], a["L1_gnn_a_e"].rearrange("h o -> (h o)")))
        block_diagonal("bd", bd)
        gat_edges("c3", rows_d[2], bd)
        join_softmax("j3", rows_d[2], HG, JG)
        finish_gat("f3", rows_d[2], a["L1_gnn_b_GAT"].rearrange("h o -> (h o)"), norm=True)
        prepare_gat("p4", gt, a["L2_gnn_W1"], a["L2_gnn_a_src1"].rearrange("h o -> (h o)"),
                    a["L2_gnn_a_dst1"].rearrange("h o -> (h o)"), HG)
        gat_edges("c4", rows_d[3])
        join_softmax("j4", rows_d[3], HG, JG)
        finish_gat("f4", rows_d[3], a["L2_gnn_b1"], gt)
        prepare_gat("p5", gt, a["L2_gnn_W2"], a["L2_gnn_a_src2"].rearrange("h o -> (h o)"),
                    a["L2_gnn_a_dst2"].rearrange("h o -> (h o)"), 1)
        gat_edges("c5", rows_d[4])
        join_softmax("j5", rows_d[4], HG, JG)
        finish_gat("f5", rows_d[4], a["L2_gnn_b2"], gt, last=True, norm=True)

    store_table("t6")
    pna_edges("c6", rows_d[5])
    join_pna("j6", rows_d[5])
    finish_pna("f6", rows_d[5])
    batch_norm("bn")
    root.close()


def kernel(**inputs):
    import concourse.bacc as bacc
    from concourse.bass_utils import run_bass_kernel_spmd

    def pad(v, n, fill=0):
        v = np.asarray(v)
        return np.concatenate([v, np.full((n - v.shape[0],) + v.shape[1:], fill, v.dtype)])

    arrays = {k: np.ascontiguousarray(v) for k, v in inputs.items()}
    arrays["x"] = pad(arrays["x"], NP_)
    arrays["src"] = pad(arrays["src"], EP)
    dst = pad(arrays["dst"], EP, N_NODES)
    arrays["dst"] = np.concatenate([np.full(1, -1, dst.dtype), dst])
    arrays["dst_chunks"] = dst.reshape(NCH, CH)
    arrays["chunk_firsts"] = np.ascontiguousarray(dst[::CH])
    arrays["edge_attr_32"] = pad(arrays["edge_attr_32"], EP)
    arrays["edge_attr_64"] = pad(arrays["edge_attr_64"], EP)
    e8 = pad(arrays["edge_attr_8"], EP).reshape(P, NG, G, 8)
    arrays["edge_attr_8"] = np.ascontiguousarray(e8.transpose(1, 2, 3, 0)).reshape(NG * G * 8, P)
    for n in ("1", "2"):
        for w in ("q", "k", "e"):
            full = arrays[f"L0_gnn_{w}{n}_w"]
            arrays[f"{w}{n}_wt"] = np.ascontiguousarray(full.T)
    arrays["gat_w"] = np.ascontiguousarray(arrays.pop("L1_gnn_W").transpose(1, 0, 2)).reshape(D, D)
    arrays["gat_we"] = np.ascontiguousarray(arrays.pop("L1_gnn_W_e").transpose(1, 0, 2)).reshape(8, D)
    for name in ("L0_gnn_q1_w", "L0_gnn_k1_w", "L0_gnn_q2_w", "L0_gnn_k2_w"):
        arrays.pop(name)

    nc = bacc.Bacc("TRN2", target_bir_lowering=False, num_devices=1)
    aps = {k: nc.dram_tensor(f"in_{k}", v.shape, mybir.dt.from_np(v.dtype), kind="ExternalInput").ap()
           for k, v in arrays.items()}
    out = nc.dram_tensor("out_0", (N_NODES, D), F32, kind="ExternalOutput").ap()
    build(nc, aps, out)
    result = run_bass_kernel_spmd(nc, [{f"in_{k}": v for k, v in arrays.items()}], core_ids=[0])
    return result.results[0]["out_0"]
```
